# Optimizing a Trainium2 kernel written in Bass

```python
import numpy as np
import jax
import jax.numpy as jnp

def _softmax(x, axis=-1):
    return jax.nn.softmax(x, axis=axis)

def _gelu(x):
    return jax.nn.gelu(x, approximate=True)

def _silu(x):
    return jax.nn.silu(x)

def _sigmoid(x):
    return jax.nn.sigmoid(x)

def _layernorm(x, axis=-1, eps=1e-05):
    m = jnp.mean(x, axis=axis, keepdims=True)
    v = jnp.var(x, axis=axis, keepdims=True)
    return (x - m) / jnp.sqrt(v + eps)

def _scatter_add(tgt, idx, src, axis=0):
    return tgt.at[idx].add(src)

def _segment_sum(src, seg, n):
    return jax.ops.segment_sum(src, seg, n)
kernel_name = 'mk_vit_tower_d2_tok_img768_r4_bea04e'

def setup_inputs(seed: int=0):
    np.random.seed(seed)
    _w = jnp.asarray

    def _rec_inputs():
        import jax
        import jax.numpy as jnp
        _rk = jax.random.key(seed)
        x = 7.57192e-06 + 1.00007 * jax.random.normal(jax.random.fold_in(_rk, 1), (32, 96, 96, 3), jnp.float32)
        return x
    x = _rec_inputs()

    def _L0_tok_setup():
        import jax, jax.numpy as jnp
        import numpy as np
        PATCH = 16
        DIM = 192
        EPS = 0.001

        def _shifts(x):
            zw = jnp.zeros_like(x[:, :, :1, :])
            right = jnp.concatenate([zw, x[:, :, :-1, :]], axis=2)
            left = jnp.concatenate([x[:, :, 1:, :], zw], axis=2)
            zh = jnp.zeros_like(x[:, :1, :, :])
            down = jnp.concatenate([zh, x[:, :-1, :, :]], axis=1)
            up = jnp.concatenate([x[:, 1:, :, :], zh], axis=1)
            return [right, left, down, up]

        def _patchify(x, p):
            b, H, W, C = x.shape
            hh, ww = (H // p, W // p)
            x = x.reshape(b, hh, p, ww, p, C)
            x = x.transpose(0, 1, 3, 2, 4, 5)
            return x.reshape(b, hh * ww, p * p * C)
        key = jax.random.key(seed)
        k1, k2 = jax.random.split(key)
        b, H, Wd, C = (64, 224, 224, 3)
        F = PATCH * PATCH * 5 * C
        x = jax.random.normal(k1, (b, H, Wd, C), dtype=jnp.float32)
        gamma = jnp.ones((F,), dtype=jnp.float32)
        beta = jnp.zeros((F,), dtype=jnp.float32)
        W = jax.random.normal(k2, (F, DIM), dtype=jnp.float32)
        bb = jnp.zeros((DIM,), dtype=jnp.float32)
        return {'x': x, 'gamma': gamma, 'beta': beta, 'W': W, 'b': bb}
    _L0_tok_all = _L0_tok_setup()
    _L0_tok_in = {k: v for k, v in _L0_tok_all.items() if k in ('gamma', 'beta', 'W', 'b')}
    del _L0_tok_all

    def _L0_attn_setup():
        import math
        import jax, jax.numpy as jnp
        import numpy as np
        HIDDEN = 192
        NUM_HEADS = 12
        HEAD_DIM = HIDDEN // NUM_HEADS
        WINDOW = 64
        DILATION = 1
        BATCH = 2
        SEQ = 512

        def _band_mask(seq_len, dtype):
            idx = jnp.arange(seq_len)
            rel = idx[None, :] - idx[:, None]
            m = (jnp.abs(rel) <= WINDOW * DILATION) & (jnp.mod(rel, DILATION) == 0)
            return m.astype(dtype)
        key = jax.random.key(seed)
        ks = jax.random.split(key, 7)
        s = 1.0 / math.sqrt(HIDDEN)
        return {'hidden_states': jax.random.normal(ks[0], (BATCH, SEQ, HIDDEN), jnp.float32), 'Wq': jax.random.normal(ks[1], (HIDDEN, HIDDEN), jnp.float32) * s, 'bq': jnp.zeros((HIDDEN,), jnp.float32), 'Wk': jax.random.normal(ks[2], (HIDDEN, HIDDEN), jnp.float32) * s, 'bk': jnp.zeros((HIDDEN,), jnp.float32), 'Wv': jax.random.normal(ks[3], (HIDDEN, HIDDEN), jnp.float32) * s, 'bv': jnp.zeros((HIDDEN,), jnp.float32)}
    _L0_attn_all = _L0_attn_setup()
    _L0_attn_in = {k: v for k, v in _L0_attn_all.items() if k in ('Wq', 'bq', 'Wk', 'bk', 'Wv', 'bv')}
    del _L0_attn_all

    def _L0_ffn_setup():
        import jax, jax.numpy as jnp
        import numpy as np
        H, I, E, S, K = (192, 768, 16, 2, 2)
        SCALE = 1.0
        key = jax.random.key(seed)
        ks = jax.random.split(key, 8)
        sd = 0.02
        return {'hidden_states': jax.random.normal(ks[0], (2, 256, H), jnp.float32), 'gate_w': jax.random.normal(ks[1], (E, H), jnp.float32) * sd, 'shared_wg': jax.random.normal(ks[2], (S, H, I), jnp.float32) * sd, 'shared_wu': jax.random.normal(ks[3], (S, H, I), jnp.float32) * sd, 'shared_wd': jax.random.normal(ks[4], (S, I, H), jnp.float32) * sd, 'wg': jax.random.normal(ks[5], (E, H, I), jnp.float32) * sd, 'wu': jax.random.normal(ks[6], (E, H, I), jnp.float32) * sd, 'wd': jax.random.normal(ks[7], (E, I, H), jnp.float32) * sd}
    _L0_ffn_all = _L0_ffn_setup()
    _L0_ffn_in = {k: v for k, v in _L0_ffn_all.items() if k in ('gate_w', 'shared_wg', 'shared_wu', 'shared_wd', 'wg', 'wu', 'wd')}
    del _L0_ffn_all

    def _L1_attn_setup():
        import jax, jax.numpy as jnp
        import numpy as np
        import math
        B, N, DIM = (4, 512, 192)
        HEADS, DIM_HEAD = (12, 64)
        SCALE = math.sqrt(DIM_HEAD)

        def _split_heads(t):
            b, n, _ = t.shape
            return t.reshape(b, n, HEADS, DIM_HEAD).transpose(0, 2, 1, 3)
        key = jax.random.key(seed)
        ks = jax.random.split(key, 5)
        inner = HEADS * DIM_HEAD
        x = jax.random.normal(ks[0], (B, N, DIM), dtype=jnp.float32)
        w_q = jax.random.normal(ks[1], (DIM, inner), dtype=jnp.float32) * 0.02
        w_k = jax.random.normal(ks[2], (DIM, inner), dtype=jnp.float32) * 0.02
        w_v = jax.random.normal(ks[3], (DIM, inner), dtype=jnp.float32) * 0.02
        w_o = jax.random.normal(ks[4], (inner, DIM), dtype=jnp.float32) * 0.02
        b_o = jnp.zeros((DIM,), dtype=jnp.float32)
        return {'x': x, 'w_q': w_q, 'w_k': w_k, 'w_v': w_v, 'w_o': w_o, 'b_o': b_o}
    _L1_attn_all = _L1_attn_setup()
    _L1_attn_in = {k: v for k, v in _L1_attn_all.items() if k in ('w_q', 'w_k', 'w_v', 'w_o', 'b_o')}
    del _L1_attn_all

    def _L1_ffn_setup():
        import jax, jax.numpy as jnp
        import numpy as np
        B, T, D, E, K = (4, 512, 192, 8, 2)
        H = 4 * D
        key = jax.random.key(seed)
        k0, k1, k2, k3, k4 = jax.random.split(key, 5)
        s = 0.02
        return {'x': jax.random.normal(k0, (B, T, D), jnp.float32), 'router_w': jax.random.uniform(k1, (E, D), jnp.float32, -s * 0.1, s * 0.1), 'Wg': jax.random.uniform(k2, (E, H, D), jnp.float32, -s * 0.4, s * 0.4), 'Wu': jax.random.uniform(k3, (E, H, D), jnp.float32, -s * 0.4, s * 0.4), 'Wd': jax.random.normal(k4, (E, D, H), jnp.float32) * 0.01}
    _L1_ffn_all = _L1_ffn_setup()
    _L1_ffn_in = {k: v for k, v in _L1_ffn_all.items() if k in ('router_w', 'Wg', 'Wu', 'Wd')}
    del _L1_ffn_all
    return {'x': x, 'L0_tok_gamma': _L0_tok_in['gamma'], 'L0_tok_beta': _L0_tok_in['beta'], 'L0_tok_W': _L0_tok_in['W'], 'L0_tok_b': _L0_tok_in['b'], 'L0_attn_Wq': _L0_attn_in['Wq'], 'L0_attn_bq': _L0_attn_in['bq'], 'L0_attn_Wk': _L0_attn_in['Wk'], 'L0_attn_bk': _L0_attn_in['bk'], 'L0_attn_Wv': _L0_attn_in['Wv'], 'L0_attn_bv': _L0_attn_in['bv'], 'L0_ffn_gate_w': _L0_ffn_in['gate_w'], 'L0_ffn_shared_wg': _L0_ffn_in['shared_wg'], 'L0_ffn_shared_wu': _L0_ffn_in['shared_wu'], 'L0_ffn_shared_wd': _L0_ffn_in['shared_wd'], 'L0_ffn_wg': _L0_ffn_in['wg'], 'L0_ffn_wu': _L0_ffn_in['wu'], 'L0_ffn_wd': _L0_ffn_in['wd'], 'L1_attn_w_q': _L1_attn_in['w_q'], 'L1_attn_w_k': _L1_attn_in['w_k'], 'L1_attn_w_v': _L1_attn_in['w_v'], 'L1_attn_w_o': _L1_attn_in['w_o'], 'L1_attn_b_o': _L1_attn_in['b_o'], 'L1_ffn_router_w': _L1_ffn_in['router_w'], 'L1_ffn_Wg': _L1_ffn_in['Wg'], 'L1_ffn_Wu': _L1_ffn_in['Wu'], 'L1_ffn_Wd': _L1_ffn_in['Wd']}

def reference(x, L0_tok_gamma, L0_tok_beta, L0_tok_W, L0_tok_b, L0_attn_Wq, L0_attn_bq, L0_attn_Wk, L0_attn_bk, L0_attn_Wv, L0_attn_bv, L0_ffn_gate_w, L0_ffn_shared_wg, L0_ffn_shared_wu, L0_ffn_shared_wd, L0_ffn_wg, L0_ffn_wu, L0_ffn_wd, L1_attn_w_q, L1_attn_w_k, L1_attn_w_v, L1_attn_w_o, L1_attn_b_o, L1_ffn_router_w, L1_ffn_Wg, L1_ffn_Wu, L1_ffn_Wd):
    import jax
    import jax.numpy as jnp

    def _L0_tok_ref(x, gamma, beta, W, b):
        import jax, jax.numpy as jnp
        import numpy as np
        PATCH = 16
        DIM = 192
        EPS = 0.001

        def _shifts(x):
            zw = jnp.zeros_like(x[:, :, :1, :])
            right = jnp.concatenate([zw, x[:, :, :-1, :]], axis=2)
            left = jnp.concatenate([x[:, :, 1:, :], zw], axis=2)
            zh = jnp.zeros_like(x[:, :1, :, :])
            down = jnp.concatenate([zh, x[:, :-1, :, :]], axis=1)
            up = jnp.concatenate([x[:, 1:, :, :], zh], axis=1)
            return [right, left, down, up]

        def _patchify(x, p):
            b, H, W, C = x.shape
            hh, ww = (H // p, W // p)
            x = x.reshape(b, hh, p, ww, p, C)
            x = x.transpose(0, 1, 3, 2, 4, 5)
            return x.reshape(b, hh * ww, p * p * C)
        x5 = jnp.concatenate([x] + _shifts(x), axis=-1)
        tokens = _patchify(x5, PATCH)
        mu = jnp.mean(tokens, axis=-1, keepdims=True)
        var = jnp.mean(jnp.square(tokens - mu), axis=-1, keepdims=True)
        ln = (tokens - mu) * jax.lax.rsqrt(var + EPS) * gamma + beta
        return jnp.einsum('bnf,fd->bnd', ln, W) + b

    def _L0_attn_ref(hidden_states, Wq, bq, Wk, bk, Wv, bv):
        import math
        import jax, jax.numpy as jnp
        import numpy as np
        HIDDEN = 192
        NUM_HEADS = 12
        HEAD_DIM = HIDDEN // NUM_HEADS
        WINDOW = 64
        DILATION = 1
        BATCH = 2
        SEQ = 512

        def _band_mask(seq_len, dtype):
            idx = jnp.arange(seq_len)
            rel = idx[None, :] - idx[:, None]
            m = (jnp.abs(rel) <= WINDOW * DILATION) & (jnp.mod(rel, DILATION) == 0)
            return m.astype(dtype)
        B, S, M = hidden_states.shape
        H, D = (NUM_HEADS, HEAD_DIM)
        q = (hidden_states @ Wq.T + bq) / math.sqrt(D)
        k = hidden_states @ Wk.T + bk
        v = hidden_states @ Wv.T + bv
        q = q.reshape(B, S, H, D).transpose(0, 2, 1, 3)
        k = k.reshape(B, S, H, D).transpose(0, 2, 1, 3)
        v = v.reshape(B, S, H, D).transpose(0, 2, 1, 3)
        scores = jnp.einsum('bhqd,bhkd->bhqk', q, k)
        mask = _band_mask(S, scores.dtype)
        scores = scores * mask
        probs = jax.nn.softmax(scores, axis=-1)
        ctx = jnp.einsum('bhqk,bhkd->bhqd', probs, v)
        return ctx.transpose(0, 2, 1, 3).reshape(B, S, M)

    def _L0_ffn_ref(hidden_states, gate_w, shared_wg, shared_wu, shared_wd, wg, wu, wd):
        import jax, jax.numpy as jnp
        import numpy as np
        H, I, E, S, K = (192, 768, 16, 2, 2)
        SCALE = 1.0
        B, T, _ = hidden_states.shape
        x = hidden_states.reshape(-1, H)
        N = x.shape[0]
        g = jnp.einsum('nh,shi->sni', x, shared_wg)
        u = jnp.einsum('nh,shi->sni', x, shared_wu)
        shared_out = jnp.einsum('sni,sih->snh', jax.nn.silu(g) * u, shared_wd).mean(axis=0)
        router_logits = x @ gate_w.T
        routing_weights = jax.nn.softmax(router_logits, axis=-1)
        topk_w, topk_idx = jax.lax.top_k(routing_weights, K)
        topk_w = topk_w / (topk_w.sum(axis=-1, keepdims=True) + 1e-08)
        topk_w = topk_w * SCALE
        combine = jnp.zeros((N, E), x.dtype).at[jnp.arange(N)[:, None], topk_idx].add(topk_w)
        ge = jnp.einsum('nh,ehi->eni', x, wg)
        ue = jnp.einsum('nh,ehi->eni', x, wu)
        ye = jnp.einsum('eni,eih->enh', jax.nn.silu(ge) * ue, wd)
        routed_out = jnp.einsum('ne,enh->nh', combine, ye)
        return (shared_out + routed_out).reshape(B, T, H)

    def _L1_attn_ref(x, w_q, w_k, w_v, w_o, b_o):
        import jax, jax.numpy as jnp
        import numpy as np
        import math
        B, N, DIM = (4, 512, 192)
        HEADS, DIM_HEAD = (12, 64)
        SCALE = math.sqrt(DIM_HEAD)

        def _split_heads(t):
            b, n, _ = t.shape
            return t.reshape(b, n, HEADS, DIM_HEAD).transpose(0, 2, 1, 3)
        q = _split_heads(x @ w_q)
        k = _split_heads(x @ w_k)
        v = _split_heads(x @ w_v)
        scores = jnp.einsum('bhnd,bhmd->bhnm', q, k) / SCALE
        attn = jax.nn.softmax(scores, axis=-1)
        h = jnp.einsum('bhnm,bhmd->bhnd', attn, v)
        H = h.transpose(0, 2, 1, 3).reshape(x.shape[0], x.shape[1], HEADS * DIM_HEAD)
        out = H @ w_o + b_o
        return out

    def _L1_ffn_ref(x, router_w, Wg, Wu, Wd):
        import jax, jax.numpy as jnp
        import numpy as np
        B, T, D, E, K = (4, 512, 192, 8, 2)
        H = 4 * D
        Bv, Tv, Dv = x.shape
        N = Bv * Tv
        xf = x.reshape(N, Dv)
        logits = (xf @ router_w.T).astype(jnp.float32)
        top_logits, top_idx = jax.lax.top_k(logits, K)
        top_w = jax.nn.softmax(top_logits, axis=-1).astype(x.dtype)
        out = jnp.zeros_like(xf)
        for e in range(E):
            w_e = jnp.sum(top_w * (top_idx == e), axis=-1)
            h = jax.nn.silu(xf @ Wg[e].T) * (xf @ Wu[e].T)
            out = out + h @ Wd[e].T * w_e[:, None]
        return out.reshape(Bv, Tv, Dv)
    h = _L0_tok_ref(x, L0_tok_gamma, L0_tok_beta, L0_tok_W, L0_tok_b)
    h = h + _L0_attn_ref(_layernorm(h, axis=-1), L0_attn_Wq, L0_attn_bq, L0_attn_Wk, L0_attn_bk, L0_attn_Wv, L0_attn_bv)
    h = h + _L0_ffn_ref(_layernorm(h, axis=-1), L0_ffn_gate_w, L0_ffn_shared_wg, L0_ffn_shared_wu, L0_ffn_shared_wd, L0_ffn_wg, L0_ffn_wu, L0_ffn_wd)
    h = h + _L1_attn_ref(_layernorm(h, axis=-1), L1_attn_w_q, L1_attn_w_k, L1_attn_w_v, L1_attn_w_o, L1_attn_b_o)
    h = h + _L1_ffn_ref(_layernorm(h, axis=-1), L1_ffn_router_w, L1_ffn_Wg, L1_ffn_Wu, L1_ffn_Wd)
    return h

_drawn_inputs = setup_inputs


def setup_inputs(seed=0):
    import zlib

    import numpy as np

    out = dict(_drawn_inputs(seed))
    spreads = {'L0_tok_gamma': (1.0, 0.2),
     'L0_tok_beta': (0.0, 0.1),
     'L0_tok_b': (0.0, 2.0),
     'L0_attn_bq': (0.0, 0.8),
     'L0_attn_bk': (0.0, 2.0),
     'L0_attn_bv': (0.0, 2.0),
     'L1_attn_b_o': (0.0, 2.0)}
    factors = {'L0_attn_Wq': 8.0,
     'L0_attn_Wk': 8.0,
     'L0_attn_Wv': 8.0,
     'L0_ffn_gate_w': 8.0,
     'L0_ffn_shared_wg': 8.0,
     'L0_ffn_shared_wu': 8.0,
     'L0_ffn_shared_wd': 8.0,
     'L0_ffn_wg': 8.0,
     'L0_ffn_wu': 8.0,
     'L0_ffn_wd': 8.0,
     'L1_attn_w_q': 8.0,
     'L1_attn_w_k': 8.0,
     'L1_attn_w_v': 8.0,
     'L1_attn_w_o': 8.0,
     'L1_ffn_router_w': 64.0,
     'L1_ffn_Wg': 64.0,
     'L1_ffn_Wu': 64.0,
     'L1_ffn_Wd': 64.0}
    for name, (base, spread) in spreads.items():
        noise = np.random.default_rng([zlib.crc32(name.encode()), seed]).standard_normal(out[name].shape)
        drawn = base * np.exp(spread * noise) if base else spread * noise
        out[name] = jnp.asarray(drawn.astype(out[name].dtype))
    for name, factor in factors.items():
        out[name] = (out[name] * factor).astype(out[name].dtype)
    return out
```

```python
import numpy as np

import concourse.bass as bass
from concourse import mybir
from concourse.alu_op_type import AluOpType as ALU

ACT = mybir.ActivationFunctionType
AX = mybir.AxisListType
F32 = mybir.dt.float32
BF16 = mybir.dt.bfloat16
U32 = mybir.dt.uint32

BATCH, IMG, CH, PATCH, D = 32, 96, 3, 16, 192
SIDE = IMG // PATCH
SEQ = SIDE * SIDE
TOKENS = BATCH * SEQ
FEATURES = PATCH * PATCH * 5 * CH
PER = 3
G = PER * SEQ
NT = -(-BATCH // PER)
PAD_TOKENS = NT * G
LAST = TOKENS - (NT - 1) * G
KD = 96
TAP_CHUNKS = 8
HEADS = 12
HD = (16, 64)
INNER = (HEADS * HD[0], HEADS * HD[1])
HIDDEN = 768
HC = HIDDEN // 128
EXPERTS = (16, 8)
BLOCK = 128
BLOCKS = tuple((2 * TOKENS + e * (BLOCK - 1)) // BLOCK for e in EXPERTS)
SLOTS = max(BLOCKS) * BLOCK
LN_EPS, TOK_EPS = 1e-5, 1e-3
MASKED = -(2.0 ** 100)


def tap_table():
    classes = {}
    for y in range(-1, PATCH + 1):
        for x in range(-1, PATCH + 1):
            n = sum(0 <= y + a < PATCH and 0 <= x + b < PATCH
                    for a, b in ((0, 0), (0, 1), (0, -1), (1, 0), (-1, 0)))
            if n:
                classes.setdefault(n, []).extend((y, x, c) for c in range(CH))
    rows, counts = [], []
    for n, taps in sorted(classes.items()):
        taps = taps + [None] * (-len(taps) % TAP_CHUNKS)
        for i in range(0, len(taps), TAP_CHUNKS):
            rows.append(taps[i:i + TAP_CHUNKS])
            counts.append(n)
    return rows, counts


TAPS, TAP_COUNTS = tap_table()
TP = len(TAPS)

C_IDENT = 0
C_UPPER = C_IDENT + 128
C_ONES = C_UPPER + G
C_IOTA_E = C_ONES + 128
C_IOTA_B = C_IOTA_E + max(EXPERTS)
C_THRESH = C_IOTA_B + max(BLOCKS)
N_THRESH = -(-TOKENS // BLOCK)
C_PIDX = C_THRESH + N_THRESH
C_INVALID = C_PIDX + 1
C_COUNT = C_INVALID + NT
C_MASK = C_COUNT + 1
C_ALL = C_MASK + 3 * G


def shape_constants():
    c = np.zeros((128, C_ALL), np.float32)
    p = np.arange(128)
    c[:, C_IDENT:C_IDENT + 128] = np.eye(128)
    c[:, C_UPPER:C_UPPER + G] = p[:, None] < np.arange(G)[None, :]
    c[:, C_ONES:C_ONES + 128] = 1
    c[:, C_IOTA_E:C_IOTA_E + max(EXPERTS)] = np.arange(max(EXPERTS))
    c[:, C_IOTA_B:C_IOTA_B + max(BLOCKS)] = np.arange(max(BLOCKS))
    c[:, C_THRESH:C_THRESH + N_THRESH] = BLOCK * np.arange(N_THRESH)
    c[:, C_PIDX] = p
    c[LAST:, C_INVALID + NT - 1] = 100
    c[:TP, C_COUNT] = TAP_COUNTS
    image = np.arange(G) // SEQ
    other = image[:, None] != image[None, :]
    c[:G, C_MASK:] = np.tile(np.where(other, MASKED, 0.0), (1, 3))
    return c


def program(nc, const, xcol, w5, gamma5, beta5, tok_b, a0_wqk, a0_bqk, a0_wv, a0_bv,
            a1_wqk, a1_wv, a1_wo, a1_bo, gate0, gate1, sh_wa, sh_wd, e0_wa, e0_wd, e1_wa, e1_wd,
            xs_dram, y_dram, out):
    def sb(name, shape, dt=F32):
        return nc.alloc_sbuf_tensor(name, shape, dt)

    def sem(name):
        return nc.alloc_semaphore(name)

    def sems(name, n):
        return [sem(f"{name}{i}") for i in range(n)]

    ps = nc.alloc_psum_tensor("ps", [128, 8, 512], F32)

    cst = sb("cst", [128, C_ALL])
    h = sb("h", [G, NT, D])
    xn = sb("xn", [G, NT, D])
    xnT = sb("xnT", [KD, 2, PAD_TOKENS])
    identb = sb("identb", [G, G], BF16)
    maskb = sb("maskb", [G, 3 * G], BF16)
    zero = sb("zero", [128, 3 * D])
    st6 = sb("st6", [G, NT, 6])
    mv = sb("mv", [G, NT, 2])
    rstd = sb("rstd", [G, NT])
    var = sb("var", [G, NT])
    rinv = sb("rinv", [G, NT])
    ident = cst[:, C_IDENT:C_IDENT + 128]
    ones = cst[:, C_ONES:C_ONES + 128]

    big = sb("big", [128, TAP_CHUNKS * 5 * D])
    w5_sb = big[:TP, :].rearrange("p (c g n) -> p c g n", c=TAP_CHUNKS, g=5)
    g5_sb = sb("g5_sb", [TP, TAP_CHUNKS, 5])
    b5_sb = sb("b5_sb", [TP, TAP_CHUNKS, 5])
    tokb_sb = sb("tokb_sb", [1, D])
    weff = sb("weff", [TP, TAP_CHUNKS, D + 1])
    crow = sb("crow", [1, D])
    cs_sb = sb("cs_sb", [G, 2, D])
    xc = sb("xc", [TP, 2, TAP_CHUNKS, G])
    xsq = sb("xsq", [TP, 2, TAP_CHUNKS, G])
    xss = sb("xss", [TP, 2, G])
    tst = sb("tst", [G, NT, 2])
    shift = sb("shift", [G, NT])

    wqk = [sb("wqk0", [KD, 2, 768]), sb("wqk1", [KD, 2, 1536])]
    wv = [sb("wv0", [KD, 2, 192]), sb("wv1", [KD, 2, 768])]
    wo = sb("wo", [128, 6, D])
    bqk = sb("bqk", [128, 2, 3])
    bv = sb("bv", [G, D])
    bo = sb("bo", [G, D])
    work = sb("work", [128, max(BLOCKS) * D])
    o_qk, o_prob, o_probT, o_ctx, o_ctxT = 0, 12 * G, 24 * G, 36 * G, 36 * G + INNER[1]
    qk = work[:, o_qk:o_prob].rearrange("p (q j t) -> p q j t", q=4, j=3)
    v = sb("v", [G, HEADS, HD[1] + 1])
    v0 = sb("v0", [G, HEADS, HD[0] + 1])
    vh = [v0, v]
    xt_s = sb("xt_s", [KD, 2, G])
    prob = work[:G, o_prob:o_probT].rearrange("p (n t) -> p n t", n=HEADS)
    probT = work[:G, o_probT:o_ctx].rearrange("p (n t) -> p n t", n=HEADS)
    mx = sb("mx", [G, HEADS])
    rs = sb("rs", [G, HEADS])
    ctx = work[:G, o_ctx:o_ctxT]
    ctxT = work[:, o_ctxT:o_ctxT + 6 * G].rearrange("p (j t) -> p j t", j=6)

    gate = [sb("gate0s", [KD, 2, EXPERTS[0]]), sb("gate1s", [KD, 2, EXPERTS[1]])]
    wa = sb("wa", [KD, 2, 2, 2, HIDDEN])
    wd = sb("wd", [128, 2, HC, D])
    lg = sb("lg", [G, NT, 16])
    m8 = sb("m8", [G, NT, 8])
    i8 = sb("i8", [G, NT, 8], U32)
    idxf = sb("idxf", [G, 2, NT])
    oh = sb("oh", [G, 3, NT, 16])
    base = sb("base", [G, NT, 16])
    tmp = sb("tmp", [G, 2, NT, 16])
    tot = sb("tot", [128, NT, 16])
    cum = sb("cum", [128, NT + 1, 16])
    cmp9 = sb("cmp9", [128, 16, N_THRESH])
    nblk = sb("nblk", [128, 16])
    oend = sb("oend", [128, 16])
    obeg = sb("obeg", [128, 16])
    cmpb = sb("cmpb", [128, max(BLOCKS), 16])
    eb = sb("eb", [128, max(BLOCKS)])
    widx = sb("widx", [128, 2, max(BLOCKS)], U32)
    slotf = sb("slotf", [G, 2, NT])
    slot_i = sb("slot_i", [G, 2, NT], U32)
    cw = sb("cw", [G, 2, NT])
    zsum = sb("zsum", [G, NT])
    pw = sb("pw", [G, 2, NT])
    xall = work[:, :].rearrange("p (b n) -> p b n", b=max(BLOCKS))
    xg = sb("xg", [BLOCK, 2, D])
    xgT = sb("xgT", [KD, 2, 2, BLOCK])
    silu = sb("silu", [128, 2, 4 * G])
    hb = sb("hb", [128, 2, HC, BLOCK])
    ysb = sb("ysb", [BLOCK, 2, D])
    hsh = big[:, 0:HC * 4 * G].rearrange("p (m t) -> p m t", m=HC)
    yg = big[:G, 0:2 * NT * D].rearrange("p (k t n) -> p k t n", k=2, t=NT)

    s_const, s_tokw, s_beta = sem("s_const"), sem("s_tokw"), sem("s_beta")
    s_attw, s_gatew, s_shw1 = sems("s_attw", 2), sem("s_gatew"), sems("s_shw", 2)
    s_zero, s_zfill, s_setup, s_weff = sem("s_zero"), sem("s_zfill"), sem("s_setup"), sem("s_weff")
    s_const_ps, s_crow, s_crep, s_cs = sem("s_const_ps"), sem("s_crow"), sem("s_crep"), sem("s_cs")
    t_in, t_sq, t_red, t_mm, t_h = sems("t_in", 2), sems("t_sq", 2), sems("t_red", 2), sems("t_mm", 2), sems("t_h", 2)
    dve_own = sem("dve_own")
    n_xn, n_tp, n_xt = sems("n_xn", 4), sems("n_tp", 4), sems("n_xt", 4)
    s_var, s_root = sem("s_var"), sem("s_root")
    a_names = ("stage", "qkp", "qke_a", "qke_d", "vp", "ve", "score", "sub", "exp", "ptp", "pta", "ptd", "pv",
               "ctx", "out")
    A = [{n: sem(f"a{l}_{n}") for n in a_names + (("ctp", "cte", "op") if l else ())} for l in range(2)]
    m_names = ("lgp", "oh", "cnt", "ex", "exr", "idx", "scat", "comb")
    M = [{n: sem(f"m{l}_{n}") for n in m_names + (() if l else ("gup", "silu", "mul", "dnp", "dne"))}
         for l in range(2)]
    b_names = ("wa", "wd", "xg", "tp", "te", "gu", "sl", "hm", "dn", "ye", "yo")
    B = [{n: sems(f"b{l}_{n}", 2) for n in b_names} for l in range(2)]
    m_xall = [sems(f"m{l}_xall", 3) for l in range(2)]
    g_y = [sems(f"g{l}_y", 2) for l in range(2)]
    s_out = sem("s_out")

    e_wa, e_wd = [e0_wa, e1_wa], [e0_wd, e1_wd]
    GROUPS = [range(0, 4), range(4, 8), range(8, NT)]

    def alternating(eng, first, count, step):
        while first < 3:
            step(first, first % 2, first // 2)
            first, count = first + 1, count - 1
        if count // 2:
            with eng.Fori(0, count // 2) as i:
                for j in (first, first + 1):
                    step(2 * i + j, j % 2, i + j // 2)
        if count % 2:
            last = first + count - 1
            step(last, last % 2, last // 2)

    block = nc.Block()
    with block:
        @block.sync
        def _(sp):
            sp.dma_start(cst[:, :], const).then_inc(s_const, 16)
            sp.dma_start(g5_sb[:, :, :], gamma5).then_inc(s_tokw, 16)
            sp.dma_start(w5_sb, w5).then_inc(s_tokw, 16)
            sp.dma_start(b5_sb[:, :, :], beta5).then_inc(s_beta, 16)
            sp.dma_start(tokb_sb[:, :], tok_b).then_inc(s_beta, 16)

            def load_tile(t, s, k):
                sp.wait_ge(t_mm[s], k)
                sp.dma_start(xc[:, s, :, :], xcol[bass.ds(t, 1)].rearrange("a p c t -> (a p) c t")
                             ).then_inc(t_in[s], 16)
            alternating(sp, 0, NT, load_tile)

            for l in range(2):
                b = B[l]
                sp.wait_ge(M[l]["scat"], 16 * 2 * NT)

                for i in range(3):
                    lo, hi = BLOCKS[l] * i // 3, BLOCKS[l] * (i + 1) // 3
                    sp.dma_start(xall[:, lo:hi, :], xs_dram[lo * BLOCK:hi * BLOCK, :].rearrange(
                        "(b p) n -> p b n", p=BLOCK)).then_inc(m_xall[l][i], 16)

                def store_y(n, s, k):
                    sp.wait_ge(b["ye"][s], k + 1)
                    sp.dma_start(y_dram[bass.ds(n * BLOCK, BLOCK), :], ysb[:, s, :]).then_inc(b["yo"][s], 16)
                alternating(sp, 0, BLOCKS[l], store_y)

            for t in range(NT):
                rows = G if t < NT - 1 else LAST
                sp.wait_ge(M[1]["comb"], t + 1)
                sp.dma_start(out[t * G:t * G + rows, :], h[:rows, t, :]).then_inc(s_out, 16)
            sp.wait_ge(s_out, 16 * NT)
            for l in range(2):
                for s in range(2):
                    sp.wait_ge(B[l]["yo"][s], 16 * ((BLOCKS[l] + 1 - s) // 2))

        @block.gpsimd
        def _(pool):
            nc.gpsimd.memset(zero[:, :], 0.0).then_inc(s_zero, 1)
            for w in vh:
                nc.gpsimd.memset(w[:, :, :], 1.0).then_inc(s_setup, 1)
            pool.wait_ge(s_weff, 1)
            for dst, src in ((wqk[0][:, :, :], a0_wqk), (bqk[:, :, :], a0_bqk), (wv[0][:, :, :], a0_wv),
                             (bv[:, :], a0_bv)):
                pool.dma_start(dst, src).then_inc(s_attw[0], 16)
            for l, src in ((0, gate0), (1, gate1)):
                pool.dma_start(gate[l][:, :, :], src).then_inc(s_gatew, 16)
            pool.dma_start(wa[:, :, :, :, :].rearrange("p s c g n -> p s (c g n)"), sh_wa).then_inc(s_shw1[0], 16)
            pool.dma_start(wd[:, :, :, :].rearrange("p s m n -> p s (m n)"), sh_wd).then_inc(s_shw1[0], 16)
            pool.wait_ge(s_zero, 1)
            for r in range(0, SLOTS, 3 * 128):
                pool.dma_start(xs_dram[r:r + 384, :].rearrange("(p r) n -> p (r n)", r=3), zero[:, :]
                               ).then_inc(s_zfill, 16)
            for dst, src in ((wqk[1][:, :, :], a1_wqk), (wv[1][:, :, :], a1_wv), (wo[:, :, :], a1_wo),
                             (bo[:, :], a1_bo)):
                pool.dma_start(dst, src).then_inc(s_attw[1], 16)

            for l in range(2):
                def stage(g):
                    nc.gpsimd.tensor_copy(xt_s[:, :, :], xnT[:, :, bass.ds(g * G, G)]).then_inc(A[l]["stage"], 1)
                pool.wait_ge(n_xt[2 * l], NT)
                stage(0)
                with pool.Fori(0, NT - 1) as g:
                    pool.wait_ge(A[l]["vp"], g + 1)
                    stage(g + 1)
                m, b = M[l], B[l]
                if l == 0:
                    pool.wait_ge(s_zfill, 16 * (SLOTS // 384))
                pool.wait_ge(m["idx"], 1)
                for t in range(NT):
                    rows = G if t < NT - 1 else LAST
                    for k in range(2):
                        nc.gpsimd.indirect_dma_start(
                            out=xs_dram, out_offset=bass.IndirectOffsetOnAxis(ap=slot_i[:rows, k, t:t + 1], axis=0),
                            in_=xn[:rows, t, :], in_offset=None).then_inc(m["scat"], 16)
                if l == 0:
                    pool.wait_ge(m["gup"], 2 * 3 * HC)
                    pool.wait_ge(m["dnp"], 2 * NT)

                def fetch_gate_up(n):
                    if n >= 2:
                        pool.wait_ge(b["gu"][1], n - 1)
                    nc.gpsimd.indirect_dma_start(
                        out=wa[:, n % 2, :, :, :].rearrange("p c g n -> p (c g n)"), out_offset=None, in_=e_wa[l],
                        in_offset=bass.IndirectOffsetOnAxis(ap=widx[:KD, 0, n:n + 1], axis=0)
                        ).then_inc(b["wa"][n % 2], 16)

                def fetch_down(n):
                    if n >= 2:
                        pool.wait_ge(b["dn"][n % 2], n // 2)
                    nc.gpsimd.indirect_dma_start(
                        out=wd[:, n % 2, :, :].rearrange("p m n -> p (m n)"), out_offset=None, in_=e_wd[l],
                        in_offset=bass.IndirectOffsetOnAxis(ap=widx[:, 1, n:n + 1], axis=0)
                        ).then_inc(b["wd"][n % 2], 16)
                fetch_gate_up(0)
                for n in range(1, BLOCKS[l]):
                    fetch_gate_up(n)
                    fetch_down(n - 1)
                fetch_down(BLOCKS[l] - 1)
                for s in range(2):
                    pool.wait_ge(b["yo"][s], 16 * ((BLOCKS[l] + 1 - s) // 2))
                for t in range(NT):
                    for k in range(2):
                        if t:
                            pool.wait_ge(g_y[l][k], 16 * t)
                        nc.gpsimd.indirect_dma_start(
                            out=yg[:, k, t, :], out_offset=None, in_=y_dram,
                            in_offset=bass.IndirectOffsetOnAxis(ap=slot_i[:, k, t:t + 1], axis=0)
                            ).then_inc(g_y[l][k], 16)

        @block.tensor
        def _(pe):
            pe.wait_ge(s_const, 16)
            pe.wait_ge(s_weff, 1)
            pe.wait_ge(s_beta, 32)
            for c in range(TAP_CHUNKS):
                nc.tensor.matmul(ps[:G, 4, 0:D], ones[:TP, :G], weff[:, c, 0:D],
                                 start=c == 0, stop=c == TAP_CHUNKS - 1)
            n = 0
            for c in range(TAP_CHUNKS):
                for g in range(5):
                    mm = nc.tensor.matmul(ps[:1, 5, 0:D], b5_sb[:, c, g:g + 1], w5_sb[:, c, g, :],
                                          start=n == 0, stop=n == 5 * TAP_CHUNKS - 1)
                    n += 1
            mm.then_inc(s_const_ps, 1)
            pe.wait_ge(s_crow, 1)
            nc.tensor.matmul(ps[:G, 6, 0:D], ones[:1, :G], crow[:, :], start=True, stop=True).then_inc(s_crep, 1)

            def tile(t, s, k):
                pe.wait_ge(t_in[s], 16 * (k + 1))
                pe.wait_ge(t_h[s], k)
                for c in range(TAP_CHUNKS):
                    nc.tensor.matmul(ps[:G, s, 0:D + 1], xc[:, s, c, :], weff[:, c, :],
                                     start=c == 0, stop=c == TAP_CHUNKS - 1)
                pe.wait_ge(t_red[s], k + 1)
                nc.tensor.matmul(ps[:G, s, D + 1:D + 2], xss[:, s, :], cst[:TP, C_COUNT:C_COUNT + 1],
                                 start=True, stop=True).then_inc(t_mm[s], 1)
            alternating(pe, 0, NT, tile)
            pe.wait_ge(t_h[0], (NT + 1) // 2)
            pe.wait_ge(t_h[1], NT // 2)

            def turn(i):
                for t in range(NT):
                    pe.wait_ge(n_xn[i], t + 1)
                    if t >= 4:
                        pe.wait_ge(n_xt[i], t - 3)
                    for c in range(2):
                        mm = nc.tensor.transpose(ps[:KD, t % 4, c * G:(c + 1) * G],
                                                 xn[:, t, c * KD:(c + 1) * KD], ident[:G, :G])
                    mm.then_inc(n_tp[i], 1)
                pe.wait_ge(n_xt[i], NT)

            def attention(l):
                a, hd, sets = A[l], HD[l], 2 * (l + 1)
                per = 4 // (l + 1)
                pe.wait_ge(s_attw[l], 64)
                if l == 0:
                    pe.wait_ge(s_setup, 3)

                def project_qk(g):
                    for q in range(sets):
                        pe.wait_ge(a["qke_d" if q % 2 else "qke_a"], g * (sets // 2) + q // 2)
                        if l == 1 or q < 2:
                            if q < 2:
                                pe.wait_ge(a["ve"], g)
                        for j in range(3):
                            n = 3 * q + j
                            for c in range(2):
                                mm = nc.tensor.matmul(ps[:, 4 + q % 2, j * G:(j + 1) * G],
                                                      wqk[l][:, c, n * 128:(n + 1) * 128],
                                                      xnT[:, c, bass.ds(g * G, G)], start=c == 0, stop=c == 1)
                        mm.then_inc(a["qkp"], 1)

                def project_v(g):
                    pe.wait_ge(a["stage"], g + 1)
                    pe.wait_ge(a["qke_a"], (g + 1) * (sets // 2))
                    pe.wait_ge(a["qke_d"], (g + 1) * (sets // 2))
                    w = INNER[l] // (l + 1)
                    for b in range(l + 1):
                        for c in range(2):
                            mm = nc.tensor.matmul(ps[:G, 4 + b, 0:w], xt_s[:, c, :], wv[l][:, c, b * w:(b + 1) * w],
                                                  start=c == 0, stop=c == 1)
                    mm.then_inc(a["vp"], 1)

                def scores(g):
                    pe.wait_ge(a["qke_a"], (g + 1) * (sets // 2))
                    pe.wait_ge(a["qke_d"], (g + 1) * (sets // 2))
                    pe.wait_ge(a["pta"], g)
                    pe.wait_ge(a["ptd"], g)
                    for b in range(4):
                        nc.tensor.matmul(ps[:G, b, 0:3 * G], identb[:, :], maskb[:, :], start=True, stop=False,
                                         skip_group_check=True)
                    for pos in range(3):
                        for b in range(4):
                            head = 4 * pos + b
                            chunk, r = head // per, (head % per) * (128 // per)
                            qs, js = chunk // 3, chunk % 3
                            mm = nc.tensor.matmul(ps[:G, b, pos * G:(pos + 1) * G],
                                                  qk[r:r + hd, qs, js, :], qk[r:r + hd, sets // 2 + qs, js, :],
                                                  start=False, stop=pos == 2, skip_group_check=True)
                    mm.then_inc(a["score"], 1)

                def turn_probs(g):
                    pe.wait_ge(a["exp"], g + 1)
                    for n in range(HEADS):
                        b, pos = n // 3, n % 3
                        mm = nc.tensor.transpose(ps[:G, b, pos * G:(pos + 1) * G], prob[:, n, :], ident[:G, :G])
                        if n == 5 or n == 11:
                            mm.then_inc(a["ptp"], 1)

                def mix(g):
                    pe.wait_ge(a["pta"], g + 1)
                    pe.wait_ge(a["ptd"], g + 1)
                    pe.wait_ge(a["ve"], g + 1)
                    pe.wait_ge(a["ctx"], g)
                    if l == 1:
                        pe.wait_ge(a["out"], g)
                    per_bank = HEADS // (l + 1)
                    for head in range(HEADS):
                        n = 3 * (head % 4) + head // 4
                        o = (head % per_bank) * (hd + 1)
                        mm = nc.tensor.matmul(ps[:G, 6 + head // per_bank, o:o + hd + 1], probT[:, n, :],
                                              vh[l][:, head, :], start=True, stop=True)
                    mm.then_inc(a["pv"], 1)

                def project_out(g):
                    pe.wait_ge(a["ctx"], g + 1)
                    for j in range(6):
                        mm = nc.tensor.transpose(ps[:, 4 + j // 3, (j % 3) * G:(j % 3 + 1) * G],
                                                 ctx[:, j * 128:(j + 1) * 128], ident[:G, :G])
                    mm.then_inc(a["ctp"], 1)
                    pe.wait_ge(a["cte"], g + 1)
                    for j in range(6):
                        mm = nc.tensor.matmul(ps[:G, 6, 0:D], ctxT[:, j, :], wo[:, j, :], start=j == 0, stop=j == 5)
                    mm.then_inc(a["op"], 1)

                def body(g, more):
                    scores(g)
                    if more:
                        project_qk(g + 1)
                    turn_probs(g)
                    mix(g)
                    if more:
                        project_v(g + 1)
                        if l == 1:
                            pe.wait_ge(a["ve"], g + 2)
                    if l == 1:
                        project_out(g)

                project_qk(0)
                project_v(0)
                body(0, True)
                with pe.Fori(1, NT - 1) as g:
                    body(g, True)
                body(NT - 1, False)
                pe.wait_ge(a["out"], NT)

            def experts(l):
                m, b = M[l], B[l]
                E = EXPERTS[l]
                pe.wait_ge(s_gatew, 32)
                for t in range(NT):
                    for c in range(2):
                        mm = nc.tensor.matmul(ps[:G, 0, t * E:(t + 1) * E], xnT[:, c, t * G:(t + 1) * G],
                                              gate[l][:, c, :], start=c == 0, stop=c == 1)
                mm.then_inc(m["lgp"], 1)
                pe.wait_ge(m["oh"], 1)
                nc.tensor.matmul(ps[:G, 4, 0:NT * E], cst[:G, C_UPPER:C_UPPER + G],
                                 oh[:, 2, :, 0:E], start=True, stop=True)
                nc.tensor.matmul(ps[:, 5, 0:NT * E], ones[:G, :], oh[:, 2, :, 0:E],
                                 start=True, stop=True).then_inc(m["cnt"], 1)
                pe.wait_ge(m["idx"], 1)
                if l == 0:
                    pe.wait_ge(s_shw1[0], 32)
                    n = ny = 0
                    done = []

                    def down(e, gi):
                        nonlocal ny
                        pe.wait_ge(m["mul"], HC * (3 * e + gi + 1))
                        for j, t in enumerate(GROUPS[gi]):
                            if ny >= 4:
                                pe.wait_ge(m["dne"], ny - 3)
                            for q in range(HC):
                                mm = nc.tensor.matmul(ps[:G, 4 + ny % 4, 0:D], hsh[:, q, j * G:(j + 1) * G],
                                                      wd[:, e, q, :], start=q == 0, stop=q == HC - 1)
                            mm.then_inc(m["dnp"], 1)
                            ny += 1

                    for e in range(2):
                        for gi, tiles in enumerate(GROUPS):
                            lo, w = tiles[0] * G, len(tiles) * G
                            for q in range(HC):
                                if n >= 2:
                                    pe.wait_ge(m["mul"], n - 1)
                                for u in range(2):
                                    for c in range(2):
                                        mm = nc.tensor.matmul(ps[:, 2 * (n % 2) + u, 0:w],
                                                              wa[:, e, c, u, q * 128:(q + 1) * 128],
                                                              xnT[:, c, lo:lo + w], start=c == 0, stop=c == 1)
                                mm.then_inc(m["gup"], 1)
                                n += 1
                            down(e, gi)
                    pe.wait_ge(m["dne"], 2 * NT)

                def turn_x(n, s, k):
                    pe.wait_ge(b["xg"][s], k + 1)
                    pe.wait_ge(b["te"][s], k)
                    for c in range(2):
                        mm = nc.tensor.transpose(ps[:KD, 4 + s, c * BLOCK:(c + 1) * BLOCK],
                                                 xg[:, s, c * KD:(c + 1) * KD], ident[:, :])
                    mm.then_inc(b["tp"][s], 1)

                def gate_up(n, s, k):
                    pe.wait_ge(b["wa"][s], 16 * (k + 1))
                    pe.wait_ge(b["te"][s], k + 1)
                    for half in range(2):
                        pe.wait_ge(b["hm"][half], n)
                        for u in range(2):
                            for q in range(3):
                                j = 3 * half + q
                                for c in range(2):
                                    mm = nc.tensor.matmul(ps[:, 2 * half + u, q * BLOCK:(q + 1) * BLOCK],
                                                          wa[:, s, c, u, j * 128:(j + 1) * 128],
                                                          xgT[:, s, c, :], start=c == 0, stop=c == 1)
                        mm.then_inc(b["gu"][half], 1)

                def down_y(n, s, k):
                    pe.wait_ge(b["wd"][s], 16 * (k + 1))
                    pe.wait_ge(b["hm"][1], n + 1)
                    pe.wait_ge(b["ye"][s], k)
                    for q in range(HC):
                        mm = nc.tensor.matmul(ps[:BLOCK, 6 + s, 0:D], hb[:, s, q, :], wd[:, s, q, :],
                                              start=q == 0, stop=q == HC - 1)
                    mm.then_inc(b["dn"][s], 1)

                NB = BLOCKS[l]
                turn_x(0, 0, 0)
                turn_x(1, 1, 0)
                gate_up(0, 0, 0)

                def step(n, s, k):
                    turn_x(n + 1, 1 - s, k + s)
                    gate_up(n, s, k)
                    down_y(n - 1, 1 - s, k - 1 + s)
                alternating(pe, 1, NB - 2, step)
                z = NB - 1
                gate_up(z, z % 2, z // 2)
                down_y(z - 1, (z - 1) % 2, (z - 1) // 2)
                down_y(z, z % 2, z // 2)
                for s in range(2):
                    pe.wait_ge(b["ye"][s], (NB + 1 - s) // 2)

            for l in range(2):
                turn(2 * l)
                attention(l)
                turn(2 * l + 1)
                experts(l)

        @block.scalar
        def _(act):
            act.wait_ge(s_const, 16)

            def take_tile(t, s, k):
                act.wait_ge(t_mm[s], k + 1)
                nc.scalar.copy(h[:, bass.ds(t, 1), :].rearrange("p a n -> p (a n)"), ps[:G, s, 0:D])
                nc.scalar.copy(tst[:, bass.ds(t, 1), :].rearrange("p a n -> p (a n)"), ps[:G, s, D:D + 2]
                               ).then_inc(t_h[s], 1)

            def square(t, s, k):
                act.wait_ge(t_in[s], 16 * (k + 1))
                act.wait_ge(t_red[s], k)
                nc.scalar.activation(xsq[:, s, :, :], xc[:, s, :, :], ACT.Square).then_inc(t_sq[s], 1)
                take_tile(t, s, k)
            alternating(act, 0, NT, square)

            def root(n):
                act.wait_ge(s_var, n)
                nc.scalar.activation(rstd[:, :], rinv[:, :], ACT.Sqrt).then_inc(s_root, 1)
            root(1)

            def evacuate_turned(i):
                for t in range(NT):
                    act.wait_ge(n_tp[i], t + 1)
                    nc.scalar.copy(xnT[:, :, t * G:(t + 1) * G],
                                   ps[:KD, t % 4, 0:2 * G].rearrange("p (c t) -> p c t", c=2)
                                   ).then_inc(n_xt[i], 1)

            def attention(l):
                a, sets = A[l], 2 * (l + 1)

                def take_qk(g):
                    for q in range(0, sets, 2):
                        act.wait_ge(a["qkp"], sets * g + q + 1)
                        act.wait_ge(a["score"], g)
                        src = ps[:, 4, 0:3 * G].rearrange("p (j t) -> p j t", j=3)
                        if l == 0:
                            for j in range(3):
                                op = nc.scalar.activation(qk[:, 0, j, :], src[:, j, :], ACT.Identity,
                                                          bias=bqk[:, 0, j:j + 1])
                            op.then_inc(a["qke_a"], 1)
                        else:
                            nc.scalar.copy(qk[:, q, :, :], src).then_inc(a["qke_a"], 1)

                def take_v(g):
                    if l == 1:
                        act.wait_ge(a["vp"], g + 1)
                        act.wait_ge(a["pv"], g)
                        nc.scalar.copy(v[:, :, 0:HD[1]].rearrange("p (b h) d -> p b h d", b=2),
                                       ps[:G, 4:6, 0:384].rearrange("p b (h d) -> p b h d", h=6)
                                       ).then_inc(a["ve"], 1)

                def body(g, more):
                    if more:
                        take_qk(g + 1)
                    act.wait_ge(a["sub"], g + 1)
                    nc.scalar.activation(prob[:, :, :], prob[:, :, :], ACT.Exp, scale=float(HD[l]) ** -0.5
                                         ).then_inc(a["exp"], 1)
                    act.wait_ge(a["ptp"], 2 * g + 1)
                    act.wait_ge(a["pv"], g)
                    nc.scalar.copy(probT[:, 0:6, :].rearrange("p (b j) t -> p b (j t)", b=2),
                                   ps[:G, 0:2, 0:3 * G]).then_inc(a["pta"], 1)
                    if more:
                        take_v(g + 1)
                    if l == 1:
                        act.wait_ge(a["ctp"], g + 1)
                        nc.scalar.copy(ctxT[:, :, :].rearrange("p (b j) t -> p b (j t)", b=2),
                                       ps[:, 4:6, 0:3 * G]).then_inc(a["cte"], 1)

                act.wait_ge(s_attw[l], 64)
                act.wait_ge(s_setup, 3)
                take_qk(0)
                take_v(0)
                body(0, True)
                with act.Fori(1, NT - 1) as g:
                    body(g, True)
                body(NT - 1, False)

            def experts(l):
                m, b = M[l], B[l]
                E = EXPERTS[l]
                act.wait_ge(m["ex"], 1)
                nc.scalar.activation(tmp[:, 0, :, 0:E], tmp[:, 0, :, 0:E], ACT.Exp).then_inc(m["exr"], 1)
                nc.scalar.activation(pw[:, 1, :], pw[:, 1, :], ACT.Exp).then_inc(m["exr"], 1)
                if l == 0:
                    n = 0
                    for e in range(2):
                        for tiles in GROUPS:
                            w = len(tiles) * G
                            for q in range(HC):
                                act.wait_ge(m["gup"], n + 1)
                                if n >= 2:
                                    act.wait_ge(m["mul"], n - 1)
                                nc.scalar.activation(silu[:, n % 2, 0:w], ps[:, 2 * (n % 2), 0:w], ACT.Silu
                                                     ).then_inc(m["silu"], 1)
                                n += 1

                def take_x(n, s, k):
                    act.wait_ge(b["tp"][s], k + 1)
                    if not isinstance(n, int) or n >= 2:
                        act.wait_ge(b["gu"][1], n - 1)
                    nc.scalar.copy(xgT[:, s, :, :].rearrange("p c t -> p (c t)"), ps[:KD, 4 + s, 0:2 * BLOCK]
                                   ).then_inc(b["te"][s], 1)

                def swish(n, s, k):
                    for half in range(2):
                        act.wait_ge(b["gu"][half], n + 1)
                        nc.scalar.activation(silu[:, half, 0:3 * BLOCK], ps[:, 2 * half, 0:3 * BLOCK], ACT.Silu
                                             ).then_inc(b["sl"][half], 1)

                def take_y(n, s, k):
                    act.wait_ge(b["dn"][s], k + 1)
                    act.wait_ge(b["yo"][s], 16 * k)
                    nc.scalar.copy(ysb[:, s, :], ps[:BLOCK, 6 + s, 0:D]).then_inc(b["ye"][s], 1)

                NB = BLOCKS[l]
                take_x(0, 0, 0)
                take_x(1, 1, 0)
                swish(0, 0, 0)

                def step(n, s, k):
                    take_x(n + 1, 1 - s, k + s)
                    swish(n, s, k)
                    take_y(n - 1, 1 - s, k - 1 + s)
                alternating(act, 1, NB - 2, step)
                z = NB - 1
                swish(z, z % 2, z // 2)
                take_y(z - 1, (z - 1) % 2, (z - 1) // 2)
                take_y(z, z % 2, z // 2)

            for l in range(2):
                root(2 * l + 2)
                evacuate_turned(2 * l)
                attention(l)
                root(2 * l + 3)
                evacuate_turned(2 * l + 1)
                experts(l)

        @block.vector
        def _(dve):
            count = [0]

            def link(op, before=None):
                op.then_inc(dve_own, 1)
                if before is None:
                    count[0] += 1
                    dve.wait_ge(dve_own, count[0])
                else:
                    dve.wait_ge(dve_own, before + 1)

            dve.wait_ge(s_const, 16)
            nc.vector.tensor_copy(identb[:, :], cst[:G, C_IDENT:C_IDENT + G])
            nc.vector.tensor_copy(maskb[:, :], cst[:G, C_MASK:C_MASK + 3 * G]).then_inc(s_setup, 1)
            dve.wait_ge(s_tokw, 32)
            for g in range(5):
                for c in range(TAP_CHUNKS):
                    if g == 0:
                        op = nc.vector.tensor_scalar(weff[:, c, 0:D], w5_sb[:, c, g, :], g5_sb[:, c, g:g + 1],
                                                     None, ALU.mult)
                    else:
                        op = nc.vector.scalar_tensor_tensor(out=weff[:, c, 0:D], in0=w5_sb[:, c, g, :],
                                                            scalar=g5_sb[:, c, g:g + 1], in1=weff[:, c, 0:D],
                                                            op0=ALU.mult, op1=ALU.add)
                link(op)
            nc.vector.tensor_copy(weff[:, :, D:D + 1],
                                  cst[:TP, C_COUNT:C_COUNT + 1].unsqueeze(2).to_broadcast([TP, TAP_CHUNKS, 1])
                                  ).then_inc(s_weff, 1)
            dve.wait_ge(s_const_ps, 1)
            dve.wait_ge(s_beta, 32)
            nc.vector.tensor_tensor(crow[:, :], ps[:1, 5, 0:D], tokb_sb[:, :], ALU.add).then_inc(s_crow, 1)
            nc.vector.tensor_copy(cs_sb[:, 0, :], ps[:G, 4, 0:D])
            dve.wait_ge(s_crep, 1)
            link(nc.vector.tensor_copy(cs_sb[:, 1, :], ps[:G, 6, 0:D]))

            def tile(t, s, k):
                dve.wait_ge(t_sq[s], k + 1)
                dve.wait_ge(t_mm[s], k)
                nc.vector.tensor_reduce(xss[:, s, :], xsq[:, s, :, :].rearrange("p c t -> p t c"), AX.X, ALU.add
                                        ).then_inc(t_red[s], 1)
            alternating(dve, 0, NT, tile)

            def inverse_root(n):
                link(nc.vector.reciprocal(rinv[:, :], var[:, :]))
                dve.sem_inc(s_var, 1)
                dve.wait_ge(s_root, n)
                link(nc.vector.tensor_tensor(rinv[:, :], rstd[:, :], rstd[:, :], ALU.mult))
                link(nc.vector.tensor_tensor(rinv[:, :], rinv[:, :], var[:, :], ALU.mult))
                link(nc.vector.tensor_scalar(rinv[:, :], rinv[:, :], -0.5, 1.5, ALU.mult, ALU.add))
                link(nc.vector.tensor_tensor(rstd[:, :], rstd[:, :], rinv[:, :], ALU.mult))

            for s in range(2):
                dve.wait_ge(t_h[s], (NT + 1 - s) // 2)
            link(nc.vector.tensor_scalar(tst[:, :, :], tst[:, :, :], 1.0 / FEATURES, None, ALU.mult))
            link(nc.vector.tensor_tensor(var[:, :], tst[:, :, 0], tst[:, :, 0], ALU.mult))
            link(nc.vector.tensor_tensor(var[:, :], tst[:, :, 1], var[:, :], ALU.subtract))
            link(nc.vector.tensor_scalar(var[:, :], var[:, :], TOK_EPS, None, ALU.add))
            inverse_root(1)
            link(nc.vector.scalar_tensor_tensor(out=shift[:, :], in0=tst[:, :, 0], scalar=-1.0, in1=rstd[:, :],
                                                op0=ALU.mult, op1=ALU.mult))
            for t in range(NT):
                op = nc.vector.scalar_tensor_tensor(out=h[:, t, :], in0=h[:, t, :], scalar=rstd[:, t:t + 1],
                                                    in1=cs_sb[:, 1, :], op0=ALU.mult, op1=ALU.add)
            link(op)
            for t in range(NT):
                op = nc.vector.scalar_tensor_tensor(out=h[:, t, :], in0=cs_sb[:, 0, :], scalar=shift[:, t:t + 1],
                                                    in1=h[:, t, :], op0=ALU.mult, op1=ALU.add)
            link(op)

            def normalise(i):
                for t in range(NT):
                    op = nc.vector.bn_stats(st6[:, t, :], h[:, t, :])
                link(op)
                for t in range(NT):
                    op = nc.vector.bn_aggr(mv[:, t, :], st6[:, t, :])
                link(op)
                link(nc.vector.tensor_scalar(var[:, :], mv[:, :, 1], LN_EPS, None, ALU.add))
                inverse_root(i + 2)
                for t in range(NT):
                    nc.vector.tensor_scalar(xn[:, t, :], h[:, t, :], mv[:, t, 0:1], rstd[:, t:t + 1],
                                            ALU.subtract, ALU.mult).then_inc(n_xn[i], 1)
                if i == 2:
                    dve.wait_ge(s_attw[1], 64)
                    dve.wait_ge(n_xn[i], NT)
                    link(nc.vector.tensor_tensor(h[:, :, :], h[:, :, :],
                                                 bo[:, :].unsqueeze(1).to_broadcast([G, NT, D]), ALU.add))

            def attention(l):
                a, hd, sets = A[l], HD[l], 2 * (l + 1)
                dve.wait_ge(s_attw[l], 64)
                dve.wait_ge(s_setup, 3)

                def take_qk(g):
                    for q in range(1, sets, 2):
                        dve.wait_ge(a["qkp"], sets * g + q + 1)
                        dve.wait_ge(a["score"], g)
                        src = ps[:, 5, 0:3 * G].rearrange("p (j t) -> p j t", j=3)
                        if l == 0:
                            op = nc.vector.tensor_tensor(qk[:, 1, :, :], src,
                                                         bqk[:, 1, :].unsqueeze(2).to_broadcast([128, 3, G]), ALU.add)
                        else:
                            op = nc.vector.tensor_copy(qk[:, q, :, :], src)
                        op.then_inc(a["qke_d"], 1)

                def take_v(g):
                    if l == 0:
                        dve.wait_ge(a["vp"], g + 1)
                        dve.wait_ge(a["pv"], g)
                        nc.vector.tensor_tensor(v0[:, :, 0:hd], ps[:G, 4, 0:D].rearrange("p (h d) -> p h d", h=HEADS),
                                                bv[:, :].rearrange("p (h d) -> p h d", h=HEADS), ALU.add
                                                ).then_inc(a["ve"], 1)

                own_n = 2
                first = count[0]

                def body(g, more):
                    own = first + own_n * g
                    scores = ps[:G, 0:4, 0:3 * G].rearrange("p b (j t) -> p b j t", j=3)
                    maxima = mx[:, :].rearrange("p (b j) -> p b j", b=4)
                    dve.wait_ge(a["score"], g + 1)
                    link(nc.vector.tensor_reduce(maxima, scores, AX.X, ALU.max), own)
                    nc.vector.tensor_tensor(prob[:, :, :].rearrange("p (b j) t -> p b j t", b=4), scores,
                                            maxima.unsqueeze(3).to_broadcast([G, 4, 3, G]), ALU.subtract
                                            ).then_inc(a["sub"], 1)
                    if more:
                        take_qk(g + 1)
                    dve.wait_ge(a["ptp"], 2 * g + 2)
                    dve.wait_ge(a["pv"], g)
                    nc.vector.tensor_copy(probT[:, 6:12, :].rearrange("p (b j) t -> p b (j t)", b=2),
                                          ps[:G, 2:4, 0:3 * G]).then_inc(a["ptd"], 1)
                    dve.wait_ge(a["pv"], g + 1)
                    nb = l + 1
                    got = ps[:G, 6:6 + nb, 0:HEADS // nb * (hd + 1)].rearrange("p b (h d) -> p b h d", d=hd + 1)
                    rv = rs[:, :].rearrange("p (b h) -> p b h", b=nb)
                    link(nc.vector.reciprocal(rv, got[:, :, :, hd]), own + 1)
                    cv = ctx[:, 0:INNER[l]].rearrange("p (b h d) -> p b h d", b=nb, d=hd)
                    op = nc.vector.tensor_tensor(cv, got[:, :, :, 0:hd],
                                                 rv.unsqueeze(3).to_broadcast([G, nb, HEADS // nb, hd]), ALU.mult)
                    ht = h[:, bass.ds(g, 1), :].rearrange("p a n -> p (a n)")
                    if l == 0:
                        op.then_inc(a["ctx"], 1)
                        dve.wait_ge(a["ctx"], g + 1)
                        nc.vector.tensor_tensor(ht, ht, ctx[:, 0:D], ALU.add).then_inc(a["out"], 1)
                        if more:
                            take_v(g + 1)
                    else:
                        op.then_inc(a["ctx"], 1)
                        dve.wait_ge(a["op"], g + 1)
                        nc.vector.tensor_tensor(ht, ps[:G, 6, 0:D], ht, ALU.add).then_inc(a["out"], 1)

                take_qk(0)
                take_v(0)
                body(0, True)
                with dve.Fori(1, NT - 1) as g:
                    body(g, True)
                body(NT - 1, False)
                count[0] = first + own_n * NT
                dve.wait_ge(a["out"], NT)

            def route(l):
                m, E, NB = M[l], EXPERTS[l], BLOCKS[l]
                iota_e = cst[:, C_IOTA_E:C_IOTA_E + E]
                dve.wait_ge(m["lgp"], 1)
                link(nc.vector.tensor_copy(lg[:, :, 0:E], ps[:G, 0, 0:NT * E].rearrange("p (t e) -> p t e", e=E)))
                for t in range(NT):
                    op = nc.vector.max(m8[:, t, :], lg[:, t, 0:E])
                link(op)
                nc.vector.tensor_tensor(tmp[:, 0, :, 0:E], lg[:, :, 0:E],
                                        m8[:, :, 0:1].to_broadcast([G, NT, E]), ALU.subtract)
                nc.vector.tensor_tensor(pw[:, 1, :], m8[:, :, 1], m8[:, :, 0], ALU.subtract).then_inc(m["ex"], 1)
                for t in range(NT):
                    op = nc.vector.max_index(i8[:, t, :], m8[:, t, :], lg[:, t, 0:E])
                link(op)
                for k in range(2):
                    op = nc.vector.tensor_tensor(idxf[:, k, :], i8[:, :, k], cst[:G, C_INVALID:C_INVALID + NT], ALU.add)
                link(op)
                for k in range(2):
                    op = nc.vector.tensor_tensor(oh[:, k, :, 0:E], iota_e[:G, :].unsqueeze(1).to_broadcast([G, NT, E]),
                                                 idxf[:, k, :].unsqueeze(2).to_broadcast([G, NT, E]), ALU.is_equal)
                link(op)
                nc.vector.tensor_tensor(oh[:, 2, :, 0:E], oh[:, 0, :, 0:E], oh[:, 1, :, 0:E], ALU.add
                                        ).then_inc(m["oh"], 1)
                dve.wait_ge(m["cnt"], 1)
                nc.vector.tensor_copy(tot[:, :, 0:E], ps[:, 5, 0:NT * E].rearrange("p (t e) -> p t e", e=E))
                link(nc.vector.memset(cum[:, 0, :], 0.0))
                for t in range(NT):
                    link(nc.vector.tensor_tensor(cum[:, t + 1, 0:E], cum[:, t, 0:E], tot[:, t, 0:E], ALU.add))
                link(nc.vector.tensor_tensor(cmp9[:, 0:E, :], cum[:, NT, 0:E].unsqueeze(2).to_broadcast([128, E, N_THRESH]),
                                             cst[:, C_THRESH:C_THRESH + N_THRESH].unsqueeze(1).to_broadcast(
                                                 [128, E, N_THRESH]), ALU.is_gt))
                link(nc.vector.tensor_reduce(nblk[:, 0:E], cmp9[:, 0:E, :], AX.X, ALU.add))
                link(nc.vector.tensor_copy(oend[:, 0:1], nblk[:, 0:1]))
                for e in range(1, E):
                    link(nc.vector.tensor_tensor(oend[:, e:e + 1], oend[:, e - 1:e], nblk[:, e:e + 1], ALU.add))
                nc.vector.tensor_tensor(obeg[:, 0:E], oend[:, 0:E], nblk[:, 0:E], ALU.subtract)
                link(nc.vector.tensor_tensor(cmpb[:, 0:NB, 0:E],
                                             cst[:, C_IOTA_B:C_IOTA_B + NB].unsqueeze(2).to_broadcast([128, NB, E]),
                                             oend[:, 0:E].unsqueeze(1).to_broadcast([128, NB, E]), ALU.is_ge))
                link(nc.vector.tensor_reduce(eb[:, 0:NB], cmpb[:, 0:NB, 0:E], AX.X, ALU.add))
                link(nc.vector.tensor_scalar(eb[:, 0:NB], eb[:, 0:NB], float(E - 1), None, ALU.min))
                for k, rows in ((0, KD), (1, 128)):
                    nc.vector.tensor_scalar(widx[:, k, 0:NB], eb[:, 0:NB], float(rows),
                                            cst[:, C_PIDX:C_PIDX + 1], ALU.mult, ALU.add)
                link(nc.vector.tensor_tensor(base[:, :, 0:E], ps[:G, 4, 0:NT * E].rearrange("p (t e) -> p t e", e=E),
                                             cum[:G, 0:NT, 0:E], ALU.add))
                link(nc.vector.scalar_tensor_tensor(out=base[:, :, 0:E],
                                                    in0=obeg[:G, 0:E].unsqueeze(1).to_broadcast([G, NT, E]),
                                                    scalar=float(BLOCK), in1=base[:, :, 0:E],
                                                    op0=ALU.mult, op1=ALU.add))
                dve.wait_ge(m["exr"], 2)
                if l == 0:
                    link(nc.vector.tensor_reduce(zsum[:, :], tmp[:, 0, :, 0:E], AX.X, ALU.add))
                for k in range(2):
                    op = nc.vector.tensor_tensor(oh[:, k, :, 0:E], oh[:, k, :, 0:E], base[:, :, 0:E], ALU.mult)
                link(op)
                link(nc.vector.tensor_reduce(slotf[:, :, :], oh[:, 0:2, :, 0:E], AX.X, ALU.add))
                nc.vector.tensor_copy(slot_i[:, :, :], slotf[:, :, :]).then_inc(m["idx"], 1)
                if l == 0:
                    link(nc.vector.reciprocal(pw[:, 0, :], zsum[:, :]))
                    link(nc.vector.tensor_tensor(pw[:, 1, :], pw[:, 1, :], pw[:, 0, :], ALU.mult))
                    link(nc.vector.scalar_tensor_tensor(out=zsum[:, :], in0=pw[:, 0, :], scalar=1e-8, in1=pw[:, 1, :],
                                                        op0=ALU.add, op1=ALU.add))
                else:
                    nc.vector.memset(pw[:, 0, :], 1.0)
                    link(nc.vector.tensor_scalar(zsum[:, :], pw[:, 1, :], 1.0, None, ALU.add))
                link(nc.vector.reciprocal(zsum[:, :], zsum[:, :]))
                link(nc.vector.tensor_tensor(cw[:, :, :], pw[:, :, :], zsum[:, :].unsqueeze(1).to_broadcast([G, 2, NT]),
                                             ALU.mult))

            def experts(l):
                m, b = M[l], B[l]
                route(l)
                if l == 0:
                    n = ny = 0
                    for e in range(2):
                        for gi, tiles in enumerate(GROUPS):
                            w = len(tiles) * G
                            for q in range(HC):
                                dve.wait_ge(m["silu"], n + 1)
                                if q == 0:
                                    if ny:
                                        dve.wait_ge(m["dnp"], ny)
                                nc.vector.tensor_tensor(hsh[:, q, 0:w], silu[:, n % 2, 0:w],
                                                        ps[:, 2 * (n % 2) + 1, 0:w], ALU.mult).then_inc(m["mul"], 1)
                                n += 1
                            for t in tiles:
                                dve.wait_ge(m["dnp"], ny + 1)
                                if e:
                                    dve.wait_ge(m["dne"], ny)
                                nc.vector.scalar_tensor_tensor(out=h[:, t, :], in0=ps[:G, 4 + ny % 4, 0:D], scalar=0.5,
                                                               in1=h[:, t, :], op0=ALU.mult, op1=ALU.add
                                                               ).then_inc(m["dne"], 1)
                                ny += 1
                    dve.wait_ge(m["dne"], ny)

                def stage(n, s, k):
                    dve.wait_ge(b["tp"][s], k)
                    nc.vector.tensor_copy(xg[:, s, :], xall[:, bass.ds(n, 1), :].rearrange("p a n -> p (a n)")
                                          ).then_inc(b["xg"][s], 1)

                def product(n, s, k):
                    dve.wait_ge(b["dn"][s], k)
                    for half in range(2):
                        dve.wait_ge(b["sl"][half], n + 1)
                        nc.vector.tensor_tensor(hb[:, s, 3 * half:3 * half + 3, :].rearrange("p q t -> p (q t)"),
                                                silu[:, half, 0:3 * BLOCK], ps[:, 2 * half + 1, 0:3 * BLOCK],
                                                ALU.mult).then_inc(b["hm"][half], 1)
                def step(n, s, k):
                    product(n, s, k)
                    stage(n + 2, s, k + 1)
                for i in range(3):
                    dve.wait_ge(m_xall[l][i], 16)
                stage(0, 0, 0)
                stage(1, 1, 0)
                alternating(dve, 0, BLOCKS[l] - 2, step)
                for n in (BLOCKS[l] - 2, BLOCKS[l] - 1):
                    product(n, n % 2, n // 2)

                for t in range(NT):
                    for k in range(2):
                        dve.wait_ge(g_y[l][k], 16 * (t + 1))
                        op = nc.vector.scalar_tensor_tensor(out=h[:, t, :], in0=yg[:, k, t, :], scalar=cw[:, k, t:t + 1],
                                                            in1=h[:, t, :], op0=ALU.mult, op1=ALU.add)
                        if k == 0:
                            link(op)
                        else:
                            op.then_inc(m["comb"], 1)
                dve.wait_ge(m["comb"], NT)

            for l in range(2):
                normalise(2 * l)
                attention(l)
                normalise(2 * l + 1)
                experts(l)


def kernel(**inputs):
    import numpy as _np
    import concourse.bacc as _bacc
    from concourse import mybir as _mybir
    from concourse.bass_utils import run_bass_kernel_spmd as _run

    a = {k: _np.asarray(v) for k, v in inputs.items()}

    def parts(w):
        return w.reshape(2, KD, -1).transpose(1, 0, 2)

    x = _np.zeros((NT * PER, IMG + 2, IMG + 2, CH), a["x"].dtype)
    x[:BATCH, 1:-1, 1:-1] = a["x"]
    xcol = _np.zeros((NT, TP, TAP_CHUNKS, PER, SIDE, SIDE), x.dtype)
    for p, row in enumerate(TAPS):
        for c, tap in enumerate(row):
            if tap is not None:
                ty, tx, ch = tap
                seen = x[:, ty + 1:ty + 2 + PATCH * (SIDE - 1):PATCH, tx + 1:tx + 2 + PATCH * (SIDE - 1):PATCH, ch]
                xcol[:, p, c] = seen.reshape(NT, PER, SIDE, SIDE)
    xcol = xcol.reshape(NT, TP, TAP_CHUNKS, G)
    moves = ((0, 0), (0, 1), (0, -1), (1, 0), (-1, 0))
    w = a["L0_tok_W"].reshape(PATCH, PATCH, 5, CH, D)
    ga = a["L0_tok_gamma"].reshape(PATCH, PATCH, 5, CH)
    be = a["L0_tok_beta"].reshape(PATCH, PATCH, 5, CH)
    w5 = _np.zeros((TP, TAP_CHUNKS, 5, D), w.dtype)
    g5 = _np.zeros((TP, TAP_CHUNKS, 5), ga.dtype)
    b5 = _np.zeros((TP, TAP_CHUNKS, 5), be.dtype)
    for p, row in enumerate(TAPS):
        for c, tap in enumerate(row):
            if tap is not None:
                for g, (my, mx_) in enumerate(moves):
                    y, xx = tap[0] + my, tap[1] + mx_
                    if 0 <= y < PATCH and 0 <= xx < PATCH:
                        w5[p, c, g], g5[p, c, g], b5[p, c, g] = w[y, xx, g, tap[2]], ga[y, xx, g, tap[2]], be[y, xx, g, tap[2]]

    qk0 = _np.zeros((D, 2, HEADS, 32), a["L0_attn_Wq"].dtype)
    bq0 = _np.zeros((2, HEADS, 32), a["L0_attn_bq"].dtype)
    for i, n in enumerate("qk"):
        qk0[:, i, :, :HD[0]] = a[f"L0_attn_W{n}"].T.reshape(D, HEADS, HD[0])
        bq0[i, :, :HD[0]] = a[f"L0_attn_b{n}"].reshape(HEADS, HD[0])

    def experts_in(g, u, d):
        e = g.shape[0]
        wa = _np.stack([g.reshape(e, 2, KD, HIDDEN), u.reshape(e, 2, KD, HIDDEN)], 3)
        return (wa.transpose(0, 2, 1, 3, 4).reshape(e * KD, 4 * HIDDEN),
                d.reshape(e, HC, 128, D).transpose(0, 2, 1, 3).reshape(e * 128, HC * D))

    sh_wa, sh_wd = experts_in(a["L0_ffn_shared_wg"], a["L0_ffn_shared_wu"], a["L0_ffn_shared_wd"])
    e0_wa, e0_wd = experts_in(a["L0_ffn_wg"], a["L0_ffn_wu"], a["L0_ffn_wd"])
    e1_wa, e1_wd = experts_in(*(a[f"L1_ffn_W{n}"].transpose(0, 2, 1) for n in "gud"))
    arrays = {
        "const": shape_constants(), "xcol": xcol, "w5": w5, "gamma5": g5, "beta5": b5,
        "tok_b": a["L0_tok_b"].reshape(1, D),
        "a0_wqk": parts(qk0.reshape(D, 768)), "a0_bqk": bq0.reshape(2, 3, 128).transpose(2, 0, 1),
        "a0_wv": parts(a["L0_attn_Wv"].T), "a0_bv": _np.broadcast_to(a["L0_attn_bv"], (G, D)),
        "a1_wqk": parts(_np.concatenate([a["L1_attn_w_q"], a["L1_attn_w_k"]], 1)),
        "a1_wv": parts(a["L1_attn_w_v"]), "a1_wo": a["L1_attn_w_o"].reshape(6, 128, D).transpose(1, 0, 2),
        "a1_bo": _np.broadcast_to(a["L1_attn_b_o"], (G, D)),
        "gate0": parts(a["L0_ffn_gate_w"].T), "gate1": parts(a["L1_ffn_router_w"].T),
        "sh_wa": sh_wa.reshape(2, KD, -1).transpose(1, 0, 2), "sh_wd": sh_wd.reshape(2, 128, -1).transpose(1, 0, 2),
        "e0_wa": e0_wa, "e0_wd": e0_wd, "e1_wa": e1_wa, "e1_wd": e1_wd,
    }
    arrays = {k: _np.ascontiguousarray(v) for k, v in arrays.items()}
    nc = _bacc.Bacc("TRN2", target_bir_lowering=False, num_devices=1)
    args = {k: nc.dram_tensor(k, v.shape, _mybir.dt.from_np(v.dtype), kind="ExternalInput").ap()
            for k, v in arrays.items()}
    out = nc.dram_tensor("out", (TOKENS, D), F32, kind="ExternalOutput").ap()
    xs = nc.dram_tensor("xs", (SLOTS, D), F32, kind="Internal").ap()
    y = nc.dram_tensor("y", (SLOTS, D), F32, kind="Internal").ap()
    program(nc, *args.values(), xs, y, out)
    r = _run(nc, [arrays], core_ids=[0])
    return r.results[0]["out"].reshape(BATCH, SEQ, D)
```

```python
import numpy as np

import concourse.bass as bass
from concourse import mybir
from concourse.alu_op_type import AluOpType as ALU

ACT = mybir.ActivationFunctionType
AX = mybir.AxisListType
F32 = mybir.dt.float32
BF16 = mybir.dt.bfloat16
F16 = mybir.dt.float16
U32 = mybir.dt.uint32

BATCH, IMG, CH, PATCH, D = 32, 96, 3, 16, 192
SIDE = IMG // PATCH
SEQ = SIDE * SIDE
TOKENS = BATCH * SEQ
FEATURES = PATCH * PATCH * 5 * CH
PER = 3
G = PER * SEQ
NT = -(-BATCH // PER)
PAD_TOKENS = NT * G
LAST = TOKENS - (NT - 1) * G
KD = 96
TAP_CHUNKS = 8
HEADS = 12
HD = (16, 64)
INNER = (HEADS * HD[0], HEADS * HD[1])
HIDDEN = 768
HC = HIDDEN // 128
EXPERTS = (16, 8)
BT = 96
BLOCK = 2 * BT
BLOCKS = tuple(-(-((2 * TOKENS + e * (BLOCK - 1)) // BLOCK) // 2) * 2 for e in EXPERTS)
SLOTS = max(BLOCKS) * BLOCK
LN_EPS, TOK_EPS = 1e-5, 1e-3
MASKED = -(2.0 ** 100)

X_SCALE, W_SCALE = 16.0, 64.0
XW = 1 / (X_SCALE * W_SCALE)
QKV_SCALE = 16.0
P_SCALE = 4096.0


def tap_table():
    classes = {}
    for y in range(-1, PATCH + 1):
        for x in range(-1, PATCH + 1):
            n = sum(0 <= y + a < PATCH and 0 <= x + b < PATCH
                    for a, b in ((0, 0), (0, 1), (0, -1), (1, 0), (-1, 0)))
            if n:
                classes.setdefault(n, []).extend((y, x, c) for c in range(CH))
    rows, counts = [], []
    for n, taps in sorted(classes.items()):
        taps = taps + [None] * (-len(taps) % TAP_CHUNKS)
        for i in range(0, len(taps), TAP_CHUNKS):
            rows.append(taps[i:i + TAP_CHUNKS])
            counts.append(n)
    return rows, counts


TAPS, TAP_COUNTS = tap_table()
TP = len(TAPS)

C_IDENT = 0
C_UPPER = C_IDENT + 128
C_ONES = C_UPPER + G
C_IOTA_E = C_ONES + 128
C_IOTA_B = C_IOTA_E + max(EXPERTS)
C_THRESH = C_IOTA_B + max(BLOCKS)
N_THRESH = -(-TOKENS // BLOCK)
C_PIDX = C_THRESH + N_THRESH
C_INVALID = C_PIDX + 1
C_COUNT = C_INVALID + NT
C_MASK = C_COUNT + 1
C_ALL = C_MASK + 4 * G


def shape_constants():
    c = np.zeros((128, C_ALL), np.float32)
    p = np.arange(128)
    c[:, C_IDENT:C_IDENT + 128] = np.eye(128)
    c[:, C_UPPER:C_UPPER + G] = p[:, None] < np.arange(G)[None, :]
    c[:, C_ONES:C_ONES + 128] = 1
    c[:, C_IOTA_E:C_IOTA_E + max(EXPERTS)] = np.arange(max(EXPERTS))
    c[:, C_IOTA_B:C_IOTA_B + max(BLOCKS)] = np.arange(max(BLOCKS))
    c[:, C_THRESH:C_THRESH + N_THRESH] = BLOCK * np.arange(N_THRESH)
    c[:, C_PIDX] = p
    c[LAST:, C_INVALID + NT - 1] = 100
    c[:TP, C_COUNT] = TAP_COUNTS
    image = np.arange(G) // SEQ
    other = image[:, None] != image[None, :]
    c[:G, C_MASK:] = np.tile(np.where(other, MASKED, 0.0), (1, 4))
    return c


def program(nc, const, xcol, w5, gamma5, beta5, tok_b, a0_w, a1_w, a1_wo, a1_bo, gate0, gate1,
            sh_wa, sh_wd, e0_wa, e0_wd, e1_wa, e1_wd, slots_dram, out):
    def sb(name, shape, dt=F32):
        return nc.alloc_sbuf_tensor(name, shape, dt)

    def sem(name):
        return nc.alloc_semaphore(name)

    def sems(name, n):
        return [sem(f"{name}{i}") for i in range(n)]

    ps = nc.alloc_psum_tensor("ps", [128, 8, 512], F32)

    cst = sb("cst", [128, C_ALL])
    h = sb("h", [G, NT, D])
    xn = sb("xn", [G, NT, D])
    xh, xl = sb("xh", [128, 2, PAD_TOKENS], F16), sb("xl", [128, 2, PAD_TOKENS], F16)
    identb = sb("identb", [G, G], BF16)
    maskb = sb("maskb", [G, 4 * G], BF16)
    zero = sb("zero", [128, 6 * D])
    st6 = sb("st6", [G, NT, 6])
    mv = sb("mv", [G, NT, 2])
    rstd = sb("rstd", [G, NT])
    var = sb("var", [G, NT])
    rinv = sb("rinv", [G, NT])
    ident = cst[:, C_IDENT:C_IDENT + 128]
    ones = cst[:, C_ONES:C_ONES + 128]

    big = sb("big", [128, TAP_CHUNKS * 5 * D])
    w5_sb = big[:TP, :].rearrange("p (c g n) -> p c g n", c=TAP_CHUNKS, g=5)
    g5_sb = sb("g5_sb", [TP, TAP_CHUNKS, 5])
    b5_sb = sb("b5_sb", [TP, TAP_CHUNKS, 5])
    tokb_sb = sb("tokb_sb", [1, D])
    weff = sb("weff", [TP, TAP_CHUNKS, D + 1])
    crow = sb("crow", [1, D])
    cs_sb = sb("cs_sb", [G, 2, D])
    shared = sb("shared", [128, 2 * 2 * 4 * HIDDEN // 2])
    xc = shared[:TP, 0:2 * TAP_CHUNKS * G].rearrange("p (s c t) -> p s c t", s=2, c=TAP_CHUNKS)
    xsq = shared[:TP, 2 * TAP_CHUNKS * G:4 * TAP_CHUNKS * G].rearrange("p (s c t) -> p s c t", s=2, c=TAP_CHUNKS)
    xss = sb("xss", [TP, 2, G])
    tst = sb("tst", [G, NT, 2])
    shift = sb("shift", [G, NT])

    W_COLS = (2 * 384 + INNER[0], 3 * INNER[1])
    ah, al = sb("ah", [128, 2, W_COLS[1]], F16), sb("al", [128, 2, W_COLS[1]], F16)
    wo = sb("wo", [128, 6, D])
    bo = sb("bo", [G, D])
    o_qkl, o_prob, o_pth, o_ptl, o_ctx = 6 * G, 12 * G, 24 * G, 30 * G, 36 * G
    o_ctxT = o_ctx + INNER[1]
    work = sb("work", [128, o_ctxT + 6 * G])
    qkh = work[:, 0:o_qkl].bitcast(F16).rearrange("p (q n) -> p q n", q=4)
    qkl = work[:, o_qkl:o_prob].bitcast(F16).rearrange("p (q n) -> p q n", q=4)
    prob = work[:G, o_prob:o_pth].rearrange("p (n t) -> p n t", n=HEADS)
    pth = work[:G, o_pth:o_ptl].bitcast(F16).rearrange("p (n t) -> p n t", n=HEADS)
    ptl = work[:G, o_ptl:o_ctx].bitcast(F16).rearrange("p (n t) -> p n t", n=HEADS)
    ctx = work[:G, o_ctx:o_ctxT]
    ctxT = work[:, o_ctxT:o_ctxT + 6 * G].rearrange("p (j t) -> p j t", j=6)
    araw = [work[:, 0:2 * w].rearrange("p (c n) -> p c n", c=2) for w in W_COLS]
    kdh = big[:, 0:6 * G].bitcast(F16).rearrange("p (c h t) -> p c h t", c=3, h=4)
    kdl = big[:, 6 * G:12 * G].bitcast(F16).rearrange("p (c h t) -> p c h t", c=3, h=4)
    vh = [sb(f"vh{l}", [G, HEADS, HD[l] + 1], F16) for l in range(2)]
    vl = [sb(f"vl{l}", [G, HEADS, HD[l] + 1], F16) for l in range(2)]
    mx = sb("mx", [G, HEADS])
    rs = sb("rs", [G, HEADS])

    graw = [sb(f"graw{l}", [KD, 2, EXPERTS[l]]) for l in range(2)]
    gh = [sb(f"gh{l}", [KD, 2, EXPERTS[l]], F16) for l in range(2)]
    gl = [sb(f"gl{l}", [KD, 2, EXPERTS[l]], F16) for l in range(2)]
    wraw = sb("wraw", [KD, 4, HIDDEN])
    half = 4 * HIDDEN // 2
    wah = [shared[:KD, s * half:(s + 1) * half].bitcast(F16).rearrange("p (q n) -> p q n", q=4) for s in range(2)]
    wal = [shared[:KD, (2 + s) * half:(3 + s) * half].bitcast(F16).rearrange("p (q n) -> p q n", q=4)
           for s in range(2)]
    wd = sb("wd", [128, 2, HC, D])
    lg = sb("lg", [G, NT, 16])
    m8 = sb("m8", [G, NT, 8])
    i8 = sb("i8", [G, NT, 8], U32)
    idxf = sb("idxf", [G, 2, NT])
    oh = sb("oh", [G, 3, NT, 16])
    base = sb("base", [G, NT, 16])
    tmp = sb("tmp", [G, 2, NT, 16])
    tot = sb("tot", [128, NT, 16])
    cum = sb("cum", [128, NT + 1, 16])
    cmp9 = sb("cmp9", [128, 16, N_THRESH])
    nblk = sb("nblk", [128, 16])
    oend = sb("oend", [128, 16])
    obeg = sb("obeg", [128, 16])
    cmpb = sb("cmpb", [128, max(BLOCKS), 16])
    eb = sb("eb", [128, max(BLOCKS)])
    ebi = sb("ebi", [1, max(BLOCKS)], U32)
    nit = sb("nit", [1, 2 + max(BLOCKS)])
    niti = sb("niti", [1, 1], U32)
    slotf = sb("slotf", [G, 2, NT])
    slot_i = sb("slot_i", [G, 2, NT], U32)
    cw = sb("cw", [G, 2, NT])
    zsum = sb("zsum", [G, NT])
    pw = sb("pw", [G, 2, NT])
    xg = sb("xg", [BT, 2, 2, D])
    xgh, xgl = sb("xgh", [KD, 2, 2, BLOCK], F16), sb("xgl", [KD, 2, 2, BLOCK], F16)
    silu = sb("silu", [128, 2, 4 * G])
    hb = sb("hb", [128, 2, HC, BLOCK])
    ysb = sb("ysb", [BT, 2, 2, D])
    hsh = big[:, 0:HC * 4 * G].rearrange("p (m t) -> p m t", m=HC)
    yg = big[:G, HC * 4 * G:HC * 4 * G + 2 * NT * D].rearrange("p (k t n) -> p k t n", k=2, t=NT)

    s_const, s_gamma, s_beta, s_tokb = sem("s_const"), sem("s_gamma"), sem("s_beta"), sem("s_tokb")
    s_w5 = sems("s_w5", 4)
    s_fold = sem("s_fold")
    s_attw, s_gatew, s_wo, s_wd = sems("s_attw", 2), sem("s_gatew"), sem("s_wo"), sem("s_wd")
    s_shared_in = sems("s_shared_in", 4)
    s_att_split, s_gate_split, s_shared_split, s_high = (sem("s_att_split"), sem("s_gate_split"),
                                                         sem("s_shared_split"), sem("s_high"))
    s_const_set, s_zfill, s_setup, s_weff = sem("s_const_set"), sem("s_zfill"), sem("s_setup"), sem("s_weff")
    s_const_ps, s_crow, s_crep, s_cs = sem("s_const_ps"), sem("s_crow"), sem("s_crep"), sem("s_cs")
    t_in, t_sq, t_red, t_mm, t_h = sems("t_in", 2), sems("t_sq", 2), sems("t_red", 2), sems("t_mm", 2), sems("t_h", 2)
    dve_own = sem("dve_own")
    n_xn, n_tp, n_xh, n_xt = sem("n_xn"), sem("n_tp"), sem("n_xh"), sem("n_xt")
    s_var, s_root = sem("s_var"), sem("s_root")
    a_names = ("qkp", "qkh", "qkl", "vp", "vh", "ve", "score", "sub", "exp", "ptp", "pth", "ptl", "pv",
               "ctx", "out")
    A = [{n: sem(f"a{l}_{n}") for n in a_names + (("ctp", "cte", "op") if l else ())} for l in range(2)]
    m_names = ("lgp", "oh", "cnt", "ex", "exr", "idx", "scat", "comb", "ydone")
    M = [{n: sem(f"m{l}_{n}") for n in m_names + (() if l else ("gup", "silu", "mul", "dnp", "dne"))}
         for l in range(2)]
    b_names = ("tp", "teh", "te", "wh", "wl", "gu", "sl", "hm", "dn", "ye")
    B = [{n: sem(f"b{l}_{n}") for n in b_names} for l in range(2)]
    w_in = [sems(f"b{l}_w", 4) for l in range(2)]
    xg_in, wd_in, y_out, g_y = ([sems(f"b{l}_{n}", 2) for l in range(2)] for n in ("xg", "wd", "yo", "gy"))
    s_out = sem("s_out")

    e_wa, e_wd = [e0_wa, e1_wa], [e0_wd, e1_wd]
    GROUPS = [range(0, 4), range(4, 8), range(8, NT)]

    def alternating(eng, first, count, step):
        while first < 3:
            step(first, first % 2, first // 2)
            first, count = first + 1, count - 1
        if count // 2:
            with eng.Fori(0, count // 2) as i:
                for j in (first, first + 1):
                    step(2 * i + j, j % 2, i + j // 2)
        if count % 2:
            last = first + count - 1
            step(last, last % 2, last // 2)

    def over_blocks(pairs, step):
        def run(eng):
            for n in range(3):
                step(n, n % 2, n // 2, True)
            with eng.Fori(0, pairs[0]) as i:
                for j in (3, 4):
                    step(2 * i + j, j % 2, i + j // 2, True)
            step(2 * pairs[1] - 1, 1, pairs[1] - 1, False)
        return run

    def wait_from(eng, s, value):
        if not isinstance(value, int) or value > 0:
            eng.wait_ge(s, value)

    def blocks_of(eng):
        beyond = eng.value_load(niti[0:1, 0:1], min_val=0, max_val=max(BLOCKS) // 2 - 2)
        return beyond, beyond + 2

    GROUPS_OF, IN_GROUP, IN_BANK = (3, 2), (4, 6), (4, 3)

    def head_of(l, n):
        return 4 * (n % 3) + n // 3 if l else n

    def in_banks(l, i):
        return ps[:G, (l + 1) * i:(l + 1) * (i + 1), 0:IN_BANK[l] * G]

    def in_group(l, i, x):
        return x[:, IN_GROUP[l] * i:IN_GROUP[l] * (i + 1), :].rearrange("p (b j) t -> p b (j t)", b=l + 1)

    block = nc.Block()
    with block:
        @block.sync
        def _(sp):
            sp.dma_start(g5_sb[:, :, :], gamma5).then_inc(s_gamma, 16)
            sp.dma_start(w5_sb[:, 0:2, :, :], w5[:, 0:2, :, :]).then_inc(s_w5[0], 16)
            sp.dma_start(b5_sb[:, :, :], beta5).then_inc(s_beta, 16)
            sp.dma_start(w5_sb[:, 2:4, :, :], w5[:, 2:4, :, :]).then_inc(s_w5[1], 16)
            sp.dma_start(cst[:, :], const).then_inc(s_const, 16)
            for c in (4, 6):
                sp.dma_start(w5_sb[:, c:c + 2, :, :], w5[:, c:c + 2, :, :]).then_inc(s_w5[c // 2], 16)
            sp.dma_start(tokb_sb[:, :], tok_b).then_inc(s_tokb, 16)

            def load_tile(t, s, k):
                sp.wait_ge(t_mm[s], k)
                sp.dma_start(xc[:, s, :, :], xcol[bass.ds(t, 1)].rearrange("a p c t -> (a p) c t")
                             ).then_inc(t_in[s], 16)
            alternating(sp, 0, NT, load_tile)

            for p in range(4):
                sp.dma_start(wraw[:, p, :], sh_wa[0:KD, p, :]).then_inc(s_shared_in[p], 16)
            sp.dma_start(wd[:, 0, :, :].rearrange("p m n -> p (m n)"), sh_wd[0:128, :]).then_inc(s_wd, 16)
            sp.wait_ge(A[0]["out"], NT)
            sp.dma_start(araw[1], a1_w).then_inc(s_attw[1], 16)

            for l in range(2):
                b, m = B[l], M[l]
                sp.wait_ge(m["idx"], 1)
                pairs = blocks_of(sp)
                if l == 0:
                    sp.wait_ge(s_shared_split, 4)

                def load_down(n, s):
                    e = sp.value_load(ebi[0:1, bass.ds(n, 1)], min_val=0, max_val=EXPERTS[l] - 1)
                    if isinstance(n, int) and n == 0 and l == 0:
                        sp.wait_ge(m["dnp"], NT)
                    wait_from(sp, b["dn"], n - 1)
                    sp.dma_start(wd[:, s, :, :].rearrange("p m n -> p (m n)"), e_wd[l][bass.ds(e * 128, 128), :]
                                 ).then_inc(wd_in[l][s], 16)

                def store_y(n, s):
                    sp.wait_ge(b["ye"], n + 1)
                    sp.dma_start(slots_dram[bass.ds(n * BLOCK, BLOCK), :].rearrange("(j p) n -> p j n", p=BT),
                                 ysb[:, s, :, :]).then_inc(y_out[l][s], 16)

                def load_rows(n, s):
                    wait_from(sp, b["tp"], n - 1)
                    sp.dma_start(xg[:, s, :, :], slots_dram[bass.ds(n * BLOCK, BLOCK), :].rearrange(
                        "(j p) n -> p j n", p=BT)).then_inc(xg_in[l][s], 16)

                def step(n, s, k, more):
                    first = isinstance(n, int) and n == 0
                    if not first:
                        load_rows(n, s)
                    e = sp.value_load(ebi[0:1, bass.ds(n, 1)], min_val=0, max_val=EXPERTS[l] - 1)
                    for p in range(4):
                        wait_from(sp, b["wl"], 4 * (n - 1) + p + 1)
                        sp.dma_start(wraw[:, p, :], e_wa[l][bass.ds(e * KD, KD), p, :]).then_inc(w_in[l][p], 16)
                    if first:
                        sp.wait_ge(m["scat"], 16 * 2 * NT)
                        load_rows(n, s)
                    if not isinstance(n, int) or n >= 1:
                        load_down(n - 1, 1 - s)
                    if not isinstance(n, int) or n >= 3:
                        store_y(n - 3, 1 - s)
                over_blocks(pairs, step)(sp)
                last = 2 * pairs[1]
                if l == 0:
                    for p in range(4):
                        sp.wait_ge(b["wl"], 4 * (last - 1) + p + 1)
                        sp.dma_start(wraw[:, p, :], sh_wa[KD:2 * KD, p, :]).then_inc(w_in[l][p], 16)
                load_down(last - 1, 1)
                if l == 0:
                    sp.wait_ge(b["dn"], last - 1)
                    sp.dma_start(wd[:, 0, :, :].rearrange("p m n -> p (m n)"), sh_wd[128:256, :]).then_inc(s_wd, 16)
                for j in (3, 2, 1):
                    store_y(2 * pairs[1] - j, j % 2)
                for s in range(2):
                    sp.wait_ge(y_out[l][s], 16 * pairs[1])
                sp.sem_inc(m["ydone"], 1)

            for t in range(NT):
                rows = G if t < NT - 1 else LAST
                sp.wait_ge(M[1]["comb"], t + 1)
                sp.dma_start(out[t * G:t * G + rows, :], h[:rows, t, :]).then_inc(s_out, 16)
            sp.wait_ge(s_out, 16 * NT)

        @block.gpsimd
        def _(pool):
            constants = [(zero[:, :], 0.0), (xh[KD:, :, :], 0.0), (xh[KD:KD + 1, 1, :], X_SCALE), (xl[KD:, :, :], 0.0)]
            for l in range(2):
                constants += [(vh[l][:, :, HD[l]:], QKV_SCALE), (vl[l][:, :, HD[l]:], 0.0)]
            for n, (to, value) in enumerate(constants):
                nc.gpsimd.memset(to, value).then_inc(s_const_set, 1)
                pool.wait_ge(s_const_set, n + 1)
            pool.wait_ge(t_in[1], 16)
            pool.dma_start(araw[0], a0_w).then_inc(s_attw[0], 16)
            for l, src in ((0, gate0), (1, gate1)):
                pool.dma_start(graw[l][:, :, :], src).then_inc(s_gatew, 16)
            pool.dma_start(wo[:, :, :], a1_wo).then_inc(s_wo, 16)
            pool.dma_start(bo[:, :], a1_bo).then_inc(s_wo, 16)
            pool.wait_ge(s_weff, 1)
            pool.wait_ge(s_const_ps, 1)
            nc.gpsimd.memset(big[:, 0:12 * G], 0.0).then_inc(s_const_set, 1)
            for lo in range(0, SLOTS, 6 * 128):
                n = lo // 768 + 2
                if n < NT:
                    pool.wait_ge(t_in[n % 2], 16 * (n // 2 + 1))
                pool.dma_start(slots_dram[lo:lo + 768, :].rearrange("(p r) n -> p (r n)", r=6), zero[:, :]
                               ).then_inc(s_zfill, 16)

            splits = 0

            def split(high, low, raw, done):
                nonlocal splits
                splits += 1
                nc.gpsimd.tensor_scalar(raw, raw, W_SCALE, None, ALU.mult).then_inc(s_high, 1)
                pool.wait_ge(s_high, 2 * splits - 1)
                nc.gpsimd.tensor_copy(high, raw).then_inc(s_high, 1)
                pool.wait_ge(s_high, 2 * splits)
                nc.gpsimd.tensor_tensor(low, raw, high, ALU.subtract).then_inc(done, 1)

            def split_attention(l):
                pool.wait_ge(s_attw[l], 16)
                if l:
                    pool.wait_ge(A[0]["out"], NT)
                split(ah[:, :, 0:W_COLS[l]], al[:, :, 0:W_COLS[l]], araw[l], s_att_split)
            split_attention(0)
            pool.wait_ge(s_gatew, 32)
            for l in range(2):
                split(gh[l][:, :, :], gl[l][:, :, :], graw[l][:, :, :], s_gate_split)
            for s in range(2):
                pool.wait_ge(t_mm[s], (NT + 1 - s) // 2)
            for p in range(4):
                pool.wait_ge(s_shared_in[p], 16)
                split(wah[0][:, p, :], wal[0][:, p, :], wraw[:, p, :], s_shared_split)

            for l in range(2):
                m, b = M[l], B[l]
                if l == 0:
                    pool.wait_ge(s_zfill, 16 * (SLOTS // 768))
                pool.wait_ge(m["idx"], 1)
                for t in range(NT):
                    rows = G if t < NT - 1 else LAST
                    for k in range(2):
                        nc.gpsimd.indirect_dma_start(
                            out=slots_dram, out_offset=bass.IndirectOffsetOnAxis(ap=slot_i[:rows, k, t:t + 1], axis=0),
                            in_=xn[:rows, t, :], in_offset=None).then_inc(m["scat"], 16)
                if l == 0:
                    split_attention(1)
                pool.wait_ge(m["ydone"], 1)
                for t in range(NT):
                    for k in range(2):
                        if t:
                            pool.wait_ge(g_y[l][k], 16 * t)
                        nc.gpsimd.indirect_dma_start(
                            out=yg[:, k, t, :], out_offset=None, in_=slots_dram,
                            in_offset=bass.IndirectOffsetOnAxis(ap=slot_i[:, k, t:t + 1], axis=0)
                            ).then_inc(g_y[l][k], 16)

        @block.tensor
        def _(pe):
            pe.wait_ge(s_beta, 16)
            n = 0
            for c in range(TAP_CHUNKS):
                if c % 2 == 0:
                    pe.wait_ge(s_w5[c // 2], 16)
                for g in range(5):
                    mm = nc.tensor.matmul(ps[:1, 5, 0:D], b5_sb[:, c, g:g + 1], w5_sb[:, c, g, :],
                                          start=n == 0, stop=n == 5 * TAP_CHUNKS - 1)
                    n += 1
            mm.then_inc(s_const_ps, 1)
            pe.wait_ge(s_const, 16)
            pe.wait_ge(s_weff, 1)

            def tile(t, s, k):
                pe.wait_ge(t_in[s], 16 * (k + 1))
                pe.wait_ge(t_h[s], k)
                for c in range(TAP_CHUNKS):
                    nc.tensor.matmul(ps[:G, s, 0:D + 1], xc[:, s, c, :], weff[:, c, :],
                                     start=c == 0, stop=c == TAP_CHUNKS - 1)
                pe.wait_ge(t_red[s], k + 1)
                nc.tensor.matmul(ps[:G, s, D + 1:D + 2], xss[:, s, :], cst[:TP, C_COUNT:C_COUNT + 1],
                                 start=True, stop=True).then_inc(t_mm[s], 1)
            alternating(pe, 0, NT, tile)
            for c in range(TAP_CHUNKS):
                nc.tensor.matmul(ps[:G, 4, 0:D], ones[:TP, :G], weff[:, c, 0:D],
                                 start=c == 0, stop=c == TAP_CHUNKS - 1)
            pe.wait_ge(s_crow, 1)
            nc.tensor.matmul(ps[:G, 6, 0:D], ones[:1, :G], crow[:, :], start=True, stop=True).then_inc(s_crep, 1)
            pe.wait_ge(t_h[0], (NT + 1) // 2)
            pe.wait_ge(t_h[1], NT // 2)

            def product(out, left, right, start, stop):
                for n, (a, b) in enumerate(((0, 0), (0, 1), (1, 0))):
                    mm = nc.tensor.matmul(out, left[a], right[b], start=start and n == 0, stop=stop and n == 2)
                return mm

            def turn(i):
                for t in range(NT):
                    pe.wait_ge(n_xn, NT * i + t + 1)
                    if t >= 4:
                        pe.wait_ge(n_xt, NT * i + t - 3)
                    for c in range(2):
                        mm = nc.tensor.transpose(ps[:KD, t % 4, c * G:(c + 1) * G],
                                                 xn[:, t, c * KD:(c + 1) * KD], ident[:G, :G])
                    mm.then_inc(n_tp, 1)
                pe.wait_ge(n_xt, NT * (i + 1))

            def attention(l):
                a, hd, sets, ng = A[l], HD[l], 2 * (l + 1), GROUPS_OF[l]
                pe.wait_ge(s_att_split, l + 1)
                pe.wait_ge(s_setup, 1)
                pe.wait_ge(s_const_set, 9)

                def project_qk(g, q):
                    if q < 2:
                        wait_from(pe, a["ve"], g)
                    else:
                        pe.wait_ge(a["qkl"], sets * g + q - 1)
                    for j in range(3):
                        n = 3 * q + j
                        for c in range(2):
                            mm = product(ps[:, 4 + q % 2, j * G:(j + 1) * G],
                                         [w[:, c, n * 128:(n + 1) * 128] for w in (ah, al)],
                                         [x[:, c, bass.ds(g * G, G)] for x in (xh, xl)], c == 0, c == 1)
                    mm.then_inc(a["qkp"], 1)

                def project_v(g):
                    pe.wait_ge(a["qkl"], sets * g + (sets if l else 1))
                    w, o = INNER[l] // (l + 1), 2 * 384 * (l + 1)
                    for b in range(l + 1):
                        for c in range(2):
                            mm = product(ps[:G, 4 + b, 0:w], [x[:, c, bass.ds(g * G, G)] for x in (xh, xl)],
                                         [m[:, c, o + b * w:o + (b + 1) * w] for m in (ah, al)],
                                         c == 0, c == 1)
                    mm.then_inc(a["vp"], 1)

                def scores(g, i):
                    if i == 0:
                        pe.wait_ge(a["qkl"], sets * (g + 1))
                    wait_from(pe, a["ptl"], ng * (g - 1) + i + 1 if not isinstance(g, int) or g else 0)
                    banks = range((l + 1) * i, (l + 1) * (i + 1))
                    w = IN_BANK[l] * G
                    for b in banks:
                        nc.tensor.matmul(ps[:G, b, 0:w], identb[:, :], maskb[:, 0:w], start=True, stop=False,
                                         skip_group_check=True)
                    if l == 0:
                        for n, (x, y) in enumerate(((qkh, kdh), (qkh, kdl), (qkl, kdh))):
                            mm = nc.tensor.matmul(ps[:G, i, 0:w], x[:, 0, i * G:(i + 1) * G],
                                                  y[:, i, :, :].rearrange("p h t -> p (h t)"),
                                                  start=False, stop=n == 2, skip_group_check=True)
                    else:
                        for j in range(3):
                            for b in banks:
                                head = head_of(l, 3 * b + j)
                                chunk, r = head // 2, (head % 2) * hd
                                qs, js = chunk // 3, chunk % 3
                                for n, (x, y) in enumerate(((qkh, qkh), (qkh, qkl), (qkl, qkh))):
                                    mm = nc.tensor.matmul(ps[:G, b, j * G:(j + 1) * G],
                                                          x[r:r + hd, qs, js * G:(js + 1) * G],
                                                          y[r:r + hd, 2 + qs, js * G:(js + 1) * G],
                                                          start=False, stop=n == 2 and j == 2, skip_group_check=True)
                    mm.then_inc(a["score"], 1)

                def turn_probs(g, i):
                    pe.wait_ge(a["exp"], ng * g + 1 + i)
                    for n in range(IN_GROUP[l] * i, IN_GROUP[l] * (i + 1)):
                        j = n % IN_BANK[l]
                        mm = nc.tensor.transpose(ps[:G, n // IN_BANK[l], j * G:(j + 1) * G], prob[:, n, :],
                                                 ident[:G, :G])
                    mm.then_inc(a["ptp"], 1)

                def mix(g, i):
                    pe.wait_ge(a["ptl"], ng * g + 1 + i)
                    if i == 0:
                        pe.wait_ge(a["ve"], g + 1)
                        wait_from(pe, a["ctx"], g)
                        if l == 1:
                            wait_from(pe, a["out"], g)
                    per_bank = HEADS // (l + 1)
                    for n in range(IN_GROUP[l] * i, IN_GROUP[l] * (i + 1)):
                        head = head_of(l, n)
                        o = (head % per_bank) * (hd + 1)
                        mm = product(ps[:G, 6 + head // per_bank, o:o + hd + 1], (pth[:, n, :], ptl[:, n, :]),
                                     (vh[l][:, head, :], vl[l][:, head, :]), True, True)
                    if i == ng - 1:
                        mm.then_inc(a["pv"], 1)

                def turn_context(g):
                    pe.wait_ge(a["ctx"], g + 1)
                    if not isinstance(g, int) or g < NT - 1:
                        pe.wait_ge(a["ve"], g + 2)
                    for j in range(6):
                        mm = nc.tensor.transpose(ps[:, 4 + j // 3, (j % 3) * G:(j % 3 + 1) * G],
                                                 ctx[:, j * 128:(j + 1) * 128], ident[:G, :G])
                        if j % 3 == 2:
                            mm.then_inc(a["ctp"], 1)

                def project_out(g):
                    for j in range(6):
                        if j == 0:
                            pe.wait_ge(a["cte"], 2 * g + 2)
                        mm = nc.tensor.matmul(ps[:G, 6, 0:D], ctxT[:, j, :], wo[:, j, :], start=j == 0, stop=j == 5)
                    mm.then_inc(a["op"], 1)

                def body(g, more, first=False):
                    for i in range(ng):
                        scores(g, i)
                    before = l == 1 and not first
                    if before:
                        turn_context(g - 1)
                    if more:
                        for q in range(2):
                            if before:
                                pe.wait_ge(a["cte"], 2 * g - 1 + q)
                            project_qk(g + 1, q)
                    if before:
                        project_out(g - 1)
                    if more and l == 0:
                        project_v(g + 1)
                    for i in range(ng):
                        turn_probs(g, i)
                        if more and l == 1:
                            project_qk(g + 1, 2 + i)
                    for i in range(ng):
                        mix(g, i)
                        if more and l == 1 and i == 0:
                            project_v(g + 1)

                for q in range(sets):
                    project_qk(0, q)
                project_v(0)
                body(0, True, True)
                with pe.Fori(1, NT - 1) as g:
                    body(g, True)
                body(NT - 1, False)
                if l == 1:
                    turn_context(NT - 1)
                    project_out(NT - 1)
                pe.wait_ge(a["out"], NT)

            def experts(l):
                m, b = M[l], B[l]
                E = EXPERTS[l]
                pe.wait_ge(s_gate_split, 2)
                for t in range(NT):
                    for c in range(2):
                        mm = product(ps[:G, 6, t * E:(t + 1) * E],
                                     [x[:KD, c, t * G:(t + 1) * G] for x in (xh, xl)],
                                     (gh[l][:, c, :], gl[l][:, c, :]), c == 0, c == 1)
                mm.then_inc(m["lgp"], 1)

                def count_choices():
                    pe.wait_ge(m["oh"], 1)
                    nc.tensor.matmul(ps[:G, 4, 0:NT * E], cst[:G, C_UPPER:C_UPPER + G],
                                     oh[:, 2, :, 0:E], start=True, stop=True)
                    nc.tensor.matmul(ps[:, 5, 0:NT * E], ones[:G, :], oh[:, 2, :, 0:E],
                                     start=True, stop=True).then_inc(m["cnt"], 1)

                def shared_expert(e, extra=None):
                    n, ny = 3 * HC * e, NT * e
                    pe.wait_ge(s_wd, 16 * (e + 1))
                    for gi, tiles in enumerate(GROUPS):
                        lo, w = tiles[0] * G, len(tiles) * G
                        for q in range(HC):
                            if n % (3 * HC) >= 2:
                                pe.wait_ge(m["mul"], n - 1)
                            for u in range(2):
                                for c in range(2):
                                    mm = product(ps[:, 2 * (n % 2) + u, 0:w],
                                                 [m_[:, 2 * c + u, q * 128:(q + 1) * 128] for m_ in (wah[0], wal[0])],
                                                 [x[:KD, c, lo:lo + w] for x in (xh, xl)], c == 0, c == 1)
                            mm.then_inc(m["gup"], 1)
                            n += 1
                            if extra and n == 2:
                                extra()
                        pe.wait_ge(m["mul"], n)
                        if extra and gi == 0:
                            pe.wait_ge(m["idx"], 1)
                        for j, t in enumerate(tiles):
                            if ny % NT >= 4:
                                pe.wait_ge(m["dne"], ny - 3)
                            for q in range(HC):
                                mm = nc.tensor.matmul(ps[:G, 4 + ny % 4, 0:D], hsh[:, q, j * G:(j + 1) * G],
                                                      wd[:, 0, q, :], start=q == 0, stop=q == HC - 1)
                            mm.then_inc(m["dnp"], 1)
                            ny += 1
                    pe.wait_ge(m["dne"], ny)
                if l == 0:
                    pe.wait_ge(s_shared_split, 4)
                    shared_expert(0, count_choices)
                else:
                    count_choices()
                    pe.wait_ge(m["idx"], 1)
                pairs = blocks_of(pe)

                def turn_x(n, s, k):
                    pe.wait_ge(xg_in[l][s], 16 * (k + 1))
                    wait_from(pe, b["te"], n - 1)
                    for c in range(2):
                        for j in range(2):
                            mm = nc.tensor.transpose(ps[:KD, 4 + s, c * BLOCK + j * BT:c * BLOCK + (j + 1) * BT],
                                                     xg[:, s, j, c * KD:(c + 1) * KD], ident[:BT, :BT])
                    mm.then_inc(b["tp"], 1)

                def gate_up(n, s, k):
                    pe.wait_ge(b["wl"], 4 * (n + 1))
                    pe.wait_ge(b["te"], n + 1)
                    for third in range(3):
                        pair = (s + third) % 2
                        wait_from(pe, b["hm"], 3 * n + third - 1)
                        for u in range(2):
                            for i in range(2):
                                q = 2 * third + i
                                for c in range(2):
                                    mm = product(ps[:, 2 * pair + u, i * BLOCK:(i + 1) * BLOCK],
                                                 [w[:, 2 * c + u, q * 128:(q + 1) * 128] for w in (wah[s], wal[s])],
                                                 (xgh[:, s, c, :], xgl[:, s, c, :]), c == 0, c == 1)
                        mm.then_inc(b["gu"], 1)

                def down_y(n, s, k):
                    pe.wait_ge(wd_in[l][s], 16 * (k + 1))
                    pe.wait_ge(b["hm"], 3 * (n + 1))
                    wait_from(pe, b["ye"], n - 1)
                    for j in range(2):
                        for q in range(HC):
                            mm = nc.tensor.matmul(ps[:BT, 6 + s, j * D:(j + 1) * D], hb[:, s, q, j * BT:(j + 1) * BT],
                                                  wd[:, s, q, :], start=q == 0, stop=q == HC - 1)
                    mm.then_inc(b["dn"], 1)

                def step(n, s, k, more):
                    if more:
                        turn_x(n + 1, 1 - s, k + s)
                    gate_up(n, s, k)
                    if not isinstance(n, int) or n >= 1:
                        down_y(n - 1, 1 - s, k - 1 + s)
                turn_x(0, 0, 0)
                over_blocks(pairs, step)(pe)
                down_y(2 * pairs[1] - 1, 1, pairs[1] - 1)
                pe.wait_ge(b["ye"], 2 * pairs[1])
                if l == 0:
                    pe.wait_ge(b["wl"], 4 * (2 * pairs[1] + 1))
                    shared_expert(1)

            for l in range(2):
                turn(2 * l)
                attention(l)
                turn(2 * l + 1)
                experts(l)

        @block.scalar
        def _(act):
            act.wait_ge(s_gamma, 16)
            for c in range(TAP_CHUNKS):
                if c % 2 == 0:
                    act.wait_ge(s_w5[c // 2], 16)
                nc.scalar.activation(weff[:, c, 0:D], w5_sb[:, c, 0, :], ACT.Copy, scale=g5_sb[:, c, 0:1]
                                     ).then_inc(s_fold, 1)

            def take_tile(t, s, k):
                act.wait_ge(t_mm[s], k + 1)
                nc.scalar.copy(h[:, bass.ds(t, 1), :].rearrange("p a n -> p (a n)"), ps[:G, s, 0:D])
                nc.scalar.copy(tst[:, bass.ds(t, 1), :].rearrange("p a n -> p (a n)"), ps[:G, s, D:D + 2]
                               ).then_inc(t_h[s], 1)

            def square(t, s, k):
                act.wait_ge(t_in[s], 16 * (k + 1))
                act.wait_ge(t_red[s], k)
                nc.scalar.activation(xsq[:, s, :, :], xc[:, s, :, :], ACT.Square).then_inc(t_sq[s], 1)
                take_tile(t, s, k)
            alternating(act, 0, NT, square)

            def root(n):
                act.wait_ge(s_var, n)
                nc.scalar.activation(rstd[:, :], rinv[:, :], ACT.Sqrt).then_inc(s_root, 1)
            root(1)

            def evacuate_turned(i):
                for t in range(NT):
                    act.wait_ge(n_tp, NT * i + t + 1)
                    nc.scalar.mul(xh[:KD, :, t * G:(t + 1) * G],
                                  ps[:KD, t % 4, 0:2 * G].rearrange("p (c t) -> p c t", c=2), X_SCALE
                                  ).then_inc(n_xh, 1)

            def split_piece(l, n, s, p, used):
                act.wait_ge(w_in[l][p], 16 * (n + 1))
                used()
                nc.scalar.mul(wah[s][:, p, :], wraw[:, p, :], W_SCALE).then_inc(B[l]["wh"], 1)

            def attention(l):
                a, sets, ng = A[l], 2 * (l + 1), GROUPS_OF[l]

                def take_qk(g, q):
                    if q == 0:
                        wait_from(act, a["score"], ng * g)
                    act.wait_ge(a["qkp"], sets * g + q + 1)
                    if l == 0 and q == 1:
                        for j in range(4):
                            rows = slice(32 * j, 32 * j + 32)
                            op = nc.scalar.mul(kdh[rows, :, j, :], ps[rows, 5, 0:3 * G].rearrange("p (c t) -> p c t", c=3),
                                               XW * QKV_SCALE)
                    else:
                        op = nc.scalar.mul(qkh[:, q, :], ps[:, 4 + q % 2, 0:3 * G], XW * QKV_SCALE)
                    op.then_inc(a["qkh"], 1)

                def take_v(g):
                    act.wait_ge(a["vp"], g + 1)
                    wait_from(act, a["pv"], g)
                    w = HEADS // (l + 1)
                    for b in range(l + 1):
                        op = nc.scalar.mul(vh[l][:, b * w:(b + 1) * w, 0:HD[l]],
                                           ps[:G, 4 + b, 0:w * HD[l]].rearrange("p (h d) -> p h d", h=w),
                                           XW * QKV_SCALE)
                    op.then_inc(a["vh"], 1)

                def take_context(g):
                    for i in range(2):
                        act.wait_ge(a["ctp"], 2 * g + 1 + i)
                        nc.scalar.copy(ctxT[:, 3 * i:3 * i + 3, :].rearrange("p j t -> p (j t)"),
                                       ps[:, 4 + i, 0:3 * G]).then_inc(a["cte"], 1)

                def exponentials(g, i):
                    act.wait_ge(a["sub"], ng * g + 1 + i)
                    part = in_group(l, i, prob)
                    nc.scalar.activation(part, part, ACT.Exp, scale=float(HD[l]) ** -0.5 / QKV_SCALE ** 2
                                         ).then_inc(a["exp"], 1)

                def take_probs(g, i):
                    if i == 0:
                        wait_from(act, a["pv"], g)
                    act.wait_ge(a["ptp"], ng * g + 1 + i)
                    nc.scalar.mul(in_group(l, i, pth), in_banks(l, i), P_SCALE).then_inc(a["pth"], 1)

                def body(g, more, first=False):
                    if l == 1 and not first:
                        take_context(g - 1)
                    for i in range(ng):
                        exponentials(g, i)
                        if more and i <= l:
                            take_qk(g + 1, i)
                    for i in range(ng):
                        take_probs(g, i)
                        if more and (l == 1 or i == ng - 1):
                            take_qk(g + 1, 2 + i if l else 1)
                    if more:
                        take_v(g + 1)

                act.wait_ge(s_setup, 1)
                act.wait_ge(s_const_set, 9)
                for q in range(sets):
                    take_qk(0, q)
                take_v(0)
                body(0, True, True)
                with act.Fori(1, NT - 1) as g:
                    body(g, True)
                body(NT - 1, False)
                if l == 1:
                    take_context(NT - 1)

            def experts(l):
                m, b = M[l], B[l]
                E = EXPERTS[l]
                act.wait_ge(m["ex"], 1)
                nc.scalar.activation(tmp[:, 0, :, 0:E], tmp[:, 0, :, 0:E], ACT.Exp).then_inc(m["exr"], 1)
                nc.scalar.activation(pw[:, 1, :], pw[:, 1, :], ACT.Exp).then_inc(m["exr"], 1)
                def shared_expert(e):
                    n = 3 * HC * e
                    for tiles in GROUPS:
                        w = len(tiles) * G
                        for q in range(HC):
                            act.wait_ge(m["gup"], n + 1)
                            if n % (3 * HC) >= 2:
                                act.wait_ge(m["mul"], n - 1)
                            nc.scalar.activation(silu[:, n % 2, 0:w], ps[:, 2 * (n % 2), 0:w], ACT.Silu, scale=XW
                                                 ).then_inc(m["silu"], 1)
                            n += 1
                if l == 0:
                    shared_expert(0)
                act.wait_ge(m["idx"], 1)
                pairs = blocks_of(act)

                def free(n):
                    if isinstance(n, int) and n < 2:
                        if l == 0 and n == 0:
                            act.wait_ge(m["gup"], 3 * HC)
                    else:
                        act.wait_ge(b["gu"], 3 * (n - 1))

                def take_x(n, s):
                    act.wait_ge(b["tp"], n + 1)
                    free(n)
                    nc.scalar.mul(xgh[:, s, :, :].rearrange("p c t -> p (c t)"), ps[:KD, 4 + s, 0:2 * BLOCK], X_SCALE
                                  ).then_inc(b["teh"], 1)

                def swish(n, s, third):
                    pair = (s + third) % 2
                    act.wait_ge(b["gu"], 3 * n + third + 1)
                    wait_from(act, b["hm"], 3 * n + third - 1)
                    nc.scalar.activation(silu[:, pair, 0:2 * BLOCK], ps[:, 2 * pair, 0:2 * BLOCK], ACT.Silu, scale=XW
                                         ).then_inc(b["sl"], 1)

                def take_y(n, s, k):
                    act.wait_ge(b["dn"], n + 1)
                    wait_from(act, y_out[l][s], 16 * k)
                    nc.scalar.copy(ysb[:, s, :, :].rearrange("p j n -> p (j n)"), ps[:BT, 6 + s, 0:2 * D]
                                   ).then_inc(b["ye"], 1)

                def step(n, s, k, more):
                    if more:
                        take_x(n + 1, 1 - s)
                    for i in range(4):
                        if more or l == 0:
                            split_piece(l, n + 1, 1 - s, i, lambda: free(n + 1))
                        if i < 3:
                            swish(n, s, i)
                    if not isinstance(n, int) or n >= 1:
                        take_y(n - 1, 1 - s, k - 1 + s)
                for p in range(4):
                    split_piece(l, 0, 0, p, lambda: free(0))
                take_x(0, 0)
                over_blocks(pairs, step)(act)
                take_y(2 * pairs[1] - 1, 1, pairs[1] - 1)
                if l == 0:
                    act.wait_ge(b["hm"], 6 * pairs[1])
                    shared_expert(1)

            for l in range(2):
                root(2 * l + 2)
                evacuate_turned(2 * l)
                attention(l)
                root(2 * l + 3)
                evacuate_turned(2 * l + 1)
                experts(l)

        @block.vector
        def _(dve):
            count = [0]

            def link(op, before=None):
                op.then_inc(dve_own, 1)
                if before is None:
                    count[0] += 1
                    dve.wait_ge(dve_own, count[0])
                else:
                    dve.wait_ge(dve_own, before + 1)

            dve.wait_ge(s_gamma, 16)
            for c in range(0, TAP_CHUNKS, 2):
                dve.wait_ge(s_w5[c // 2], 16)
                dve.wait_ge(s_fold, c + 2)
                for g in range(1, 5):
                    for cc in (c, c + 1):
                        op = nc.vector.scalar_tensor_tensor(out=weff[:, cc, 0:D], in0=w5_sb[:, cc, g, :],
                                                            scalar=g5_sb[:, cc, g:g + 1], in1=weff[:, cc, 0:D],
                                                            op0=ALU.mult, op1=ALU.add)
                    link(op)
            dve.wait_ge(s_const, 16)
            nc.vector.tensor_copy(weff[:, :, D:D + 1],
                                  cst[:TP, C_COUNT:C_COUNT + 1].unsqueeze(2).to_broadcast([TP, TAP_CHUNKS, 1])
                                  ).then_inc(s_weff, 1)
            nc.vector.tensor_copy(identb[:, :], cst[:G, C_IDENT:C_IDENT + G])
            nc.vector.tensor_copy(maskb[:, :], cst[:G, C_MASK:C_MASK + 4 * G]).then_inc(s_setup, 1)
            dve.wait_ge(s_const_ps, 1)
            dve.wait_ge(s_tokb, 16)
            nc.vector.tensor_tensor(crow[:, :], ps[:1, 5, 0:D], tokb_sb[:, :], ALU.add).then_inc(s_crow, 1)

            def tile(t, s, k):
                dve.wait_ge(t_sq[s], k + 1)
                dve.wait_ge(t_mm[s], k)
                nc.vector.tensor_reduce(xss[:, s, :], xsq[:, s, :, :].rearrange("p c t -> p t c"), AX.X, ALU.add
                                        ).then_inc(t_red[s], 1)
            alternating(dve, 0, NT, tile)

            def inverse_root(n):
                link(nc.vector.reciprocal(rinv[:, :], var[:, :]))
                dve.sem_inc(s_var, 1)
                dve.wait_ge(s_root, n)
                link(nc.vector.tensor_tensor(rinv[:, :], rstd[:, :], rstd[:, :], ALU.mult))
                link(nc.vector.tensor_tensor(rinv[:, :], rinv[:, :], var[:, :], ALU.mult))
                link(nc.vector.tensor_scalar(rinv[:, :], rinv[:, :], -0.5, 1.5, ALU.mult, ALU.add))
                link(nc.vector.tensor_tensor(rstd[:, :], rstd[:, :], rinv[:, :], ALU.mult))

            dve.wait_ge(s_crep, 1)
            nc.vector.tensor_copy(cs_sb[:, 0, :], ps[:G, 4, 0:D])
            link(nc.vector.tensor_copy(cs_sb[:, 1, :], ps[:G, 6, 0:D]))

            for s in range(2):
                dve.wait_ge(t_h[s], (NT + 1 - s) // 2)
            link(nc.vector.tensor_scalar(tst[:, :, :], tst[:, :, :], 1.0 / FEATURES, None, ALU.mult))
            link(nc.vector.tensor_tensor(var[:, :], tst[:, :, 0], tst[:, :, 0], ALU.mult))
            link(nc.vector.tensor_tensor(var[:, :], tst[:, :, 1], var[:, :], ALU.subtract))
            link(nc.vector.tensor_scalar(var[:, :], var[:, :], TOK_EPS, None, ALU.add))
            inverse_root(1)
            link(nc.vector.scalar_tensor_tensor(out=shift[:, :], in0=tst[:, :, 0], scalar=-1.0, in1=rstd[:, :],
                                                op0=ALU.mult, op1=ALU.mult))
            for t in range(NT):
                op = nc.vector.scalar_tensor_tensor(out=h[:, t, :], in0=h[:, t, :], scalar=rstd[:, t:t + 1],
                                                    in1=cs_sb[:, 1, :], op0=ALU.mult, op1=ALU.add)
            link(op)
            for t in range(NT):
                op = nc.vector.scalar_tensor_tensor(out=h[:, t, :], in0=cs_sb[:, 0, :], scalar=shift[:, t:t + 1],
                                                    in1=h[:, t, :], op0=ALU.mult, op1=ALU.add)
            link(op)

            def split_piece(l, n, s, p):
                dve.wait_ge(B[l]["wh"], 4 * n + p + 1)
                nc.vector.scalar_tensor_tensor(out=wal[s][:, p, :], in0=wraw[:, p, :], scalar=W_SCALE,
                                               in1=wah[s][:, p, :], op0=ALU.mult, op1=ALU.subtract
                                               ).then_inc(B[l]["wl"], 1)

            def normalise(i):
                for t in range(NT):
                    op = nc.vector.bn_stats(st6[:, t, :], h[:, t, :])
                link(op)
                for t in range(NT):
                    op = nc.vector.bn_aggr(mv[:, t, :], st6[:, t, :])
                link(op)
                link(nc.vector.tensor_scalar(var[:, :], mv[:, :, 1], LN_EPS, None, ALU.add))
                inverse_root(i + 2)
                for t in range(NT):
                    nc.vector.tensor_scalar(xn[:, t, :], h[:, t, :], mv[:, t, 0:1], rstd[:, t:t + 1],
                                            ALU.subtract, ALU.mult).then_inc(n_xn, 1)
                for t in range(NT):
                    dve.wait_ge(n_xh, NT * i + t + 1)
                    nc.vector.scalar_tensor_tensor(
                        out=xl[:KD, :, t * G:(t + 1) * G],
                        in0=ps[:KD, t % 4, 0:2 * G].rearrange("p (c t) -> p c t", c=2), scalar=X_SCALE,
                        in1=xh[:KD, :, t * G:(t + 1) * G], op0=ALU.mult, op1=ALU.subtract).then_inc(n_xt, 1)
                if i == 2:
                    dve.wait_ge(s_wo, 32)
                    link(nc.vector.tensor_tensor(h[:, :, :], h[:, :, :],
                                                 bo[:, :].unsqueeze(1).to_broadcast([G, NT, D]), ALU.add))

            def attention(l):
                a, hd, sets, ng = A[l], HD[l], 2 * (l + 1), GROUPS_OF[l]
                dve.wait_ge(s_setup, 1)
                dve.wait_ge(s_const_set, 9)

                def take_qk(g, q):
                    dve.wait_ge(a["qkh"], sets * g + q + 1)
                    if l == 0 and q == 1:
                        for j in range(4):
                            rows = slice(32 * j, 32 * j + 32)
                            op = nc.vector.scalar_tensor_tensor(
                                out=kdl[rows, :, j, :], in0=ps[rows, 5, 0:3 * G].rearrange("p (c t) -> p c t", c=3),
                                scalar=XW * QKV_SCALE, in1=kdh[rows, :, j, :], op0=ALU.mult, op1=ALU.subtract)
                    else:
                        op = nc.vector.scalar_tensor_tensor(out=qkl[:, q, :], in0=ps[:, 4 + q % 2, 0:3 * G],
                                                            scalar=XW * QKV_SCALE, in1=qkh[:, q, :], op0=ALU.mult,
                                                            op1=ALU.subtract)
                    op.then_inc(a["qkl"], 1)

                def take_v(g):
                    dve.wait_ge(a["vh"], g + 1)
                    w = HEADS // (l + 1)
                    for b in range(l + 1):
                        op = nc.vector.scalar_tensor_tensor(
                            out=vl[l][:, b * w:(b + 1) * w, 0:hd],
                            in0=ps[:G, 4 + b, 0:w * hd].rearrange("p (h d) -> p h d", h=w),
                            scalar=XW * QKV_SCALE, in1=vh[l][:, b * w:(b + 1) * w, 0:hd], op0=ALU.mult,
                            op1=ALU.subtract)
                    op.then_inc(a["ve"], 1)

                own_n = ng + 1
                first_own = count[0]

                def row(g):
                    return h[:, bass.ds(g, 1), :].rearrange("p a n -> p (a n)")

                def take_out(g):
                    dve.wait_ge(a["op"], g + 1)
                    nc.vector.tensor_tensor(row(g), ps[:G, 6, 0:D], row(g), ALU.add).then_inc(a["out"], 1)

                def body(g, more, first=False):
                    own = first_own + own_n * g
                    for i in range(ng):
                        scores = in_banks(l, i).rearrange("p b (j t) -> p b j t", t=G)
                        part = slice(IN_GROUP[l] * i, IN_GROUP[l] * (i + 1))
                        maxima = mx[:, part].rearrange("p (b j) -> p b j", b=l + 1)
                        dve.wait_ge(a["score"], ng * g + 1 + i)
                        link(nc.vector.tensor_reduce(maxima, scores, AX.X, ALU.max), own + i)
                        nc.vector.tensor_tensor(prob[:, part, :].rearrange("p (b j) t -> p b j t", b=l + 1), scores,
                                                maxima.unsqueeze(3).to_broadcast([G, l + 1, IN_BANK[l], G]),
                                                ALU.subtract).then_inc(a["sub"], 1)
                        if more and i <= l:
                            take_qk(g + 1, i)
                    if l == 1 and not first:
                        take_out(g - 1)
                    for i in range(ng):
                        dve.wait_ge(a["pth"], ng * g + 1 + i)
                        nc.vector.scalar_tensor_tensor(out=in_group(l, i, ptl), in0=in_banks(l, i), scalar=P_SCALE,
                                                       in1=in_group(l, i, pth), op0=ALU.mult, op1=ALU.subtract
                                                       ).then_inc(a["ptl"], 1)
                        if more and (l == 1 or i == ng - 1):
                            take_qk(g + 1, 2 + i if l else 1)
                    dve.wait_ge(a["pv"], g + 1)
                    nb = l + 1
                    got = ps[:G, 6:6 + nb, 0:HEADS // nb * (hd + 1)].rearrange("p b (h d) -> p b h d", d=hd + 1)
                    rv = rs[:, :].rearrange("p (b h) -> p b h", b=nb)
                    link(nc.vector.reciprocal(rv, got[:, :, :, hd]), own + ng)
                    cv = ctx[:, 0:INNER[l]].rearrange("p (b h d) -> p b h d", b=nb, d=hd)
                    nc.vector.tensor_tensor(cv, got[:, :, :, 0:hd],
                                            rv.unsqueeze(3).to_broadcast([G, nb, HEADS // nb, hd]), ALU.mult
                                            ).then_inc(a["ctx"], 1)
                    if l == 0:
                        dve.wait_ge(a["ctx"], g + 1)
                        nc.vector.tensor_tensor(row(g), row(g), ctx[:, 0:D], ALU.add).then_inc(a["out"], 1)
                    if more:
                        take_v(g + 1)

                for q in range(sets):
                    take_qk(0, q)
                take_v(0)
                body(0, True, True)
                with dve.Fori(1, NT - 1) as g:
                    body(g, True)
                body(NT - 1, False)
                if l == 1:
                    take_out(NT - 1)
                count[0] = first_own + own_n * NT
                dve.wait_ge(a["out"], NT)

            def choose(l):
                m, E = M[l], EXPERTS[l]
                iota_e = cst[:, C_IOTA_E:C_IOTA_E + E]
                dve.wait_ge(m["lgp"], 1)
                link(nc.vector.tensor_scalar(lg[:, :, 0:E], ps[:G, 6, 0:NT * E].rearrange("p (t e) -> p t e", e=E),
                                             XW, None, ALU.mult))
                for t in range(NT):
                    op = nc.vector.max(m8[:, t, :], lg[:, t, 0:E])
                link(op)
                nc.vector.tensor_tensor(tmp[:, 0, :, 0:E], lg[:, :, 0:E],
                                        m8[:, :, 0:1].to_broadcast([G, NT, E]), ALU.subtract)
                nc.vector.tensor_tensor(pw[:, 1, :], m8[:, :, 1], m8[:, :, 0], ALU.subtract).then_inc(m["ex"], 1)
                for t in range(NT):
                    op = nc.vector.max_index(i8[:, t, :], m8[:, t, :], lg[:, t, 0:E])
                link(op)
                for k in range(2):
                    op = nc.vector.tensor_tensor(idxf[:, k, :], i8[:, :, k], cst[:G, C_INVALID:C_INVALID + NT], ALU.add)
                link(op)
                for k in range(2):
                    op = nc.vector.tensor_tensor(oh[:, k, :, 0:E], iota_e[:G, :].unsqueeze(1).to_broadcast([G, NT, E]),
                                                 idxf[:, k, :].unsqueeze(2).to_broadcast([G, NT, E]), ALU.is_equal)
                link(op)
                nc.vector.tensor_tensor(oh[:, 2, :, 0:E], oh[:, 0, :, 0:E], oh[:, 1, :, 0:E], ALU.add
                                        ).then_inc(m["oh"], 1)

            def add_up(l):
                m, E = M[l], EXPERTS[l]
                dve.wait_ge(m["cnt"], 1)
                nc.vector.tensor_copy(tot[:, :, 0:E], ps[:, 5, 0:NT * E].rearrange("p (t e) -> p t e", e=E))
                link(nc.vector.memset(cum[:, 0, :], 0.0))
                for t in range(NT):
                    link(nc.vector.tensor_tensor(cum[:, t + 1, 0:E], cum[:, t, 0:E], tot[:, t, 0:E], ALU.add))

            def place_experts(l):
                E = EXPERTS[l]
                link(nc.vector.tensor_tensor(cmp9[:, 0:E, :], cum[:, NT, 0:E].unsqueeze(2).to_broadcast([128, E, N_THRESH]),
                                             cst[:, C_THRESH:C_THRESH + N_THRESH].unsqueeze(1).to_broadcast(
                                                 [128, E, N_THRESH]), ALU.is_gt))
                link(nc.vector.tensor_reduce(nblk[:, 0:E], cmp9[:, 0:E, :], AX.X, ALU.add))
                link(nc.vector.tensor_copy(oend[:, 0:1], nblk[:, 0:1]))
                for e in range(1, E):
                    link(nc.vector.tensor_tensor(oend[:, e:e + 1], oend[:, e - 1:e], nblk[:, e:e + 1], ALU.add))
                link(nc.vector.tensor_tensor(obeg[:, 0:E], oend[:, 0:E], nblk[:, 0:E], ALU.subtract))

            def place_tokens(l):
                m, E, NB = M[l], EXPERTS[l], BLOCKS[l]
                link(nc.vector.tensor_tensor(cmpb[:, 0:NB, 0:E],
                                             cst[:, C_IOTA_B:C_IOTA_B + NB].unsqueeze(2).to_broadcast([128, NB, E]),
                                             oend[:, 0:E].unsqueeze(1).to_broadcast([128, NB, E]), ALU.is_ge))
                link(nc.vector.tensor_reduce(eb[:, 0:NB], cmpb[:, 0:NB, 0:E], AX.X, ALU.add))
                link(nc.vector.tensor_scalar(eb[:, 0:NB], eb[:, 0:NB], float(E - 1), None, ALU.min))
                nc.vector.tensor_copy(ebi[:, 0:NB], eb[0:1, 0:NB])
                link(nc.vector.tensor_scalar(nit[:, 2:NB // 2], cst[0:1, C_IOTA_B + 2:C_IOTA_B + NB // 2], 2.0,
                                             oend[0:1, E - 1:E], ALU.mult, ALU.is_lt))
                link(nc.vector.tensor_reduce(nit[:, 0:1], nit[:, 2:NB // 2], AX.X, ALU.add))
                nc.vector.tensor_copy(niti[:, :], nit[:, 0:1])
                link(nc.vector.tensor_tensor(base[:, :, 0:E], ps[:G, 4, 0:NT * E].rearrange("p (t e) -> p t e", e=E),
                                             cum[:G, 0:NT, 0:E], ALU.add))
                link(nc.vector.scalar_tensor_tensor(out=base[:, :, 0:E],
                                                    in0=obeg[:G, 0:E].unsqueeze(1).to_broadcast([G, NT, E]),
                                                    scalar=float(BLOCK), in1=base[:, :, 0:E],
                                                    op0=ALU.mult, op1=ALU.add))
                dve.wait_ge(m["exr"], 2)
                if l == 0:
                    link(nc.vector.tensor_reduce(zsum[:, :], tmp[:, 0, :, 0:E], AX.X, ALU.add))
                for k in range(2):
                    op = nc.vector.tensor_tensor(oh[:, k, :, 0:E], oh[:, k, :, 0:E], base[:, :, 0:E], ALU.mult)
                link(op)
                link(nc.vector.tensor_reduce(slotf[:, :, :], oh[:, 0:2, :, 0:E], AX.X, ALU.add))
                nc.vector.tensor_copy(slot_i[:, :, :], slotf[:, :, :]).then_inc(m["idx"], 1)

            def weigh(l):
                if l == 0:
                    link(nc.vector.reciprocal(pw[:, 0, :], zsum[:, :]))
                    link(nc.vector.tensor_tensor(pw[:, 1, :], pw[:, 1, :], pw[:, 0, :], ALU.mult))
                    link(nc.vector.scalar_tensor_tensor(out=zsum[:, :], in0=pw[:, 0, :], scalar=1e-8, in1=pw[:, 1, :],
                                                        op0=ALU.add, op1=ALU.add))
                else:
                    nc.vector.memset(pw[:, 0, :], 1.0)
                    link(nc.vector.tensor_scalar(zsum[:, :], pw[:, 1, :], 1.0, None, ALU.add))
                link(nc.vector.reciprocal(zsum[:, :], zsum[:, :]))
                link(nc.vector.tensor_tensor(cw[:, :, :], pw[:, :, :], zsum[:, :].unsqueeze(1).to_broadcast([G, 2, NT]),
                                             ALU.mult))

            def experts(l):
                m, b = M[l], B[l]
                stages = [add_up, place_experts, place_tokens, weigh]

                def shared_expert(e):
                    n, ny = 3 * HC * e, NT * e
                    for gi, tiles in enumerate(GROUPS):
                        w = len(tiles) * G
                        for q in range(HC):
                            dve.wait_ge(m["silu"], n + 1)
                            if q == 0 and gi:
                                dve.wait_ge(m["dnp"], ny)
                            nc.vector.scalar_tensor_tensor(out=hsh[:, q, 0:w], in0=ps[:, 2 * (n % 2) + 1, 0:w],
                                                           scalar=XW, in1=silu[:, n % 2, 0:w], op0=ALU.mult,
                                                           op1=ALU.mult).then_inc(m["mul"], 1)
                            n += 1
                            if 1 <= n <= len(stages):
                                stages[n - 1](l)
                        if e == 0 and gi == len(GROUPS) - 1:
                            for p in range(4):
                                split_piece(l, 0, 0, p)
                        for t in tiles:
                            dve.wait_ge(m["dnp"], ny + 1)
                            nc.vector.scalar_tensor_tensor(out=h[:, t, :], in0=ps[:G, 4 + ny % 4, 0:D], scalar=0.5,
                                                           in1=h[:, t, :], op0=ALU.mult, op1=ALU.add
                                                           ).then_inc(m["dne"], 1)
                            ny += 1
                        if e:
                            dve.wait_ge(m["dne"], ny)
                            combine(tiles)

                def combine(tiles):
                    for t in tiles:
                        for k in range(2):
                            dve.wait_ge(g_y[l][k], 16 * (t + 1))
                            op = nc.vector.scalar_tensor_tensor(out=h[:, t, :], in0=yg[:, k, t, :],
                                                                scalar=cw[:, k, t:t + 1], in1=h[:, t, :],
                                                                op0=ALU.mult, op1=ALU.add)
                            if k == 0:
                                link(op)
                            else:
                                op.then_inc(m["comb"], 1)
                choose(l)
                if l == 0:
                    shared_expert(0)
                    dve.wait_ge(m["dne"], NT)
                else:
                    for stage in stages:
                        stage(l)
                dve.wait_ge(m["idx"], 1)
                pairs = blocks_of(dve)

                def take_x(n, s):
                    dve.wait_ge(b["teh"], n + 1)
                    nc.vector.scalar_tensor_tensor(out=xgl[:, s, :, :].rearrange("p c t -> p (c t)"),
                                                   in0=ps[:KD, 4 + s, 0:2 * BLOCK], scalar=X_SCALE,
                                                   in1=xgh[:, s, :, :].rearrange("p c t -> p (c t)"),
                                                   op0=ALU.mult, op1=ALU.subtract).then_inc(b["te"], 1)

                def multiply(n, s, third):
                    pair = (s + third) % 2
                    dve.wait_ge(b["sl"], 3 * n + third + 1)
                    wait_from(dve, b["dn"], n - 1)
                    nc.vector.scalar_tensor_tensor(
                        out=hb[:, s, 2 * third:2 * third + 2, :].rearrange("p q t -> p (q t)"),
                        in0=ps[:, 2 * pair + 1, 0:2 * BLOCK], scalar=XW, in1=silu[:, pair, 0:2 * BLOCK],
                        op0=ALU.mult, op1=ALU.mult).then_inc(b["hm"], 1)

                def step(n, s, k, more):
                    if more:
                        take_x(n + 1, 1 - s)
                    for i in range(4):
                        if more or l == 0:
                            split_piece(l, n + 1, 1 - s, i)
                        if i < 3:
                            multiply(n, s, i)
                if l == 1:
                    for p in range(4):
                        split_piece(l, 0, 0, p)
                take_x(0, 0)
                over_blocks(pairs, step)(dve)

                if l == 0:
                    dve.wait_ge(b["hm"], 6 * pairs[1])
                    shared_expert(1)
                else:
                    combine(range(NT))
                dve.wait_ge(m["comb"], NT)

            for l in range(2):
                normalise(2 * l)
                attention(l)
                normalise(2 * l + 1)
                experts(l)


def kernel(**inputs):
    import numpy as _np
    import concourse.bacc as _bacc
    from concourse import mybir as _mybir
    from concourse.bass_utils import run_bass_kernel_spmd as _run

    a = {k: _np.asarray(v) for k, v in inputs.items()}

    def parts(w):
        return w.reshape(2, KD, -1).transpose(1, 0, 2)

    x = _np.zeros((NT * PER, IMG + 2, IMG + 2, CH), a["x"].dtype)
    x[:BATCH, 1:-1, 1:-1] = a["x"]
    xcol = _np.zeros((NT, TP, TAP_CHUNKS, PER, SIDE, SIDE), x.dtype)
    for p, row in enumerate(TAPS):
        for c, tap in enumerate(row):
            if tap is not None:
                ty, tx, ch = tap
                seen = x[:, ty + 1:ty + 2 + PATCH * (SIDE - 1):PATCH, tx + 1:tx + 2 + PATCH * (SIDE - 1):PATCH, ch]
                xcol[:, p, c] = seen.reshape(NT, PER, SIDE, SIDE)
    xcol = xcol.reshape(NT, TP, TAP_CHUNKS, G)
    moves = ((0, 0), (0, 1), (0, -1), (1, 0), (-1, 0))
    w = a["L0_tok_W"].reshape(PATCH, PATCH, 5, CH, D)
    ga = a["L0_tok_gamma"].reshape(PATCH, PATCH, 5, CH)
    be = a["L0_tok_beta"].reshape(PATCH, PATCH, 5, CH)
    w5 = _np.zeros((TP, TAP_CHUNKS, 5, D), w.dtype)
    g5 = _np.zeros((TP, TAP_CHUNKS, 5), ga.dtype)
    b5 = _np.zeros((TP, TAP_CHUNKS, 5), be.dtype)
    for p, row in enumerate(TAPS):
        for c, tap in enumerate(row):
            if tap is not None:
                for g, (my, mx_) in enumerate(moves):
                    y, xx = tap[0] + my, tap[1] + mx_
                    if 0 <= y < PATCH and 0 <= xx < PATCH:
                        w5[p, c, g], g5[p, c, g], b5[p, c, g] = w[y, xx, g, tap[2]], ga[y, xx, g, tap[2]], be[y, xx, g, tap[2]]

    qk0 = _np.zeros((D + 1, 2, HEADS, 32), a["L0_attn_Wq"].dtype)
    for i, n in enumerate("qk"):
        qk0[:D, i, :, :HD[0]] = a[f"L0_attn_W{n}"].T.reshape(D, HEADS, HD[0])
        qk0[D, i, :, :HD[0]] = a[f"L0_attn_b{n}"].reshape(HEADS, HD[0])
    v0 = _np.concatenate([a["L0_attn_Wv"].T, a["L0_attn_bv"][None]])
    a0 = _np.concatenate([qk0.reshape(D + 1, 768), v0], 1)
    a1 = _np.concatenate([a["L1_attn_w_q"], a["L1_attn_w_k"], a["L1_attn_w_v"]], 1)
    a1 = _np.concatenate([a1, _np.zeros((1, a1.shape[1]), a1.dtype)])

    def biased(w):
        full = _np.zeros((128, 2, w.shape[1]), w.dtype)
        full[:KD, 0], full[:KD + 1, 1] = w[:KD], w[KD:]
        return full

    def experts_in(g, u, d):
        e = g.shape[0]
        wa = _np.stack([g.reshape(e, 2, KD, HIDDEN), u.reshape(e, 2, KD, HIDDEN)], 3)
        return (wa.transpose(0, 2, 1, 3, 4).reshape(e * KD, 4, HIDDEN),
                d.reshape(e, HC, 128, D).transpose(0, 2, 1, 3).reshape(e * 128, HC * D))

    sh_wa, sh_wd = experts_in(a["L0_ffn_shared_wg"], a["L0_ffn_shared_wu"], a["L0_ffn_shared_wd"])
    e0_wa, e0_wd = experts_in(a["L0_ffn_wg"], a["L0_ffn_wu"], a["L0_ffn_wd"])
    e1_wa, e1_wd = experts_in(*(a[f"L1_ffn_W{n}"].transpose(0, 2, 1) for n in "gud"))
    arrays = {
        "const": shape_constants(), "xcol": xcol, "w5": w5, "gamma5": g5, "beta5": b5,
        "tok_b": a["L0_tok_b"].reshape(1, D),
        "a0_w": biased(a0), "a1_w": biased(a1), "a1_wo": a["L1_attn_w_o"].reshape(6, 128, D).transpose(1, 0, 2),
        "a1_bo": _np.broadcast_to(a["L1_attn_b_o"], (G, D)),
        "gate0": parts(a["L0_ffn_gate_w"].T), "gate1": parts(a["L1_ffn_router_w"].T),
        "sh_wa": sh_wa, "sh_wd": sh_wd,
        "e0_wa": e0_wa, "e0_wd": e0_wd, "e1_wa": e1_wa, "e1_wd": e1_wd,
    }
    arrays = {k: _np.ascontiguousarray(v) for k, v in arrays.items()}
    nc = _bacc.Bacc("TRN2", target_bir_lowering=False, num_devices=1)
    args = {k: nc.dram_tensor(k, v.shape, _mybir.dt.from_np(v.dtype), kind="ExternalInput").ap()
            for k, v in arrays.items()}
    out = nc.dram_tensor("out", (TOKENS, D), F32, kind="ExternalOutput").ap()
    slots = nc.dram_tensor("slots", (SLOTS, D), F32, kind="Internal").ap()
    program(nc, *args.values(), slots, out)
    r = _run(nc, [arrays], core_ids=[0])
    return r.results[0]["out"].reshape(BATCH, SEQ, D)
```

```python
import numpy as np

import concourse.bass as bass
from concourse import mybir
from concourse.alu_op_type import AluOpType as ALU

ACT = mybir.ActivationFunctionType
AX = mybir.AxisListType
F32 = mybir.dt.float32
BF16 = mybir.dt.bfloat16
F16 = mybir.dt.float16
U32 = mybir.dt.uint32

BATCH, IMG, CH, PATCH, D = 32, 96, 3, 16, 192
SIDE = IMG // PATCH
SEQ = SIDE * SIDE
TOKENS = BATCH * SEQ
FEATURES = PATCH * PATCH * 5 * CH
PER = 3
G = PER * SEQ
NT = -(-BATCH // PER)
PAD_TOKENS = NT * G
LAST = TOKENS - (NT - 1) * G
KD = 96
TAP_CHUNKS = 8
HEADS = 12
HD = (16, 64)
INNER = (HEADS * HD[0], HEADS * HD[1])
HIDDEN = 768
HC = HIDDEN // 128
EXPERTS = (16, 8)
BT = (96, 80)
BLOCK = tuple(2 * t for t in BT)
BLOCKS = tuple(-(-((2 * TOKENS + e * (b - 1)) // b) // 2) * 2 for e, b in zip(EXPERTS, BLOCK))
LN_EPS, TOK_EPS = 1e-5, 1e-3
MASKED = -(2.0 ** 100)

X_SCALE, W_SCALE = 16.0, 64.0
XW = 1 / (X_SCALE * W_SCALE)
QKV_SCALE = 16.0
P_SCALE = 4096.0
FILL_ROWS = 6 * 128
SLOTS = -(-max(n * b for n, b in zip(BLOCKS, BLOCK)) // FILL_ROWS) * FILL_ROWS


def tap_table():
    classes = {}
    for y in range(-1, PATCH + 1):
        for x in range(-1, PATCH + 1):
            n = sum(0 <= y + a < PATCH and 0 <= x + b < PATCH
                    for a, b in ((0, 0), (0, 1), (0, -1), (1, 0), (-1, 0)))
            if n:
                classes.setdefault(n, []).extend((y, x, c) for c in range(CH))
    rows, counts = [], []
    for n, taps in sorted(classes.items()):
        taps = taps + [None] * (-len(taps) % TAP_CHUNKS)
        for i in range(0, len(taps), TAP_CHUNKS):
            rows.append(taps[i:i + TAP_CHUNKS])
            counts.append(n)
    return rows, counts


TAPS, TAP_COUNTS = tap_table()
TP = len(TAPS)

C_IDENT = 0
C_UPPER = C_IDENT + 128
C_ONES = C_UPPER + G
C_IOTA_E = C_ONES + 128
C_IOTA_B = C_IOTA_E + max(EXPERTS)
C_THRESH = C_IOTA_B + max(BLOCKS)
N_THRESH = -(-TOKENS // min(BLOCK))
C_INVALID = C_THRESH + 2 * N_THRESH
C_COUNT = C_INVALID + NT
C_MASK = C_COUNT + 1
C_ALL = C_MASK + 4 * G


def shape_constants():
    c = np.zeros((128, C_ALL), np.float32)
    p = np.arange(128)
    c[:, C_IDENT:C_IDENT + 128] = np.eye(128)
    c[:, C_UPPER:C_UPPER + G] = p[:, None] < np.arange(G)[None, :]
    c[:, C_ONES:C_ONES + 128] = 1
    c[:, C_IOTA_E:C_IOTA_E + max(EXPERTS)] = np.arange(max(EXPERTS))
    c[:, C_IOTA_B:C_IOTA_B + max(BLOCKS)] = np.arange(max(BLOCKS))
    for l in range(2):
        c[:, C_THRESH + l * N_THRESH:C_THRESH + (l + 1) * N_THRESH] = BLOCK[l] * np.arange(N_THRESH)
    c[LAST:, C_INVALID + NT - 1] = 100
    c[:TP, C_COUNT] = TAP_COUNTS
    image = np.arange(G) // SEQ
    other = image[:, None] != image[None, :]
    c[:G, C_MASK:] = np.tile(np.where(other, MASKED, 0.0), (1, 4))
    return c


def program(nc, const, xcol, w5, gamma5, beta5, tok_b, a0_w, a1_w, a1_wo, a1_bo, gate0, gate1,
            sh_wa, sh_wd, e0_wa, e0_wd, e1_wa, e1_wd, slots_dram, out):
    def sb(name, shape, dt=F32):
        return nc.alloc_sbuf_tensor(name, shape, dt)

    def sem(name):
        return nc.alloc_semaphore(name)

    def sems(name, n):
        return [sem(f"{name}{i}") for i in range(n)]

    ps = nc.alloc_psum_tensor("ps", [128, 8, 512], F32)

    cst = sb("cst", [128, C_ALL])
    h = sb("h", [G, NT, D])
    xn = sb("xn", [G, NT, D])
    xh, xl = sb("xh", [128, 2, PAD_TOKENS], F16), sb("xl", [128, 2, PAD_TOKENS], F16)
    identb = sb("identb", [G, G], BF16)
    maskb = sb("maskb", [G, 4 * G], BF16)
    zero = sb("zero", [128, 6 * D])
    st6 = sb("st6", [G, NT, 6])
    mv = sb("mv", [G, NT, 2])
    rstd = sb("rstd", [G, NT])
    var = sb("var", [G, NT])
    rinv = sb("rinv", [G, NT])
    ident = cst[:, C_IDENT:C_IDENT + 128]
    ones = cst[:, C_ONES:C_ONES + 128]

    big = sb("big", [128, TAP_CHUNKS * 5 * D])
    w5_sb = big[:TP, :].rearrange("p (c g n) -> p c g n", c=TAP_CHUNKS, g=5)
    g5_sb = sb("g5_sb", [TP, TAP_CHUNKS, 5])
    b5_sb = sb("b5_sb", [TP, TAP_CHUNKS, 5])
    tokb_sb = sb("tokb_sb", [1, D])
    weff = sb("weff", [TP, TAP_CHUNKS, D + 1])
    crow = sb("crow", [1, D])
    cs_sb = sb("cs_sb", [G, 2, D])
    shared = sb("shared", [128, 2 * 2 * 4 * HIDDEN // 2])
    xc = shared[:TP, 0:2 * TAP_CHUNKS * G].rearrange("p (s c t) -> p s c t", s=2, c=TAP_CHUNKS)
    xsq = shared[:TP, 2 * TAP_CHUNKS * G:4 * TAP_CHUNKS * G].rearrange("p (s c t) -> p s c t", s=2, c=TAP_CHUNKS)
    xss = sb("xss", [TP, 2, G])
    tst = sb("tst", [G, NT, 2])
    shift = sb("shift", [G, NT])

    W_COLS = (2 * 384 + INNER[0], 3 * INNER[1])
    ah, al = sb("ah", [128, 2, W_COLS[1]], F16), sb("al", [128, 2, W_COLS[1]], F16)
    wo = sb("wo", [128, 6, D])
    bo = sb("bo", [G, D])
    o_qkl, o_prob, o_pth, o_ptl, o_ctx = 6 * G, 12 * G, 24 * G, 30 * G, 36 * G
    o_ctxT = o_ctx + INNER[1]
    work = sb("work", [128, o_ctxT + 6 * G])
    qkh = work[:, 0:o_qkl].bitcast(F16).rearrange("p (q n) -> p q n", q=4)
    qkl = work[:, o_qkl:o_prob].bitcast(F16).rearrange("p (q n) -> p q n", q=4)
    prob = work[:G, o_prob:o_pth].rearrange("p (n t) -> p n t", n=HEADS)
    pth = work[:G, o_pth:o_ptl].bitcast(F16).rearrange("p (n t) -> p n t", n=HEADS)
    ptl = work[:G, o_ptl:o_ctx].bitcast(F16).rearrange("p (n t) -> p n t", n=HEADS)
    ctx = work[:G, o_ctx:o_ctxT]
    ctxT = work[:, o_ctxT:o_ctxT + 6 * G].rearrange("p (j t) -> p j t", j=6)
    araw = [work[:, 0:2 * w].rearrange("p (c n) -> p c n", c=2) for w in W_COLS]
    kdh = big[:, 0:6 * G].bitcast(F16).rearrange("p (c h t) -> p c h t", c=3, h=4)
    kdl = big[:, 6 * G:12 * G].bitcast(F16).rearrange("p (c h t) -> p c h t", c=3, h=4)
    vh = [sb(f"vh{l}", [G, HEADS, HD[l] + 1], F16) for l in range(2)]
    vl = [sb(f"vl{l}", [G, HEADS, HD[l] + 1], F16) for l in range(2)]
    mx = sb("mx", [G, HEADS])
    rs = sb("rs", [G, HEADS])

    graw = [sb(f"graw{l}", [KD, 2, EXPERTS[l]]) for l in range(2)]
    gh = [sb(f"gh{l}", [KD, 2, EXPERTS[l]], F16) for l in range(2)]
    gl = [sb(f"gl{l}", [KD, 2, EXPERTS[l]], F16) for l in range(2)]
    wraw = sb("wraw", [KD, 4, HIDDEN])
    half = 4 * HIDDEN // 2
    wah = [shared[:KD, s * half:(s + 1) * half].bitcast(F16).rearrange("p (q n) -> p q n", q=4) for s in range(2)]
    wal = [shared[:KD, (2 + s) * half:(3 + s) * half].bitcast(F16).rearrange("p (q n) -> p q n", q=4)
           for s in range(2)]
    wd = sb("wd", [128, 2, HC, D])
    lg = sb("lg", [G, NT, 16])
    m8 = sb("m8", [G, NT, 8])
    i8 = sb("i8", [G, NT, 8], U32)
    idxf = sb("idxf", [G, 2, NT])
    oh = sb("oh", [G, 3, NT, 16])
    base = sb("base", [G, NT, 16])
    tmp = sb("tmp", [G, 2, NT, 16])
    tot = sb("tot", [128, NT, 16])
    cum = sb("cum", [128, NT + 1, 16])
    cmp9 = sb("cmp9", [128, 16, N_THRESH])
    nblk = sb("nblk", [128, 16])
    oend = sb("oend", [128, 16])
    obeg = sb("obeg", [128, 16])
    cmpb = sb("cmpb", [128, max(BLOCKS), 16])
    eb = sb("eb", [128, max(BLOCKS)])
    ebi = sb("ebi", [1, max(BLOCKS)], U32)
    nit = sb("nit", [1, 2 + max(BLOCKS)])
    niti = sb("niti", [1, 1], U32)
    slotf = sb("slotf", [G, 2, NT])
    slot_i = sb("slot_i", [G, 2, NT], U32)
    cw = sb("cw", [G, 2, NT])
    zsum = sb("zsum", [G, NT])
    pw = sb("pw", [G, 2, NT])
    xg = sb("xg", [BT[0], 2, 2, D])
    xgh, xgl = sb("xgh", [KD, 2, 2 * BLOCK[0]], F16), sb("xgl", [KD, 2, 2 * BLOCK[0]], F16)
    silu = sb("silu", [128, 2, 4 * G])
    hb = sb("hb", [128, 2, HC * BLOCK[0]])
    ysb = sb("ysb", [BT[0], 2, 2, D])
    hsh = big[:, 0:HC * 4 * G].rearrange("p (m t) -> p m t", m=HC)
    yg = big[:G, HC * 4 * G:HC * 4 * G + 2 * NT * D].rearrange("p (k t n) -> p k t n", k=2, t=NT)

    s_const, s_gamma, s_beta, s_tokb = sem("s_const"), sem("s_gamma"), sem("s_beta"), sem("s_tokb")
    s_w5 = sems("s_w5", 4)
    s_fold = sem("s_fold")
    s_attw, s_gatew, s_wo, s_wd = sems("s_attw", 2), sem("s_gatew"), sem("s_wo"), sem("s_wd")
    s_shared_in = sems("s_shared_in", 4)
    s_att_split, s_gate_split, s_shared_split, s_high = (sem("s_att_split"), sem("s_gate_split"),
                                                         sem("s_shared_split"), sem("s_high"))
    s_const_set, s_zfill, s_setup, s_weff = sem("s_const_set"), sem("s_zfill"), sem("s_setup"), sem("s_weff")
    s_const_ps, s_crow, s_crep = sem("s_const_ps"), sem("s_crow"), sem("s_crep")
    t_in, t_sq, t_red, t_mm, t_h = sems("t_in", 2), sems("t_sq", 2), sems("t_red", 2), sems("t_mm", 2), sems("t_h", 2)
    dve_own = sem("dve_own")
    n_stat, n_xn, n_tp, n_xh, n_xt = sem("n_stat"), sem("n_xn"), sem("n_tp"), sem("n_xh"), sem("n_xt")
    s_var, s_root = sem("s_var"), sem("s_root")
    a_names = ("qkp", "qkh", "qkl", "vp", "vh", "ve", "score", "sub", "exp", "ptp", "pth", "ptl", "pv",
               "ctx", "out")
    A = [{n: sem(f"a{l}_{n}") for n in a_names + (("ctp", "cte", "op") if l else ())} for l in range(2)]
    m_names = ("lgp", "oh", "cnt", "ex", "exr", "idx", "scat", "comb", "ydone")
    M = [{n: sem(f"m{l}_{n}") for n in m_names + (() if l else ("gup", "silu", "mul", "dnp", "dne"))}
         for l in range(2)]
    b_names = ("tp", "teh", "te", "wh", "wl", "gu", "sl", "hm", "dn", "ye")
    B = [{n: sem(f"b{l}_{n}") for n in b_names} for l in range(2)]
    w_in = [sems(f"b{l}_w", 4) for l in range(2)]
    xg_in, wd_in, y_out = ([sems(f"b{l}_{n}", 2) for l in range(2)] for n in ("xg", "wd", "yo"))
    FLYING = 6
    g_y = [sems(f"b{l}_gy", FLYING) for l in range(2)]
    s_out = sem("s_out")

    e_wa, e_wd = [e0_wa, e1_wa], [e0_wd, e1_wd]
    GROUPS = [range(0, 4), range(4, 8), range(8, NT)]

    def alternating(eng, first, count, step):
        while first < 3:
            step(first, first % 2, first // 2)
            first, count = first + 1, count - 1
        if count // 2:
            with eng.Fori(0, count // 2) as i:
                for j in (first, first + 1):
                    step(2 * i + j, j % 2, i + j // 2)
        if count % 2:
            last = first + count - 1
            step(last, last % 2, last // 2)

    def over_blocks(pairs, step):
        def run(eng):
            for n in range(3):
                step(n, n % 2, n // 2, True)
            with eng.Fori(0, pairs[0]) as i:
                for j in (3, 4):
                    step(2 * i + j, j % 2, i + j // 2, True)
            step(2 * pairs[1] - 1, 1, pairs[1] - 1, False)
        return run

    def wait_from(eng, s, value):
        if not isinstance(value, int) or value > 0:
            eng.wait_ge(s, value)

    def blocks_of(eng):
        beyond = eng.value_load(niti[0:1, 0:1], min_val=0, max_val=max(BLOCKS) // 2 - 2)
        return beyond, beyond + 2

    GROUPS_OF, IN_GROUP, IN_BANK = (3, 2), (4, 6), (4, 3)

    def head_of(l, n):
        return 4 * (n % 3) + n // 3 if l else n

    def score_bank(l, i):
        return (l + 1) * i

    def turned_bank(l, i):
        return (3, 7, 3)[i] if l == 0 else score_bank(l, i)

    def in_banks(l, first):
        return ps[:G, first:first + l + 1, 0:IN_BANK[l] * G]

    V_BANK = (7, 4)

    def over_tiles(eng, full, short, last):
        full(0)
        with eng.Fori(1, NT - 2) as g:
            full(g)
        short(NT - 2)
        last(NT - 1)

    def in_group(l, i, x):
        return x[:, IN_GROUP[l] * i:IN_GROUP[l] * (i + 1), :].rearrange("p (b j) t -> p b (j t)", b=l + 1)

    block = nc.Block()
    with block:
        @block.sync
        def _(sp):
            sp.dma_start(g5_sb[:, :, :], gamma5).then_inc(s_gamma, 16)
            sp.dma_start(w5_sb[:, 0:2, :, :], w5[:, 0:2, :, :]).then_inc(s_w5[0], 16)
            sp.dma_start(b5_sb[:, :, :], beta5).then_inc(s_beta, 16)
            sp.dma_start(w5_sb[:, 2:4, :, :], w5[:, 2:4, :, :]).then_inc(s_w5[1], 16)
            sp.dma_start(cst[:, :], const).then_inc(s_const, 16)
            for c in (4, 6):
                sp.dma_start(w5_sb[:, c:c + 2, :, :], w5[:, c:c + 2, :, :]).then_inc(s_w5[c // 2], 16)
            sp.dma_start(tokb_sb[:, :], tok_b).then_inc(s_tokb, 16)

            def load_tile(t, s, k):
                sp.wait_ge(t_mm[s], k)
                sp.dma_start(xc[:, s, :, :], xcol[bass.ds(t, 1)].rearrange("a p c t -> (a p) c t")
                             ).then_inc(t_in[s], 16)
            alternating(sp, 0, NT, load_tile)

            for p in range(4):
                sp.dma_start(wraw[:, p, :], sh_wa[0:KD, p, :]).then_inc(s_shared_in[p], 16)
            sp.dma_start(wd[:, 0, :, :].rearrange("p m n -> p (m n)"), sh_wd[0:128, :]).then_inc(s_wd, 16)
            sp.wait_ge(A[0]["out"], NT)
            sp.dma_start(araw[1], a1_w).then_inc(s_attw[1], 16)

            for l in range(2):
                b, m = B[l], M[l]
                sp.wait_ge(m["idx"], 1)
                pairs = blocks_of(sp)
                if l == 0:
                    sp.wait_ge(s_shared_split, 4)

                def load_down(n, s):
                    e = sp.value_load(ebi[0:1, bass.ds(n, 1)], min_val=0, max_val=EXPERTS[l] - 1)
                    if isinstance(n, int) and n == 0 and l == 0:
                        sp.wait_ge(m["dnp"], NT)
                    wait_from(sp, b["dn"], n - 1)
                    sp.dma_start(wd[:, s, :, :].rearrange("p m n -> p (m n)"), e_wd[l][bass.ds(e * 128, 128), :]
                                 ).then_inc(wd_in[l][s], 16)

                def store_y(n, s):
                    sp.wait_ge(b["ye"], n + 1)
                    sp.dma_start(slots_dram[bass.ds(n * BLOCK[l], BLOCK[l]), :].rearrange("(j p) n -> p j n", p=BT[l]),
                                 ysb[:BT[l], s, :, :]).then_inc(y_out[l][s], 16)

                def load_rows(n, s):
                    wait_from(sp, b["tp"], n - 1)
                    sp.dma_start(xg[:BT[l], s, :, :], slots_dram[bass.ds(n * BLOCK[l], BLOCK[l]), :].rearrange(
                        "(j p) n -> p j n", p=BT[l])).then_inc(xg_in[l][s], 16)

                def step(n, s, k, more):
                    first = isinstance(n, int) and n == 0
                    if not first:
                        load_rows(n, s)
                    e = sp.value_load(ebi[0:1, bass.ds(n, 1)], min_val=0, max_val=EXPERTS[l] - 1)
                    for p in range(4):
                        wait_from(sp, b["wl"], 4 * (n - 1) + p + 1)
                        sp.dma_start(wraw[:, p, :], e_wa[l][bass.ds(e * KD, KD), p, :]).then_inc(w_in[l][p], 16)
                    if first:
                        sp.wait_ge(m["scat"], 16 * 2 * NT)
                        load_rows(n, s)
                    if not isinstance(n, int) or n >= 1:
                        load_down(n - 1, 1 - s)
                    if not isinstance(n, int) or n >= 3:
                        store_y(n - 3, 1 - s)
                over_blocks(pairs, step)(sp)
                last = 2 * pairs[1]
                if l == 0:
                    for p in range(4):
                        sp.wait_ge(b["wl"], 4 * (last - 1) + p + 1)
                        sp.dma_start(wraw[:, p, :], sh_wa[KD:2 * KD, p, :]).then_inc(w_in[l][p], 16)
                load_down(last - 1, 1)
                if l == 0:
                    sp.wait_ge(b["dn"], last - 1)
                    sp.dma_start(wd[:, 0, :, :].rearrange("p m n -> p (m n)"), sh_wd[128:256, :]).then_inc(s_wd, 16)
                for j in (3, 2, 1):
                    store_y(2 * pairs[1] - j, j % 2)
                for s in range(2):
                    sp.wait_ge(y_out[l][s], 16 * pairs[1])
                sp.sem_inc(m["ydone"], 1)

            for t in range(NT):
                rows = G if t < NT - 1 else LAST
                sp.wait_ge(M[1]["comb"], t + 1)
                sp.dma_start(out[t * G:t * G + rows, :], h[:rows, t, :]).then_inc(s_out, 16)
            sp.wait_ge(s_out, 16 * NT)

        @block.gpsimd
        def _(pool):
            constants = [(zero[:, :], 0.0), (xh[KD:, :, :], 0.0), (xh[KD:KD + 1, 1, :], X_SCALE), (xl[KD:, :, :], 0.0)]
            for l in range(2):
                constants += [(vh[l][:, :, HD[l]:], QKV_SCALE), (vl[l][:, :, HD[l]:], 0.0)]
            for n, (to, value) in enumerate(constants):
                nc.gpsimd.memset(to, value).then_inc(s_const_set, 1)
                pool.wait_ge(s_const_set, n + 1)
            pool.wait_ge(t_in[1], 16)
            pool.dma_start(araw[0], a0_w).then_inc(s_attw[0], 16)
            for l, src in ((0, gate0), (1, gate1)):
                pool.dma_start(graw[l][:, :, :], src).then_inc(s_gatew, 16)
            pool.dma_start(wo[:, :, :], a1_wo).then_inc(s_wo, 16)
            pool.dma_start(bo[:, :], a1_bo).then_inc(s_wo, 16)
            pool.wait_ge(s_weff, 1)
            pool.wait_ge(s_const_ps, 1)
            nc.gpsimd.memset(big[:, 0:12 * G], 0.0).then_inc(s_const_set, 1)
            for lo in range(0, SLOTS, FILL_ROWS):
                n = lo // FILL_ROWS + 2
                if n < NT:
                    pool.wait_ge(t_in[n % 2], 16 * (n // 2 + 1))
                pool.dma_start(slots_dram[lo:lo + FILL_ROWS, :].rearrange("(p r) n -> p (r n)", r=6), zero[:, :]
                               ).then_inc(s_zfill, 16)

            splits = 0

            def split(high, low, raw, done):
                nonlocal splits
                splits += 1
                nc.gpsimd.tensor_scalar(raw, raw, W_SCALE, None, ALU.mult).then_inc(s_high, 1)
                pool.wait_ge(s_high, 2 * splits - 1)
                nc.gpsimd.tensor_copy(high, raw).then_inc(s_high, 1)
                pool.wait_ge(s_high, 2 * splits)
                nc.gpsimd.tensor_tensor(low, raw, high, ALU.subtract).then_inc(done, 1)

            def split_attention(l):
                pool.wait_ge(s_attw[l], 16)
                if l:
                    pool.wait_ge(A[0]["out"], NT)
                split(ah[:, :, 0:W_COLS[l]], al[:, :, 0:W_COLS[l]], araw[l], s_att_split)
            split_attention(0)
            pool.wait_ge(s_gatew, 32)
            for l in range(2):
                split(gh[l][:, :, :], gl[l][:, :, :], graw[l][:, :, :], s_gate_split)
            for s in range(2):
                pool.wait_ge(t_mm[s], (NT + 1 - s) // 2)
            for p in range(4):
                pool.wait_ge(s_shared_in[p], 16)
                split(wah[0][:, p, :], wal[0][:, p, :], wraw[:, p, :], s_shared_split)

            for l in range(2):
                m, b = M[l], B[l]
                if l == 0:
                    pool.wait_ge(s_zfill, 16 * (SLOTS // FILL_ROWS))
                pool.wait_ge(m["idx"], 1)
                for t in range(NT):
                    rows = G if t < NT - 1 else LAST
                    for k in range(2):
                        nc.gpsimd.indirect_dma_start(
                            out=slots_dram, out_offset=bass.IndirectOffsetOnAxis(ap=slot_i[:rows, k, t:t + 1], axis=0),
                            in_=xn[:rows, t, :], in_offset=None).then_inc(m["scat"], 16)
                if l == 0:
                    split_attention(1)
                pool.wait_ge(m["ydone"], 1)
                for t in range(NT):
                    for k in range(2):
                        n = 2 * t + k
                        if n >= FLYING:
                            pool.wait_ge(g_y[l][n % FLYING], 16 * (n // FLYING))
                        nc.gpsimd.indirect_dma_start(
                            out=yg[:, k, t, :], out_offset=None, in_=slots_dram,
                            in_offset=bass.IndirectOffsetOnAxis(ap=slot_i[:, k, t:t + 1], axis=0)
                            ).then_inc(g_y[l][n % FLYING], 16)

        @block.tensor
        def _(pe):
            pe.wait_ge(s_beta, 16)
            n = 0
            for c in range(TAP_CHUNKS):
                if c % 2 == 0:
                    pe.wait_ge(s_w5[c // 2], 16)
                for g in range(5):
                    mm = nc.tensor.matmul(ps[:1, 5, 0:D], b5_sb[:, c, g:g + 1], w5_sb[:, c, g, :],
                                          start=n == 0, stop=n == 5 * TAP_CHUNKS - 1)
                    n += 1
            mm.then_inc(s_const_ps, 1)
            pe.wait_ge(s_const, 16)
            pe.wait_ge(s_weff, 1)

            def tile(t, s, k):
                pe.wait_ge(t_in[s], 16 * (k + 1))
                pe.wait_ge(t_h[s], k)
                for c in range(TAP_CHUNKS):
                    nc.tensor.matmul(ps[:G, s, 0:D + 1], xc[:, s, c, :], weff[:, c, :],
                                     start=c == 0, stop=c == TAP_CHUNKS - 1)
                pe.wait_ge(t_red[s], k + 1)
                nc.tensor.matmul(ps[:G, s, D + 1:D + 2], xss[:, s, :], cst[:TP, C_COUNT:C_COUNT + 1],
                                 start=True, stop=True).then_inc(t_mm[s], 1)
            alternating(pe, 0, NT, tile)
            for c in range(TAP_CHUNKS):
                nc.tensor.matmul(ps[:G, 4, 0:D], ones[:TP, :G], weff[:, c, 0:D],
                                 start=c == 0, stop=c == TAP_CHUNKS - 1)
            pe.wait_ge(s_crow, 1)
            nc.tensor.matmul(ps[:G, 6, 0:D], ones[:1, :G], crow[:, :], start=True, stop=True).then_inc(s_crep, 1)
            pe.wait_ge(t_h[0], (NT + 1) // 2)
            pe.wait_ge(t_h[1], NT // 2)

            def product(out, left, right, start, stop):
                for n, (a, b) in enumerate(((0, 0), (0, 1), (1, 0))):
                    mm = nc.tensor.matmul(out, left[a], right[b], start=start and n == 0, stop=stop and n == 2)
                return mm

            def turn(i):
                for t in range(NT):
                    pe.wait_ge(n_xn, NT * i + t + 1)
                    if t >= 4:
                        pe.wait_ge(n_xt, NT * i + t - 3)
                    for c in range(2):
                        mm = nc.tensor.transpose(ps[:KD, t % 4, c * G:(c + 1) * G],
                                                 xn[:, t, c * KD:(c + 1) * KD], ident[:G, :G])
                    mm.then_inc(n_tp, 1)
                pe.wait_ge(n_xt, NT * (i + 1))

            def attention(l):
                a, hd, sets, ng = A[l], HD[l], 2 * (l + 1), GROUPS_OF[l]
                pe.wait_ge(s_att_split, l + 1)
                pe.wait_ge(s_setup, 1)
                pe.wait_ge(s_const_set, 9)

                def project_qk(g, q):
                    if l == 1 and q < 2:
                        wait_from(pe, a["ve"], g)
                    elif l == 1:
                        pe.wait_ge(a["qkl"], sets * g + q - 1)
                    for j in range(3):
                        n = 3 * q + j
                        for c in range(2):
                            mm = product(ps[:, 4 + q % 2, j * G:(j + 1) * G],
                                         [w[:, c, n * 128:(n + 1) * 128] for w in (ah, al)],
                                         [x[:, c, bass.ds(g * G, G)] for x in (xh, xl)], c == 0, c == 1)
                    mm.then_inc(a["qkp"], 1)

                def project_v(g):
                    if l == 1:
                        pe.wait_ge(a["qkl"], sets * (g + 1))
                    w, o = INNER[l] // (l + 1), 2 * 384 * (l + 1)
                    for b in range(l + 1):
                        for c in range(2):
                            mm = product(ps[:G, V_BANK[l] + b, 0:w], [x[:, c, bass.ds(g * G, G)] for x in (xh, xl)],
                                         [m[:, c, o + b * w:o + (b + 1) * w] for m in (ah, al)],
                                         c == 0, c == 1)
                    mm.then_inc(a["vp"], 1)

                def scores(g, i):
                    if i == 0:
                        pe.wait_ge(a["qkl"], sets * (g + 1))
                    wait_from(pe, a["ptl" if l else "sub"], ng * (g - 1) + i + 1 if not isinstance(g, int) or g else 0)
                    banks = range(score_bank(l, i), score_bank(l, i + 1))
                    w = IN_BANK[l] * G
                    for b in banks:
                        nc.tensor.matmul(ps[:G, b, 0:w], identb[:, :], maskb[:, 0:w], start=True, stop=False,
                                         skip_group_check=True)
                    if l == 0:
                        for n, (x, y) in enumerate(((qkh, kdh), (qkh, kdl), (qkl, kdh))):
                            mm = nc.tensor.matmul(ps[:G, i, 0:w], x[:, 0, i * G:(i + 1) * G],
                                                  y[:, i, :, :].rearrange("p h t -> p (h t)"),
                                                  start=False, stop=n == 2, skip_group_check=True)
                    else:
                        for j in range(3):
                            for b in banks:
                                head = head_of(l, 3 * b + j)
                                chunk, r = head // 2, (head % 2) * hd
                                qs, js = chunk // 3, chunk % 3
                                for n, (x, y) in enumerate(((qkh, qkh), (qkh, qkl), (qkl, qkh))):
                                    mm = nc.tensor.matmul(ps[:G, b, j * G:(j + 1) * G],
                                                          x[r:r + hd, qs, js * G:(js + 1) * G],
                                                          y[r:r + hd, 2 + qs, js * G:(js + 1) * G],
                                                          start=False, stop=n == 2 and j == 2, skip_group_check=True)
                    mm.then_inc(a["score"], 1)

                def turn_probs(g, i):
                    pe.wait_ge(a["exp"], ng * g + 1 + i)
                    if l == 0 and i == 1:
                        pe.wait_ge(a["ve"], g + 1)
                    if l == 0 and i == 2:
                        pe.wait_ge(a["ptl"], ng * g + 1)
                    for n in range(IN_GROUP[l] * i, IN_GROUP[l] * (i + 1)):
                        j = n % IN_BANK[l]
                        bank = turned_bank(l, i) + (n - IN_GROUP[l] * i) // IN_BANK[l]
                        mm = nc.tensor.transpose(ps[:G, bank, j * G:(j + 1) * G], prob[:, n, :],
                                                 ident[:G, :G])
                    mm.then_inc(a["ptp"], 1)

                def mix(g, i):
                    pe.wait_ge(a["ptl"], ng * g + 1 + i)
                    if i == 0:
                        pe.wait_ge(a["ve"], g + 1)
                        wait_from(pe, a["ctx"], g)
                        if l == 1:
                            wait_from(pe, a["out"], g)
                    per_bank = HEADS // (l + 1)
                    for n in range(IN_GROUP[l] * i, IN_GROUP[l] * (i + 1)):
                        head = head_of(l, n)
                        o = (head % per_bank) * (hd + 1)
                        mm = product(ps[:G, 6 + head // per_bank, o:o + hd + 1], (pth[:, n, :], ptl[:, n, :]),
                                     (vh[l][:, head, :], vl[l][:, head, :]), True, True)
                    if i == ng - 1:
                        mm.then_inc(a["pv"], 1)

                def turn_context(g):
                    pe.wait_ge(a["ctx"], g + 1)
                    if not isinstance(g, int) or g < NT - 1:
                        pe.wait_ge(a["ve"], g + 2)
                    for j in range(6):
                        mm = nc.tensor.transpose(ps[:, 4 + j // 3, (j % 3) * G:(j % 3 + 1) * G],
                                                 ctx[:, j * 128:(j + 1) * 128], ident[:G, :G])
                        if j % 3 == 2:
                            mm.then_inc(a["ctp"], 1)

                def project_out(g):
                    for j in range(6):
                        if j == 0:
                            pe.wait_ge(a["cte"], 2 * g + 2)
                        mm = nc.tensor.matmul(ps[:G, 6, 0:D], ctxT[:, j, :], wo[:, j, :], start=j == 0, stop=j == 5)
                    mm.then_inc(a["op"], 1)

                def body(g, more, first=False):
                    for i in range(ng):
                        scores(g, i)
                    if not first:
                        turn_context(g - 1)
                    if more:
                        for q in range(2):
                            if not first:
                                pe.wait_ge(a["cte"], 2 * g - 1 + q)
                            project_qk(g + 1, q)
                    if not first:
                        project_out(g - 1)
                    for i in range(ng):
                        turn_probs(g, i)
                        if more:
                            project_qk(g + 1, 2 + i)
                    for i in range(ng):
                        mix(g, i)
                        if more and i == 1:
                            project_v(g + 1)

                def body0(g, ahead):
                    for i in range(ng):
                        turn_probs(g, i)
                        if ahead:
                            scores(g + 1, i)
                    if ahead == 2:
                        for q in range(sets):
                            project_qk(g + 2, q)
                    for i in range(ng):
                        mix(g, i)
                    if ahead:
                        project_v(g + 1)

                for q in range(sets):
                    project_qk(0, q)
                project_v(0)
                if l == 0:
                    for i in range(ng):
                        scores(0, i)
                    for q in range(sets):
                        project_qk(1, q)
                    over_tiles(pe, lambda g: body0(g, 2), lambda g: body0(g, 1), lambda g: body0(g, 0))
                else:
                    body(0, True, True)
                    with pe.Fori(1, NT - 1) as g:
                        body(g, True)
                    body(NT - 1, False)
                if l == 1:
                    turn_context(NT - 1)
                    project_out(NT - 1)
                pe.wait_ge(a["out"], NT)

            def experts(l):
                m, b = M[l], B[l]
                E = EXPERTS[l]
                pe.wait_ge(s_gate_split, 2)
                for t in range(NT):
                    for c in range(2):
                        mm = product(ps[:G, 6, t * E:(t + 1) * E],
                                     [x[:KD, c, t * G:(t + 1) * G] for x in (xh, xl)],
                                     (gh[l][:, c, :], gl[l][:, c, :]), c == 0, c == 1)
                mm.then_inc(m["lgp"], 1)

                def count_choices():
                    pe.wait_ge(m["oh"], 1)
                    nc.tensor.matmul(ps[:G, 4, 0:NT * E], cst[:G, C_UPPER:C_UPPER + G],
                                     oh[:, 2, :, 0:E], start=True, stop=True)
                    nc.tensor.matmul(ps[:, 5, 0:NT * E], ones[:G, :], oh[:, 2, :, 0:E],
                                     start=True, stop=True).then_inc(m["cnt"], 1)

                def shared_expert(e, extra=None):
                    n, ny = 3 * HC * e, NT * e
                    pe.wait_ge(s_wd, 16 * (e + 1))
                    for gi, tiles in enumerate(GROUPS):
                        lo, w = tiles[0] * G, len(tiles) * G
                        for q in range(HC):
                            if n % (3 * HC) >= 2:
                                pe.wait_ge(m["mul"], n - 1)
                            for u in range(2):
                                for c in range(2):
                                    mm = product(ps[:, 2 * (n % 2) + u, 0:w],
                                                 [m_[:, 2 * c + u, q * 128:(q + 1) * 128] for m_ in (wah[0], wal[0])],
                                                 [x[:KD, c, lo:lo + w] for x in (xh, xl)], c == 0, c == 1)
                            mm.then_inc(m["gup"], 1)
                            n += 1
                            if extra and n == 2:
                                extra()
                        pe.wait_ge(m["mul"], n)
                        if extra and gi == 0:
                            pe.wait_ge(m["idx"], 1)
                        for j, t in enumerate(tiles):
                            if ny % NT >= 4:
                                pe.wait_ge(m["dne"], ny - 3)
                            for q in range(HC):
                                mm = nc.tensor.matmul(ps[:G, 4 + ny % 4, 0:D], hsh[:, q, j * G:(j + 1) * G],
                                                      wd[:, 0, q, :], start=q == 0, stop=q == HC - 1)
                            mm.then_inc(m["dnp"], 1)
                            ny += 1
                    pe.wait_ge(m["dne"], ny)
                if l == 0:
                    pe.wait_ge(s_shared_split, 4)
                    shared_expert(0, count_choices)
                else:
                    count_choices()
                    pe.wait_ge(m["idx"], 1)
                pairs = blocks_of(pe)

                def turn_x(n, s, k):
                    pe.wait_ge(xg_in[l][s], 16 * (k + 1))
                    wait_from(pe, b["te"], n - 1)
                    for c in range(2):
                        for j in range(2):
                            o = c * BLOCK[l] + j * BT[l]
                            mm = nc.tensor.transpose(ps[:KD, 4 + s, o:o + BT[l]],
                                                     xg[:BT[l], s, j, c * KD:(c + 1) * KD], ident[:BT[l], :BT[l]])
                    mm.then_inc(b["tp"], 1)

                def gate_up(n, s, k):
                    pe.wait_ge(b["wl"], 4 * (n + 1))
                    pe.wait_ge(b["te"], n + 1)
                    for third in range(3):
                        pair = (s + third) % 2
                        wait_from(pe, b["hm"], 3 * n + third - 1)
                        for u in range(2):
                            for i in range(2):
                                q = 2 * third + i
                                for c in range(2):
                                    mm = product(ps[:, 2 * pair + u, i * BLOCK[l]:(i + 1) * BLOCK[l]],
                                                 [w[:, 2 * c + u, q * 128:(q + 1) * 128] for w in (wah[s], wal[s])],
                                                 [x[:, s, c * BLOCK[l]:(c + 1) * BLOCK[l]] for x in (xgh, xgl)],
                                                 c == 0, c == 1)
                        mm.then_inc(b["gu"], 1)

                def down_y(n, s, k):
                    pe.wait_ge(wd_in[l][s], 16 * (k + 1))
                    pe.wait_ge(b["hm"], 3 * (n + 1))
                    wait_from(pe, b["ye"], n - 1)
                    for j in range(2):
                        for q in range(HC):
                            o = q * BLOCK[l] + j * BT[l]
                            mm = nc.tensor.matmul(ps[:BT[l], 6 + s, j * D:(j + 1) * D], hb[:, s, o:o + BT[l]],
                                                  wd[:, s, q, :], start=q == 0, stop=q == HC - 1)
                    mm.then_inc(b["dn"], 1)

                def step(n, s, k, more):
                    if more:
                        turn_x(n + 1, 1 - s, k + s)
                    gate_up(n, s, k)
                    if not isinstance(n, int) or n >= 1:
                        down_y(n - 1, 1 - s, k - 1 + s)
                turn_x(0, 0, 0)
                over_blocks(pairs, step)(pe)
                down_y(2 * pairs[1] - 1, 1, pairs[1] - 1)
                pe.wait_ge(b["ye"], 2 * pairs[1])
                if l == 0:
                    pe.wait_ge(b["wl"], 4 * (2 * pairs[1] + 1))
                    shared_expert(1)

            for l in range(2):
                turn(2 * l)
                attention(l)
                turn(2 * l + 1)
                experts(l)

        @block.scalar
        def _(act):
            act.wait_ge(s_gamma, 16)
            for c in range(TAP_CHUNKS):
                if c % 2 == 0:
                    act.wait_ge(s_w5[c // 2], 16)
                nc.scalar.activation(weff[:, c, 0:D], w5_sb[:, c, 0, :], ACT.Copy, scale=g5_sb[:, c, 0:1]
                                     ).then_inc(s_fold, 1)

            def take_tile(t, s, k):
                act.wait_ge(t_mm[s], k + 1)
                nc.scalar.copy(h[:, bass.ds(t, 1), :].rearrange("p a n -> p (a n)"), ps[:G, s, 0:D])
                nc.scalar.copy(tst[:, bass.ds(t, 1), :].rearrange("p a n -> p (a n)"), ps[:G, s, D:D + 2]
                               ).then_inc(t_h[s], 1)

            def square(t, s, k):
                act.wait_ge(t_in[s], 16 * (k + 1))
                act.wait_ge(t_red[s], k)
                nc.scalar.activation(xsq[:, s, :, :], xc[:, s, :, :], ACT.Square).then_inc(t_sq[s], 1)
                take_tile(t, s, k)
            alternating(act, 0, NT, square)

            def root(n):
                act.wait_ge(s_var, n)
                nc.scalar.activation(rstd[:, :], rinv[:, :], ACT.Sqrt).then_inc(s_root, 1)
            root(1)

            def evacuate_turned(i):
                for t in range(NT):
                    act.wait_ge(n_tp, NT * i + t + 1)
                    nc.scalar.mul(xh[:KD, :, t * G:(t + 1) * G],
                                  ps[:KD, t % 4, 0:2 * G].rearrange("p (c t) -> p c t", c=2), X_SCALE
                                  ).then_inc(n_xh, 1)

            def split_piece(l, n, s, p, used):
                act.wait_ge(w_in[l][p], 16 * (n + 1))
                used()
                nc.scalar.mul(wah[s][:, p, :], wraw[:, p, :], W_SCALE).then_inc(B[l]["wh"], 1)

            def attention(l):
                a, sets, ng = A[l], 2 * (l + 1), GROUPS_OF[l]

                def take_qk(g, q):
                    if q == 0:
                        wait_from(act, a["score"], ng * g)
                    act.wait_ge(a["qkp"], sets * g + q + 1)
                    if l == 0 and q == 1:
                        for j in range(4):
                            rows = slice(32 * j, 32 * j + 32)
                            op = nc.scalar.mul(kdh[rows, :, j, :], ps[rows, 5, 0:3 * G].rearrange("p (c t) -> p c t", c=3),
                                               XW * QKV_SCALE)
                    else:
                        op = nc.scalar.mul(qkh[:, q, :], ps[:, 4 + q % 2, 0:3 * G], XW * QKV_SCALE)
                    op.then_inc(a["qkh"], 1)

                def take_v(g):
                    act.wait_ge(a["vp"], g + 1)
                    wait_from(act, a["pv"], g)
                    w = HEADS // (l + 1)
                    for b in range(l + 1):
                        op = nc.scalar.mul(vh[l][:, b * w:(b + 1) * w, 0:HD[l]],
                                           ps[:G, V_BANK[l] + b, 0:w * HD[l]].rearrange("p (h d) -> p h d", h=w),
                                           XW * QKV_SCALE)
                    op.then_inc(a["vh"], 1)

                def take_context(g):
                    for i in range(2):
                        act.wait_ge(a["ctp"], 2 * g + 1 + i)
                        nc.scalar.copy(ctxT[:, 3 * i:3 * i + 3, :].rearrange("p j t -> p (j t)"),
                                       ps[:, 4 + i, 0:3 * G]).then_inc(a["cte"], 1)

                def exponentials(g, i):
                    act.wait_ge(a["sub"], ng * g + 1 + i)
                    part = in_group(l, i, prob)
                    nc.scalar.activation(part, part, ACT.Exp, scale=float(HD[l]) ** -0.5 / QKV_SCALE ** 2
                                         ).then_inc(a["exp"], 1)

                def take_probs(g, i):
                    if i == 0:
                        wait_from(act, a["pv"], g)
                    act.wait_ge(a["ptp"], ng * g + 1 + i)
                    nc.scalar.mul(in_group(l, i, pth), in_banks(l, turned_bank(l, i)), P_SCALE).then_inc(a["pth"], 1)

                def body(g, more, first=False):
                    if not first:
                        take_context(g - 1)
                    for i in range(ng):
                        exponentials(g, i)
                        if more:
                            take_qk(g + 1, i)
                    for i in range(ng):
                        take_probs(g, i)
                        if more:
                            take_qk(g + 1, 2 + i)
                    if more:
                        take_v(g + 1)

                def body0(g, ahead):
                    for i in range(ng):
                        take_probs(g, i)
                        if ahead == 2 and i == ng - 1:
                            for q in range(sets):
                                take_qk(g + 2, q)
                        if ahead:
                            exponentials(g + 1, i)
                    if ahead:
                        take_v(g + 1)

                act.wait_ge(s_setup, 1)
                act.wait_ge(s_const_set, 9)
                for q in range(sets):
                    take_qk(0, q)
                take_v(0)
                if l == 0:
                    for i in range(ng):
                        exponentials(0, i)
                    for q in range(sets):
                        take_qk(1, q)
                    over_tiles(act, lambda g: body0(g, 2), lambda g: body0(g, 1), lambda g: body0(g, 0))
                else:
                    body(0, True, True)
                    with act.Fori(1, NT - 1) as g:
                        body(g, True)
                    body(NT - 1, False)
                if l == 1:
                    take_context(NT - 1)

            def experts(l):
                m, b = M[l], B[l]
                E = EXPERTS[l]
                act.wait_ge(m["ex"], 1)
                nc.scalar.activation(tmp[:, 0, :, 0:E], tmp[:, 0, :, 0:E], ACT.Exp).then_inc(m["exr"], 1)
                nc.scalar.activation(pw[:, 1, :], pw[:, 1, :], ACT.Exp).then_inc(m["exr"], 1)

                def shared_expert(e):
                    n = 3 * HC * e
                    for tiles in GROUPS:
                        w = len(tiles) * G
                        for q in range(HC):
                            act.wait_ge(m["gup"], n + 1)
                            if n % (3 * HC) >= 2:
                                act.wait_ge(m["mul"], n - 1)
                            nc.scalar.activation(silu[:, n % 2, 0:w], ps[:, 2 * (n % 2), 0:w], ACT.Silu, scale=XW
                                                 ).then_inc(m["silu"], 1)
                            n += 1
                if l == 0:
                    shared_expert(0)
                act.wait_ge(m["idx"], 1)
                pairs = blocks_of(act)

                def free(n):
                    if isinstance(n, int) and n < 2:
                        if l == 0 and n == 0:
                            act.wait_ge(m["gup"], 3 * HC)
                    else:
                        act.wait_ge(b["gu"], 3 * (n - 1))

                def take_x(n, s):
                    act.wait_ge(b["tp"], n + 1)
                    free(n)
                    nc.scalar.mul(xgh[:, s, 0:2 * BLOCK[l]], ps[:KD, 4 + s, 0:2 * BLOCK[l]], X_SCALE
                                  ).then_inc(b["teh"], 1)

                def swish(n, s, third):
                    pair = (s + third) % 2
                    act.wait_ge(b["gu"], 3 * n + third + 1)
                    wait_from(act, b["hm"], 3 * n + third - 1)
                    nc.scalar.activation(silu[:, pair, 0:2 * BLOCK[l]], ps[:, 2 * pair, 0:2 * BLOCK[l]], ACT.Silu, scale=XW
                                         ).then_inc(b["sl"], 1)

                def take_y(n, s, k):
                    act.wait_ge(b["dn"], n + 1)
                    wait_from(act, y_out[l][s], 16 * k)
                    nc.scalar.copy(ysb[:BT[l], s, :, :].rearrange("p j n -> p (j n)"), ps[:BT[l], 6 + s, 0:2 * D]
                                   ).then_inc(b["ye"], 1)

                def step(n, s, k, more):
                    if more:
                        take_x(n + 1, 1 - s)
                    for i in range(4):
                        if more or l == 0:
                            split_piece(l, n + 1, 1 - s, i, lambda: free(n + 1))
                        if i < 3:
                            swish(n, s, i)
                    if not isinstance(n, int) or n >= 1:
                        take_y(n - 1, 1 - s, k - 1 + s)
                for p in range(4):
                    split_piece(l, 0, 0, p, lambda: free(0))
                take_x(0, 0)
                over_blocks(pairs, step)(act)
                take_y(2 * pairs[1] - 1, 1, pairs[1] - 1)
                if l == 0:
                    act.wait_ge(b["hm"], 6 * pairs[1])
                    shared_expert(1)

            for l in range(2):
                root(2 * l + 2)
                evacuate_turned(2 * l)
                attention(l)
                root(2 * l + 3)
                evacuate_turned(2 * l + 1)
                experts(l)

        @block.vector
        def _(dve):
            count = [0]

            def link(op, before=None):
                op.then_inc(dve_own, 1)
                if before is None:
                    count[0] += 1
                    dve.wait_ge(dve_own, count[0])
                else:
                    dve.wait_ge(dve_own, before + 1)

            dve.wait_ge(s_gamma, 16)
            for c in range(0, TAP_CHUNKS, 2):
                dve.wait_ge(s_w5[c // 2], 16)
                dve.wait_ge(s_fold, c + 2)
                for g in range(1, 5):
                    for cc in (c, c + 1):
                        op = nc.vector.scalar_tensor_tensor(out=weff[:, cc, 0:D], in0=w5_sb[:, cc, g, :],
                                                            scalar=g5_sb[:, cc, g:g + 1], in1=weff[:, cc, 0:D],
                                                            op0=ALU.mult, op1=ALU.add)
                    link(op)
            dve.wait_ge(s_const, 16)
            nc.vector.tensor_copy(weff[:, :, D:D + 1],
                                  cst[:TP, C_COUNT:C_COUNT + 1].unsqueeze(2).to_broadcast([TP, TAP_CHUNKS, 1])
                                  ).then_inc(s_weff, 1)
            nc.vector.tensor_copy(identb[:, :], cst[:G, C_IDENT:C_IDENT + G])
            nc.vector.tensor_copy(maskb[:, :], cst[:G, C_MASK:C_MASK + 4 * G]).then_inc(s_setup, 1)
            dve.wait_ge(s_const_ps, 1)
            dve.wait_ge(s_tokb, 16)
            nc.vector.tensor_tensor(crow[:, :], ps[:1, 5, 0:D], tokb_sb[:, :], ALU.add).then_inc(s_crow, 1)

            def tile(t, s, k):
                dve.wait_ge(t_sq[s], k + 1)
                dve.wait_ge(t_mm[s], k)
                nc.vector.tensor_reduce(xss[:, s, :], xsq[:, s, :, :].rearrange("p c t -> p t c"), AX.X, ALU.add
                                        ).then_inc(t_red[s], 1)
            alternating(dve, 0, NT, tile)

            def inverse_root(n):
                link(nc.vector.reciprocal(rinv[:, :], var[:, :]))
                dve.sem_inc(s_var, 1)
                dve.wait_ge(s_root, n)
                link(nc.vector.tensor_tensor(rinv[:, :], rstd[:, :], rstd[:, :], ALU.mult))
                link(nc.vector.tensor_tensor(rinv[:, :], rinv[:, :], var[:, :], ALU.mult))
                link(nc.vector.tensor_scalar(rinv[:, :], rinv[:, :], -0.5, 1.5, ALU.mult, ALU.add))
                link(nc.vector.tensor_tensor(rstd[:, :], rstd[:, :], rinv[:, :], ALU.mult))

            dve.wait_ge(s_crep, 1)
            nc.vector.tensor_copy(cs_sb[:, 0, :], ps[:G, 4, 0:D])
            link(nc.vector.tensor_copy(cs_sb[:, 1, :], ps[:G, 6, 0:D]))

            for s in range(2):
                dve.wait_ge(t_h[s], (NT + 1 - s) // 2)
            link(nc.vector.tensor_scalar(tst[:, :, :], tst[:, :, :], 1.0 / FEATURES, None, ALU.mult))
            link(nc.vector.tensor_tensor(var[:, :], tst[:, :, 0], tst[:, :, 0], ALU.mult))
            link(nc.vector.tensor_tensor(var[:, :], tst[:, :, 1], var[:, :], ALU.subtract))
            link(nc.vector.tensor_scalar(var[:, :], var[:, :], TOK_EPS, None, ALU.add))
            inverse_root(1)
            link(nc.vector.scalar_tensor_tensor(out=shift[:, :], in0=tst[:, :, 0], scalar=-1.0, in1=rstd[:, :],
                                                op0=ALU.mult, op1=ALU.mult))
            for t in range(NT):
                op = nc.vector.scalar_tensor_tensor(out=h[:, t, :], in0=h[:, t, :], scalar=rstd[:, t:t + 1],
                                                    in1=cs_sb[:, 1, :], op0=ALU.mult, op1=ALU.add)
            link(op)
            for t in range(NT):
                op = nc.vector.scalar_tensor_tensor(out=h[:, t, :], in0=cs_sb[:, 0, :], scalar=shift[:, t:t + 1],
                                                    in1=h[:, t, :], op0=ALU.mult, op1=ALU.add)
            link(op)

            def split_piece(l, n, s, p):
                dve.wait_ge(B[l]["wh"], 4 * n + p + 1)
                nc.vector.scalar_tensor_tensor(out=wal[s][:, p, :], in0=wraw[:, p, :], scalar=W_SCALE,
                                               in1=wah[s][:, p, :], op0=ALU.mult, op1=ALU.subtract
                                               ).then_inc(B[l]["wl"], 1)

            def normalise(i):
                if i == 0:
                    for t in range(NT):
                        nc.vector.bn_stats(st6[:, t, :], h[:, t, :]).then_inc(n_stat, 1)
                dve.wait_ge(n_stat, NT * (i + 1))
                for t in range(NT):
                    op = nc.vector.bn_aggr(mv[:, t, :], st6[:, t, :])
                link(op)
                link(nc.vector.tensor_scalar(var[:, :], mv[:, :, 1], LN_EPS, None, ALU.add))
                inverse_root(i + 2)
                for t in range(NT):
                    nc.vector.tensor_scalar(xn[:, t, :], h[:, t, :], mv[:, t, 0:1], rstd[:, t:t + 1],
                                            ALU.subtract, ALU.mult).then_inc(n_xn, 1)
                for t in range(NT):
                    dve.wait_ge(n_xh, NT * i + t + 1)
                    nc.vector.scalar_tensor_tensor(
                        out=xl[:KD, :, t * G:(t + 1) * G],
                        in0=ps[:KD, t % 4, 0:2 * G].rearrange("p (c t) -> p c t", c=2), scalar=X_SCALE,
                        in1=xh[:KD, :, t * G:(t + 1) * G], op0=ALU.mult, op1=ALU.subtract).then_inc(n_xt, 1)
                if i == 2:
                    dve.wait_ge(s_wo, 32)
                    link(nc.vector.tensor_tensor(h[:, :, :], h[:, :, :],
                                                 bo[:, :].unsqueeze(1).to_broadcast([G, NT, D]), ALU.add))

            def attention(l):
                a, hd, sets, ng = A[l], HD[l], 2 * (l + 1), GROUPS_OF[l]
                dve.wait_ge(s_setup, 1)
                dve.wait_ge(s_const_set, 9)

                def take_qk(g, q):
                    dve.wait_ge(a["qkh"], sets * g + q + 1)
                    if l == 0 and q == 1:
                        for j in range(4):
                            rows = slice(32 * j, 32 * j + 32)
                            op = nc.vector.scalar_tensor_tensor(
                                out=kdl[rows, :, j, :], in0=ps[rows, 5, 0:3 * G].rearrange("p (c t) -> p c t", c=3),
                                scalar=XW * QKV_SCALE, in1=kdh[rows, :, j, :], op0=ALU.mult, op1=ALU.subtract)
                    else:
                        op = nc.vector.scalar_tensor_tensor(out=qkl[:, q, :], in0=ps[:, 4 + q % 2, 0:3 * G],
                                                            scalar=XW * QKV_SCALE, in1=qkh[:, q, :], op0=ALU.mult,
                                                            op1=ALU.subtract)
                    op.then_inc(a["qkl"], 1)

                def take_v(g):
                    dve.wait_ge(a["vh"], g + 1)
                    w = HEADS // (l + 1)
                    for b in range(l + 1):
                        op = nc.vector.scalar_tensor_tensor(
                            out=vl[l][:, b * w:(b + 1) * w, 0:hd],
                            in0=ps[:G, V_BANK[l] + b, 0:w * hd].rearrange("p (h d) -> p h d", h=w),
                            scalar=XW * QKV_SCALE, in1=vh[l][:, b * w:(b + 1) * w, 0:hd], op0=ALU.mult,
                            op1=ALU.subtract)
                    op.then_inc(a["ve"], 1)

                own_n = ng + 1
                first_own = count[0]

                def row(g):
                    return h[:, bass.ds(g, 1), :].rearrange("p a n -> p (a n)")

                def statistics(g):
                    dve.wait_ge(a["out"], g + 1)
                    nc.vector.bn_stats(st6[:, bass.ds(g, 1), :].rearrange("p a n -> p (a n)"), row(g)
                                       ).then_inc(n_stat, 1)

                def take_out(g):
                    dve.wait_ge(a["op"], g + 1)
                    nc.vector.tensor_tensor(row(g), ps[:G, 6, 0:D], row(g), ALU.add).then_inc(a["out"], 1)
                    statistics(g)

                def of_scores(i):
                    part = slice(IN_GROUP[l] * i, IN_GROUP[l] * (i + 1))
                    return (in_banks(l, score_bank(l, i)).rearrange("p b (j t) -> p b j t", t=G),
                            mx[:, part].rearrange("p (b j) -> p b j", b=l + 1),
                            prob[:, part, :].rearrange("p (b j) t -> p b j t", b=l + 1))

                def maximum(g, i, own):
                    scores, maxima, _ = of_scores(i)
                    dve.wait_ge(a["score"], ng * g + 1 + i)
                    nc.vector.tensor_reduce(maxima, scores, AX.X, ALU.max).then_inc(dve_own, 1)

                def subtract(g, i, own):
                    scores, maxima, to = of_scores(i)
                    dve.wait_ge(dve_own, own + i + 1)
                    if l == 0:
                        wait_from(dve, a["ptp"], ng * (g - 1) + 1 + i if not isinstance(g, int) or g else 0)
                    nc.vector.tensor_tensor(to, scores, maxima.unsqueeze(3).to_broadcast([G, l + 1, IN_BANK[l], G]),
                                            ALU.subtract).then_inc(a["sub"], 1)

                def take_probs(g, i):
                    dve.wait_ge(a["pth"], ng * g + 1 + i)
                    nc.vector.scalar_tensor_tensor(out=in_group(l, i, ptl), in0=in_banks(l, turned_bank(l, i)),
                                                   scalar=P_SCALE, in1=in_group(l, i, pth), op0=ALU.mult,
                                                   op1=ALU.subtract).then_inc(a["ptl"], 1)

                def context(g, own):
                    dve.wait_ge(a["pv"], g + 1)
                    nb = l + 1
                    got = ps[:G, 6:6 + nb, 0:HEADS // nb * (hd + 1)].rearrange("p b (h d) -> p b h d", d=hd + 1)
                    rv = rs[:, :].rearrange("p (b h) -> p b h", b=nb)
                    link(nc.vector.reciprocal(rv, got[:, :, :, hd]), own)
                    cv = ctx[:, 0:INNER[l]].rearrange("p (b h d) -> p b h d", b=nb, d=hd)
                    nc.vector.tensor_tensor(cv, got[:, :, :, 0:hd],
                                            rv.unsqueeze(3).to_broadcast([G, nb, HEADS // nb, hd]), ALU.mult
                                            ).then_inc(a["ctx"], 1)
                    if l == 0:
                        dve.wait_ge(a["ctx"], g + 1)
                        nc.vector.tensor_tensor(row(g), row(g), ctx[:, 0:D], ALU.add).then_inc(a["out"], 1)

                def body(g, more, first=False):
                    own = first_own + own_n * g
                    for i in range(ng):
                        maximum(g, i, own)
                        subtract(g, i, own)
                        if more:
                            take_qk(g + 1, i)
                    if not first:
                        take_out(g - 1)
                    for i in range(ng):
                        take_probs(g, i)
                        if more:
                            take_qk(g + 1, 2 + i)
                    context(g, own + ng)
                    if more:
                        take_v(g + 1)

                def body0(g, ahead):
                    own = first_own + ng + own_n * g
                    for i in range(ng):
                        take_probs(g, i)
                        if ahead:
                            maximum(g + 1, i, own)
                            subtract(g + 1, i, own)
                    if ahead == 2:
                        for q in range(sets):
                            take_qk(g + 2, q)
                    context(g, own + (ng if ahead else 0))
                    if ahead:
                        take_v(g + 1)
                    statistics(g)

                for q in range(sets):
                    take_qk(0, q)
                take_v(0)
                if l == 0:
                    for i in range(ng):
                        maximum(0, i, first_own)
                        subtract(0, i, first_own)
                    for q in range(sets):
                        take_qk(1, q)
                    over_tiles(dve, lambda g: body0(g, 2), lambda g: body0(g, 1), lambda g: body0(g, 0))
                else:
                    body(0, True, True)
                    with dve.Fori(1, NT - 1) as g:
                        body(g, True)
                    body(NT - 1, False)
                    take_out(NT - 1)
                count[0] = first_own + own_n * NT
                dve.wait_ge(a["out"], NT)

            def choose(l):
                m, E = M[l], EXPERTS[l]
                iota_e = cst[:, C_IOTA_E:C_IOTA_E + E]
                dve.wait_ge(m["lgp"], 1)
                link(nc.vector.tensor_scalar(lg[:, :, 0:E], ps[:G, 6, 0:NT * E].rearrange("p (t e) -> p t e", e=E),
                                             XW, None, ALU.mult))
                for t in range(NT):
                    op = nc.vector.max(m8[:, t, :], lg[:, t, 0:E])
                link(op)
                nc.vector.tensor_tensor(tmp[:, 0, :, 0:E], lg[:, :, 0:E],
                                        m8[:, :, 0:1].to_broadcast([G, NT, E]), ALU.subtract)
                nc.vector.tensor_tensor(pw[:, 1, :], m8[:, :, 1], m8[:, :, 0], ALU.subtract).then_inc(m["ex"], 1)
                for t in range(NT):
                    op = nc.vector.max_index(i8[:, t, :], m8[:, t, :], lg[:, t, 0:E])
                link(op)
                for k in range(2):
                    op = nc.vector.tensor_tensor(idxf[:, k, :], i8[:, :, k], cst[:G, C_INVALID:C_INVALID + NT], ALU.add)
                link(op)
                for k in range(2):
                    op = nc.vector.tensor_tensor(oh[:, k, :, 0:E], iota_e[:G, :].unsqueeze(1).to_broadcast([G, NT, E]),
                                                 idxf[:, k, :].unsqueeze(2).to_broadcast([G, NT, E]), ALU.is_equal)
                link(op)
                nc.vector.tensor_tensor(oh[:, 2, :, 0:E], oh[:, 0, :, 0:E], oh[:, 1, :, 0:E], ALU.add
                                        ).then_inc(m["oh"], 1)

            def add_up(l):
                m, E = M[l], EXPERTS[l]
                dve.wait_ge(m["cnt"], 1)
                nc.vector.tensor_copy(tot[:, :, 0:E], ps[:, 5, 0:NT * E].rearrange("p (t e) -> p t e", e=E))
                link(nc.vector.memset(cum[:, 0, :], 0.0))
                for t in range(NT):
                    link(nc.vector.tensor_tensor(cum[:, t + 1, 0:E], cum[:, t, 0:E], tot[:, t, 0:E], ALU.add))

            def place_experts(l):
                E = EXPERTS[l]
                thresholds = cst[:, C_THRESH + l * N_THRESH:C_THRESH + (l + 1) * N_THRESH]
                link(nc.vector.tensor_tensor(cmp9[:, 0:E, :],
                                             cum[:, NT, 0:E].unsqueeze(2).to_broadcast([128, E, N_THRESH]),
                                             thresholds.unsqueeze(1).to_broadcast([128, E, N_THRESH]), ALU.is_gt))
                link(nc.vector.tensor_reduce(nblk[:, 0:E], cmp9[:, 0:E, :], AX.X, ALU.add))
                link(nc.vector.tensor_copy(oend[:, 0:1], nblk[:, 0:1]))
                for e in range(1, E):
                    link(nc.vector.tensor_tensor(oend[:, e:e + 1], oend[:, e - 1:e], nblk[:, e:e + 1], ALU.add))
                link(nc.vector.tensor_tensor(obeg[:, 0:E], oend[:, 0:E], nblk[:, 0:E], ALU.subtract))

            def place_tokens(l):
                m, E, NB = M[l], EXPERTS[l], BLOCKS[l]
                link(nc.vector.tensor_tensor(cmpb[:, 0:NB, 0:E],
                                             cst[:, C_IOTA_B:C_IOTA_B + NB].unsqueeze(2).to_broadcast([128, NB, E]),
                                             oend[:, 0:E].unsqueeze(1).to_broadcast([128, NB, E]), ALU.is_ge))
                link(nc.vector.tensor_reduce(eb[:, 0:NB], cmpb[:, 0:NB, 0:E], AX.X, ALU.add))
                link(nc.vector.tensor_scalar(eb[:, 0:NB], eb[:, 0:NB], float(E - 1), None, ALU.min))
                nc.vector.tensor_copy(ebi[:, 0:NB], eb[0:1, 0:NB])
                link(nc.vector.tensor_scalar(nit[:, 2:NB // 2], cst[0:1, C_IOTA_B + 2:C_IOTA_B + NB // 2], 2.0,
                                             oend[0:1, E - 1:E], ALU.mult, ALU.is_lt))
                link(nc.vector.tensor_reduce(nit[:, 0:1], nit[:, 2:NB // 2], AX.X, ALU.add))
                nc.vector.tensor_copy(niti[:, :], nit[:, 0:1])
                link(nc.vector.tensor_tensor(base[:, :, 0:E], ps[:G, 4, 0:NT * E].rearrange("p (t e) -> p t e", e=E),
                                             cum[:G, 0:NT, 0:E], ALU.add))
                link(nc.vector.scalar_tensor_tensor(out=base[:, :, 0:E],
                                                    in0=obeg[:G, 0:E].unsqueeze(1).to_broadcast([G, NT, E]),
                                                    scalar=float(BLOCK[l]), in1=base[:, :, 0:E],
                                                    op0=ALU.mult, op1=ALU.add))
                dve.wait_ge(m["exr"], 2)
                if l == 0:
                    link(nc.vector.tensor_reduce(zsum[:, :], tmp[:, 0, :, 0:E], AX.X, ALU.add))
                for k in range(2):
                    op = nc.vector.tensor_tensor(oh[:, k, :, 0:E], oh[:, k, :, 0:E], base[:, :, 0:E], ALU.mult)
                link(op)
                link(nc.vector.tensor_reduce(slotf[:, :, :], oh[:, 0:2, :, 0:E], AX.X, ALU.add))
                nc.vector.tensor_copy(slot_i[:, :, :], slotf[:, :, :]).then_inc(m["idx"], 1)

            def weigh(l):
                if l == 0:
                    link(nc.vector.reciprocal(pw[:, 0, :], zsum[:, :]))
                    link(nc.vector.tensor_tensor(pw[:, 1, :], pw[:, 1, :], pw[:, 0, :], ALU.mult))
                    link(nc.vector.scalar_tensor_tensor(out=zsum[:, :], in0=pw[:, 0, :], scalar=1e-8, in1=pw[:, 1, :],
                                                        op0=ALU.add, op1=ALU.add))
                else:
                    nc.vector.memset(pw[:, 0, :], 1.0)
                    link(nc.vector.tensor_scalar(zsum[:, :], pw[:, 1, :], 1.0, None, ALU.add))
                link(nc.vector.reciprocal(zsum[:, :], zsum[:, :]))
                link(nc.vector.tensor_tensor(cw[:, :, :], pw[:, :, :], zsum[:, :].unsqueeze(1).to_broadcast([G, 2, NT]),
                                             ALU.mult))

            def experts(l):
                m, b = M[l], B[l]
                stages = [add_up, place_experts, place_tokens, weigh]

                def shared_expert(e):
                    n, ny = 3 * HC * e, NT * e
                    for gi, tiles in enumerate(GROUPS):
                        w = len(tiles) * G
                        for q in range(HC):
                            dve.wait_ge(m["silu"], n + 1)
                            if q == 0 and gi:
                                dve.wait_ge(m["dnp"], ny)
                            nc.vector.scalar_tensor_tensor(out=hsh[:, q, 0:w], in0=ps[:, 2 * (n % 2) + 1, 0:w],
                                                           scalar=XW, in1=silu[:, n % 2, 0:w], op0=ALU.mult,
                                                           op1=ALU.mult).then_inc(m["mul"], 1)
                            n += 1
                            if 1 <= n <= len(stages):
                                stages[n - 1](l)
                        if e == 0 and gi == len(GROUPS) - 1:
                            for p in range(4):
                                split_piece(l, 0, 0, p)
                        for t in tiles:
                            dve.wait_ge(m["dnp"], ny + 1)
                            nc.vector.scalar_tensor_tensor(out=h[:, t, :], in0=ps[:G, 4 + ny % 4, 0:D], scalar=0.5,
                                                           in1=h[:, t, :], op0=ALU.mult, op1=ALU.add
                                                           ).then_inc(m["dne"], 1)
                            ny += 1
                        if e:
                            dve.wait_ge(m["dne"], ny)
                            combine(tiles)

                def combine(tiles):
                    for t in tiles:
                        for k in range(2):
                            n = 2 * t + k
                            dve.wait_ge(g_y[l][n % FLYING], 16 * (n // FLYING + 1))
                            op = nc.vector.scalar_tensor_tensor(out=h[:, t, :], in0=yg[:, k, t, :],
                                                                scalar=cw[:, k, t:t + 1], in1=h[:, t, :],
                                                                op0=ALU.mult, op1=ALU.add)
                            if k == 0:
                                link(op)
                            else:
                                op.then_inc(m["comb"], 1)
                        if l == 0:
                            dve.wait_ge(m["comb"], t + 1)
                            nc.vector.bn_stats(st6[:, t, :], h[:, t, :]).then_inc(n_stat, 1)
                choose(l)
                if l == 0:
                    shared_expert(0)
                    dve.wait_ge(m["dne"], NT)
                else:
                    for stage in stages:
                        stage(l)
                dve.wait_ge(m["idx"], 1)
                pairs = blocks_of(dve)

                def take_x(n, s):
                    dve.wait_ge(b["teh"], n + 1)
                    nc.vector.scalar_tensor_tensor(out=xgl[:, s, 0:2 * BLOCK[l]],
                                                   in0=ps[:KD, 4 + s, 0:2 * BLOCK[l]], scalar=X_SCALE,
                                                   in1=xgh[:, s, 0:2 * BLOCK[l]],
                                                   op0=ALU.mult, op1=ALU.subtract).then_inc(b["te"], 1)

                def multiply(n, s, third):
                    pair = (s + third) % 2
                    dve.wait_ge(b["sl"], 3 * n + third + 1)
                    wait_from(dve, b["dn"], n - 1)
                    nc.vector.scalar_tensor_tensor(
                        out=hb[:, s, 2 * third * BLOCK[l]:2 * (third + 1) * BLOCK[l]],
                        in0=ps[:, 2 * pair + 1, 0:2 * BLOCK[l]], scalar=XW, in1=silu[:, pair, 0:2 * BLOCK[l]],
                        op0=ALU.mult, op1=ALU.mult).then_inc(b["hm"], 1)

                def step(n, s, k, more):
                    if more:
                        take_x(n + 1, 1 - s)
                    for i in range(4):
                        if more or l == 0:
                            split_piece(l, n + 1, 1 - s, i)
                        if i < 3:
                            multiply(n, s, i)
                if l == 1:
                    for p in range(4):
                        split_piece(l, 0, 0, p)
                take_x(0, 0)
                over_blocks(pairs, step)(dve)

                if l == 0:
                    dve.wait_ge(b["hm"], 6 * pairs[1])
                    shared_expert(1)
                else:
                    combine(range(NT))
                dve.wait_ge(m["comb"], NT)

            for l in range(2):
                normalise(2 * l)
                attention(l)
                normalise(2 * l + 1)
                experts(l)


def kernel(**inputs):
    import numpy as _np
    import concourse.bacc as _bacc
    from concourse import mybir as _mybir
    from concourse.bass_utils import run_bass_kernel_spmd as _run

    a = {k: _np.asarray(v) for k, v in inputs.items()}

    def parts(w):
        return w.reshape(2, KD, -1).transpose(1, 0, 2)

    x = _np.zeros((NT * PER, IMG + 2, IMG + 2, CH), a["x"].dtype)
    x[:BATCH, 1:-1, 1:-1] = a["x"]
    xcol = _np.zeros((NT, TP, TAP_CHUNKS, PER, SIDE, SIDE), x.dtype)
    for p, row in enumerate(TAPS):
        for c, tap in enumerate(row):
            if tap is not None:
                ty, tx, ch = tap
                seen = x[:, ty + 1:ty + 2 + PATCH * (SIDE - 1):PATCH, tx + 1:tx + 2 + PATCH * (SIDE - 1):PATCH, ch]
                xcol[:, p, c] = seen.reshape(NT, PER, SIDE, SIDE)
    xcol = xcol.reshape(NT, TP, TAP_CHUNKS, G)
    moves = ((0, 0), (0, 1), (0, -1), (1, 0), (-1, 0))
    w = a["L0_tok_W"].reshape(PATCH, PATCH, 5, CH, D)
    ga = a["L0_tok_gamma"].reshape(PATCH, PATCH, 5, CH)
    be = a["L0_tok_beta"].reshape(PATCH, PATCH, 5, CH)
    w5 = _np.zeros((TP, TAP_CHUNKS, 5, D), w.dtype)
    g5 = _np.zeros((TP, TAP_CHUNKS, 5), ga.dtype)
    b5 = _np.zeros((TP, TAP_CHUNKS, 5), be.dtype)
    for p, row in enumerate(TAPS):
        for c, tap in enumerate(row):
            if tap is not None:
                for g, (my, mx_) in enumerate(moves):
                    y, xx = tap[0] + my, tap[1] + mx_
                    if 0 <= y < PATCH and 0 <= xx < PATCH:
                        w5[p, c, g], g5[p, c, g], b5[p, c, g] = w[y, xx, g, tap[2]], ga[y, xx, g, tap[2]], be[y, xx, g, tap[2]]

    qk0 = _np.zeros((D + 1, 2, HEADS, 32), a["L0_attn_Wq"].dtype)
    for i, n in enumerate("qk"):
        qk0[:D, i, :, :HD[0]] = a[f"L0_attn_W{n}"].T.reshape(D, HEADS, HD[0])
        qk0[D, i, :, :HD[0]] = a[f"L0_attn_b{n}"].reshape(HEADS, HD[0])
    v0 = _np.concatenate([a["L0_attn_Wv"].T, a["L0_attn_bv"][None]])
    a0 = _np.concatenate([qk0.reshape(D + 1, 768), v0], 1)
    a1 = _np.concatenate([a["L1_attn_w_q"], a["L1_attn_w_k"], a["L1_attn_w_v"]], 1)
    a1 = _np.concatenate([a1, _np.zeros((1, a1.shape[1]), a1.dtype)])

    def biased(w):
        full = _np.zeros((128, 2, w.shape[1]), w.dtype)
        full[:KD, 0], full[:KD + 1, 1] = w[:KD], w[KD:]
        return full

    def experts_in(g, u, d):
        e = g.shape[0]
        wa = _np.stack([g.reshape(e, 2, KD, HIDDEN), u.reshape(e, 2, KD, HIDDEN)], 3)
        return (wa.transpose(0, 2, 1, 3, 4).reshape(e * KD, 4, HIDDEN),
                d.reshape(e, HC, 128, D).transpose(0, 2, 1, 3).reshape(e * 128, HC * D))

    sh_wa, sh_wd = experts_in(a["L0_ffn_shared_wg"], a["L0_ffn_shared_wu"], a["L0_ffn_shared_wd"])
    e0_wa, e0_wd = experts_in(a["L0_ffn_wg"], a["L0_ffn_wu"], a["L0_ffn_wd"])
    e1_wa, e1_wd = experts_in(*(a[f"L1_ffn_W{n}"].transpose(0, 2, 1) for n in "gud"))
    arrays = {
        "const": shape_constants(), "xcol": xcol, "w5": w5, "gamma5": g5, "beta5": b5,
        "tok_b": a["L0_tok_b"].reshape(1, D),
        "a0_w": biased(a0), "a1_w": biased(a1), "a1_wo": a["L1_attn_w_o"].reshape(6, 128, D).transpose(1, 0, 2),
        "a1_bo": _np.broadcast_to(a["L1_attn_b_o"], (G, D)),
        "gate0": parts(a["L0_ffn_gate_w"].T), "gate1": parts(a["L1_ffn_router_w"].T),
        "sh_wa": sh_wa, "sh_wd": sh_wd,
        "e0_wa": e0_wa, "e0_wd": e0_wd, "e1_wa": e1_wa, "e1_wd": e1_wd,
    }
    arrays = {k: _np.ascontiguousarray(v) for k, v in arrays.items()}
    nc = _bacc.Bacc("TRN2", target_bir_lowering=False, num_devices=1)
    args = {k: nc.dram_tensor(k, v.shape, _mybir.dt.from_np(v.dtype), kind="ExternalInput").ap()
            for k, v in arrays.items()}
    out = nc.dram_tensor("out", (TOKENS, D), F32, kind="ExternalOutput").ap()
    slots = nc.dram_tensor("slots", (SLOTS, D), F32, kind="Internal").ap()
    program(nc, *args.values(), slots, out)
    r = _run(nc, [arrays], core_ids=[0])
    return r.results[0]["out"].reshape(BATCH, SEQ, D)
```
